# Optimizing a Trainium2 kernel written in Bass

```python
import numpy as np
import jax
import jax.numpy as jnp

def _softmax(x, axis=-1):
    return jax.nn.softmax(x, axis=axis)

def _gelu(x):
    return jax.nn.gelu(x, approximate=True)

def _silu(x):
    return jax.nn.silu(x)

def _sigmoid(x):
    return jax.nn.sigmoid(x)

def _layernorm(x, axis=-1, eps=1e-05):
    m = jnp.mean(x, axis=axis, keepdims=True)
    v = jnp.var(x, axis=axis, keepdims=True)
    return (x - m) / jnp.sqrt(v + eps)

def _scatter_add(tgt, idx, src, axis=0):
    return tgt.at[idx].add(src)

def _segment_sum(src, seg, n):
    return jax.ops.segment_sum(src, seg, n)
kernel_name = 'mk_sandwich_d2_jaxref_r8_510598'

def setup_inputs(seed: int=0):
    np.random.seed(seed)
    _w = jnp.asarray

    def _L0_attn_setup():
        import jax, jax.numpy as jnp
        import numpy as np
        LN_EPS = 1e-05

        def _layernorm(x, g, b):
            mu = jnp.mean(x, axis=-1, keepdims=True)
            var = jnp.var(x, axis=-1, keepdims=True)
            return (x - mu) * jax.lax.rsqrt(var + LN_EPS) * g + b
        key = jax.random.key(seed)
        B, S, D, H = (2, 256, 128, 16)
        dh = D // H
        r = 48
        r_out = 96
        I = 4 * D
        r_mlp = 64
        ks = jax.random.split(key, 24)
        sc = lambda *sh: 0.02
        inp = {'hidden_states': jax.random.normal(ks[0], (B, S, D), jnp.float32), 'ln1_g': jnp.ones((D,), jnp.float32), 'ln1_b': jnp.zeros((D,), jnp.float32), 'ln2_g': jnp.ones((D,), jnp.float32), 'ln2_b': jnp.zeros((D,), jnp.float32), 'q_U': jax.random.normal(ks[1], (D, H, r), jnp.float32) * 0.02, 'q_V': jax.random.normal(ks[2], (H, r, dh), jnp.float32) * 0.02, 'q_b': jax.random.normal(ks[3], (H, dh), jnp.float32) * 0.02, 'k_U': jax.random.normal(ks[4], (D, H, r), jnp.float32) * 0.02, 'k_V': jax.random.normal(ks[5], (H, r, dh), jnp.float32) * 0.02, 'k_b': jax.random.normal(ks[6], (H, dh), jnp.float32) * 0.02, 'v_U': jax.random.normal(ks[7], (D, H, r), jnp.float32) * 0.02, 'v_V': jax.random.normal(ks[8], (H, r, dh), jnp.float32) * 0.02, 'v_b': jax.random.normal(ks[9], (H, dh), jnp.float32) * 0.02, 'out_U': jax.random.normal(ks[10], (D, r_out), jnp.float32) * 0.02, 'out_V': jax.random.normal(ks[11], (r_out, D), jnp.float32) * 0.02, 'out_b': jnp.zeros((D,), jnp.float32), 'fc1_U': jax.random.normal(ks[12], (D, r_mlp), jnp.float32) * 0.02, 'fc1_V': jax.random.normal(ks[13], (r_mlp, I), jnp.float32) * 0.02, 'fc1_b': jnp.zeros((I,), jnp.float32), 'fc2_U': jax.random.normal(ks[14], (I, r_mlp), jnp.float32) * 0.02, 'fc2_V': jax.random.normal(ks[15], (r_mlp, D), jnp.float32) * 0.02, 'fc2_b': jnp.zeros((D,), jnp.float32)}
        return inp
    _L0_attn_in = _L0_attn_setup()

    def _L0_ffn_setup():
        import jax, jax.numpy as jnp
        import numpy as np
        B, T, H = (2, 256, 128)
        I = 512
        HEADS = 4
        RET = 128
        NUM_EXPERTS = 512
        NUM_KEYS = 64
        K = 8
        key = jax.random.key(seed)
        ks = jax.random.split(key, 7)
        return {'hidden_states': jax.random.normal(ks[0], (B, T, H), jnp.float32), 'W_up': jax.random.normal(ks[1], (I, H), jnp.float32) * 0.02, 'W_down': jax.random.normal(ks[2], (H, I), jnp.float32) * 0.02, 'W_q': jax.random.normal(ks[3], (HEADS * RET, H), jnp.float32) * 0.02, 'keys': jax.random.normal(ks[4], (HEADS, NUM_KEYS, 2, RET // 2), jnp.float32) * 0.02, 'down_embed': jax.random.normal(ks[5], (NUM_EXPERTS, H), jnp.float32) * 0.02, 'up_embed': jax.random.normal(ks[6], (NUM_EXPERTS, H), jnp.float32) * 0.02}
    _L0_ffn_in = _L0_ffn_setup()

    def _L1_attn_setup():
        import jax, jax.numpy as jnp
        import numpy as np
        B, S, D = (4, 256, 128)
        H = 16
        HD = D // H
        key = jax.random.key(seed)
        ks = jax.random.split(key, 6)
        scale = 1.0 / np.sqrt(D)
        x = jax.random.normal(ks[0], (B, S, D), dtype=jnp.float32)
        Wq = jax.random.normal(ks[1], (D, D), dtype=jnp.float32) * scale
        Wk = jax.random.normal(ks[2], (D, D), dtype=jnp.float32) * scale
        Wv = jax.random.normal(ks[3], (D, D), dtype=jnp.float32) * scale
        Wo = jax.random.normal(ks[4], (D, D), dtype=jnp.float32) * scale
        bo = jax.random.normal(ks[5], (D,), dtype=jnp.float32) * 0.01
        return {'x': x, 'Wq': Wq, 'Wk': Wk, 'Wv': Wv, 'Wo': Wo, 'bo': bo}
    _L1_attn_in = _L1_attn_setup()

    def _L1_ffn_setup():
        import jax, jax.numpy as jnp
        import numpy as np
        DIM = 128
        DEPTH = 6
        HEADS = 16
        DIM_HEAD = 64
        WINDOW = 32
        INNER = HEADS * DIM_HEAD
        DIM_INNER = int(DIM * 4 * 2 / 3)
        QK_SCALE = 8.0

        def shift_tokens(t):
            a, s = jnp.split(t, 2, -1)
            s = jnp.pad(s, ((0, 0), (1, 0), (0, 0)))[:, :-1]
            return jnp.concatenate([a, s], -1)

        def l2norm(t):
            return t / jnp.maximum(jnp.linalg.norm(t, axis=-1, keepdims=True), 1e-12)

        def rotate_half(x):
            x1, x2 = jnp.split(x, 2, -1)
            return jnp.concatenate([-x2, x1], -1)

        def rotary_tables(n):
            half = jnp.arange(0, DIM_HEAD, 2, dtype=jnp.float32)
            inv_freq = 1.0 / 10000.0 ** (half / DIM_HEAD)
            t = jnp.arange(n, dtype=jnp.float32)
            freqs = t[:, None] * inv_freq[None, :]
            freqs = jnp.concatenate([freqs, freqs], -1)
            base_scale = (half + 0.4 * DIM_HEAD) / (1.4 * DIM_HEAD)
            power = (t - n // 2) / (WINDOW // 2)
            scale = base_scale[None, :] ** power[:, None]
            scale = jnp.concatenate([scale, scale], -1)
            return (freqs, scale)

        def local_attention(q, k, v):
            b, h, n, d = q.shape
            w = WINDOW
            nw = n // w
            bq = q.reshape(b, h, nw, w, d)
            bk = k.reshape(b, h, nw, w, d)
            bv = v.reshape(b, h, nw, w, d)

            def look(t):
                p = jnp.pad(t, ((0, 0), (0, 0), (1, 0), (0, 0), (0, 0)))
                return jnp.concatenate([p[:, :, :nw], p[:, :, 1:]], axis=3)
            bk2, bv2 = (look(bk), look(bv))
            seq = jnp.arange(n).reshape(nw, w)
            seq_p = jnp.pad(seq, ((1, 0), (0, 0)), constant_values=-1)
            jt = jnp.concatenate([seq_p[:nw], seq_p[1:]], axis=1)
            it = seq[:, :, None]
            jb = jt[:, None, :]
            mask = (it < jb) | (it > jb + w) | (jb == -1)
            sim = jnp.einsum('bhwie,bhwje->bhwij', bq, bk2) * QK_SCALE
            sim = jnp.where(mask, -jnp.finfo(sim.dtype).max, sim)
            attn = jax.nn.softmax(sim, -1)
            out = jnp.einsum('bhwij,bhwje->bhwie', attn, bv2)
            return out.reshape(b, h, n, d)

        def attn_layer(x, Wqkv, qs, ksc, Wo):
            b, n, _ = x.shape
            qkv = x @ Wqkv
            q, k, v = jnp.split(qkv, 3, -1)
            sh = lambda t: t.reshape(b, n, HEADS, DIM_HEAD).transpose(0, 2, 1, 3)
            q, k, v = (sh(q), sh(k), sh(v))
            q = l2norm(q) * qs
            k = l2norm(k) * ksc
            freqs, scale = rotary_tables(n)
            cos, sin = (jnp.cos(freqs), jnp.sin(freqs))
            q = q * cos * scale + rotate_half(q) * sin * scale
            inv = 1.0 / scale
            k = k * cos * inv + rotate_half(k) * sin * inv
            out = local_attention(q, k, v)
            out = out.transpose(0, 2, 1, 3).reshape(b, n, INNER)
            return out @ Wo

        def ffn_layer(x, g, bln, W1, b1, W2, b2):
            mu = x.mean(-1, keepdims=True)
            var = ((x - mu) ** 2).mean(-1, keepdims=True)
            xn = (x - mu) / jnp.sqrt(var + 1e-05) * g + bln
            hg = xn @ W1 + b1
            a, gate = jnp.split(hg, 2, -1)
            return a * jax.nn.gelu(gate, approximate=False) @ W2 + b2
        key = jax.random.key(seed)
        ks = jax.random.split(key, 8)
        B, N = (2, 256)
        init = lambda k, shape: jax.random.normal(k, shape, jnp.float32) * 0.02
        return {'x': jax.random.normal(ks[0], (B, N, DIM), jnp.float32), 'Wqkv': init(ks[1], (DEPTH, DIM, 3 * INNER)), 'q_scale': jnp.ones((DEPTH, DIM_HEAD), jnp.float32), 'k_scale': jnp.ones((DEPTH, DIM_HEAD), jnp.float32), 'Wo': init(ks[2], (DEPTH, INNER, DIM)), 'ln_g': jnp.ones((DEPTH, DIM), jnp.float32), 'ln_b': jnp.zeros((DEPTH, DIM), jnp.float32), 'W1': init(ks[3], (DEPTH, DIM, 2 * DIM_INNER)), 'b1': jnp.zeros((DEPTH, 2 * DIM_INNER), jnp.float32), 'W2': init(ks[4], (DEPTH, DIM_INNER, DIM)), 'b2': jnp.zeros((DEPTH, DIM), jnp.float32)}
    _L1_ffn_in = _L1_ffn_setup()
    _d = {'L0_attn_hidden_states': _L0_attn_in['hidden_states'], 'L0_attn_ln1_g': _L0_attn_in['ln1_g'], 'L0_attn_ln1_b': _L0_attn_in['ln1_b'], 'L0_attn_ln2_g': _L0_attn_in['ln2_g'], 'L0_attn_ln2_b': _L0_attn_in['ln2_b'], 'L0_attn_q_U': _L0_attn_in['q_U'], 'L0_attn_q_V': _L0_attn_in['q_V'], 'L0_attn_q_b': _L0_attn_in['q_b'], 'L0_attn_k_U': _L0_attn_in['k_U'], 'L0_attn_k_V': _L0_attn_in['k_V'], 'L0_attn_k_b': _L0_attn_in['k_b'], 'L0_attn_v_U': _L0_attn_in['v_U'], 'L0_attn_v_V': _L0_attn_in['v_V'], 'L0_attn_v_b': _L0_attn_in['v_b'], 'L0_attn_out_U': _L0_attn_in['out_U'], 'L0_attn_out_V': _L0_attn_in['out_V'], 'L0_attn_out_b': _L0_attn_in['out_b'], 'L0_attn_fc1_U': _L0_attn_in['fc1_U'], 'L0_attn_fc1_V': _L0_attn_in['fc1_V'], 'L0_attn_fc1_b': _L0_attn_in['fc1_b'], 'L0_attn_fc2_U': _L0_attn_in['fc2_U'], 'L0_attn_fc2_V': _L0_attn_in['fc2_V'], 'L0_attn_fc2_b': _L0_attn_in['fc2_b'], 'L0_ffn_W_up': _L0_ffn_in['W_up'], 'L0_ffn_W_down': _L0_ffn_in['W_down'], 'L0_ffn_W_q': _L0_ffn_in['W_q'], 'L0_ffn_keys': _L0_ffn_in['keys'], 'L0_ffn_down_embed': _L0_ffn_in['down_embed'], 'L0_ffn_up_embed': _L0_ffn_in['up_embed'], 'L1_attn_Wq': _L1_attn_in['Wq'], 'L1_attn_Wk': _L1_attn_in['Wk'], 'L1_attn_Wv': _L1_attn_in['Wv'], 'L1_attn_Wo': _L1_attn_in['Wo'], 'L1_attn_bo': _L1_attn_in['bo'], 'L1_ffn_Wqkv': _L1_ffn_in['Wqkv'], 'L1_ffn_q_scale': _L1_ffn_in['q_scale'], 'L1_ffn_k_scale': _L1_ffn_in['k_scale'], 'L1_ffn_Wo': _L1_ffn_in['Wo'], 'L1_ffn_ln_g': _L1_ffn_in['ln_g'], 'L1_ffn_ln_b': _L1_ffn_in['ln_b'], 'L1_ffn_W1': _L1_ffn_in['W1'], 'L1_ffn_b1': _L1_ffn_in['b1'], 'L1_ffn_W2': _L1_ffn_in['W2'], 'L1_ffn_b2': _L1_ffn_in['b2']}
    _x0 = _d['L0_attn_hidden_states']
    _d['L0_attn_hidden_states'] = jax.random.normal(jax.random.fold_in(jax.random.key(seed), 1), (16, 256, 128), dtype=_x0.dtype)
    del _x0
    return _d

def reference(L0_attn_hidden_states, L0_attn_ln1_g, L0_attn_ln1_b, L0_attn_ln2_g, L0_attn_ln2_b, L0_attn_q_U, L0_attn_q_V, L0_attn_q_b, L0_attn_k_U, L0_attn_k_V, L0_attn_k_b, L0_attn_v_U, L0_attn_v_V, L0_attn_v_b, L0_attn_out_U, L0_attn_out_V, L0_attn_out_b, L0_attn_fc1_U, L0_attn_fc1_V, L0_attn_fc1_b, L0_attn_fc2_U, L0_attn_fc2_V, L0_attn_fc2_b, L0_ffn_W_up, L0_ffn_W_down, L0_ffn_W_q, L0_ffn_keys, L0_ffn_down_embed, L0_ffn_up_embed, L1_attn_Wq, L1_attn_Wk, L1_attn_Wv, L1_attn_Wo, L1_attn_bo, L1_ffn_Wqkv, L1_ffn_q_scale, L1_ffn_k_scale, L1_ffn_Wo, L1_ffn_ln_g, L1_ffn_ln_b, L1_ffn_W1, L1_ffn_b1, L1_ffn_W2, L1_ffn_b2):

    def _L0_attn_ref(hidden_states, ln1_g, ln1_b, ln2_g, ln2_b, q_U, q_V, q_b, k_U, k_V, k_b, v_U, v_V, v_b, out_U, out_V, out_b, fc1_U, fc1_V, fc1_b, fc2_U, fc2_V, fc2_b):
        import jax, jax.numpy as jnp
        import numpy as np
        LN_EPS = 1e-05

        def _layernorm(x, g, b):
            mu = jnp.mean(x, axis=-1, keepdims=True)
            var = jnp.var(x, axis=-1, keepdims=True)
            return (x - mu) * jax.lax.rsqrt(var + LN_EPS) * g + b
        B, S, D = hidden_states.shape
        H, dh = (q_V.shape[0], q_V.shape[2])
        x = _layernorm(hidden_states, ln1_g, ln1_b)
        Q = jnp.einsum('bsd,dhr,hre->bhse', x, q_U, q_V) + q_b[None, :, None, :]
        Pk = jnp.einsum('bsd,dhr->bhsr', x, k_U)
        Pv = jnp.einsum('bsd,dhr->bhsr', x, v_U)
        K = jnp.einsum('bhsr,hrd->bhsd', Pk, k_V) + k_b[None, :, None, :]
        V = jnp.einsum('bhsr,hrd->bhsd', Pv, v_V) + v_b[None, :, None, :]
        scale = 1.0 / jnp.sqrt(jnp.asarray(dh, x.dtype))
        scores = jnp.einsum('bhse,bhte->bhst', Q, K) * scale
        causal = jnp.tril(jnp.ones((S, S), bool))
        scores = jnp.where(causal[None, None], scores, jnp.asarray(-1000000000.0, scores.dtype))
        attn = jax.nn.softmax(scores, axis=-1)
        ctx = jnp.einsum('bhst,bhtd->bhsd', attn, V)
        ctx = ctx.transpose(0, 2, 1, 3).reshape(B, S, D)
        attn_out = ctx @ out_U @ out_V + out_b
        h = hidden_states + attn_out
        x2 = _layernorm(h, ln2_g, ln2_b)
        hmid = jax.nn.gelu(x2 @ fc1_U @ fc1_V + fc1_b, approximate=True)
        mlp_out = hmid @ fc2_U @ fc2_V + fc2_b
        return h + mlp_out

    def _L0_ffn_ref(hidden_states, W_up, W_down, W_q, keys, down_embed, up_embed):
        import jax, jax.numpy as jnp
        import numpy as np
        B, T, H = (2, 256, 128)
        I = 512
        HEADS = 4
        RET = 128
        NUM_EXPERTS = 512
        NUM_KEYS = 64
        K = 8
        b, t, hd = hidden_states.shape
        h, nk, _, n = keys.shape
        q = jnp.einsum('btd,ed->bte', hidden_states, W_q)
        q = q.reshape(b, t, 2, h, n).transpose(2, 0, 1, 3, 4)
        sim = jnp.einsum('pbthn,hkpn->pbthk', q, keys)
        scores_xy, idx_xy = jax.lax.top_k(sim, K)
        sx, sy = (scores_xy[0], scores_xy[1])
        ix, iy = (idx_xy[0], idx_xy[1])
        all_scores = (sx[..., :, None] + sy[..., None, :]).reshape(b, t, h, K * K)
        all_idx = (ix[..., :, None] * nk + iy[..., None, :]).reshape(b, t, h, K * K)
        scores, pk = jax.lax.top_k(all_scores, K)
        indices = jnp.take_along_axis(all_idx, pk, axis=-1)
        de = down_embed[indices]
        ue = up_embed[indices]
        w = jax.nn.silu(jnp.einsum('btd,bthkd->bthk', hidden_states, de) * jax.nn.softmax(scores, axis=-1))
        experts_states = jnp.einsum('bthk,bthkd->btd', w, ue)
        dense = jnp.einsum('bti,di->btd', jax.nn.silu(jnp.einsum('btd,id->bti', hidden_states, W_up)), W_down)
        return dense + experts_states

    def _L1_attn_ref(x, Wq, Wk, Wv, Wo, bo):
        import jax, jax.numpy as jnp
        import numpy as np
        B, S, D = (4, 256, 128)
        H = 16
        HD = D // H
        b, n, _ = x.shape
        q = (x @ Wq).reshape(b, n, H, HD).transpose(0, 2, 1, 3)
        k = (x @ Wk).reshape(b, n, H, HD).transpose(0, 2, 1, 3)
        v = (x @ Wv).reshape(b, n, H, HD).transpose(0, 2, 1, 3)
        scores = jnp.einsum('bhqd,bhkd->bhqk', q, k) / jnp.sqrt(jnp.float32(HD))
        causal = jnp.tril(jnp.ones((n, n), dtype=bool))
        scores = jnp.where(causal, scores, -jnp.inf)
        attn = jax.nn.softmax(scores, axis=-1)
        ctx = jnp.einsum('bhqk,bhkd->bhqd', attn, v)
        ctx = ctx.transpose(0, 2, 1, 3).reshape(b, n, D)
        return ctx @ Wo + bo

    def _L1_ffn_ref(x, Wqkv, q_scale, k_scale, Wo, ln_g, ln_b, W1, b1, W2, b2):
        import jax, jax.numpy as jnp
        import numpy as np
        DIM = 128
        DEPTH = 6
        HEADS = 16
        DIM_HEAD = 64
        WINDOW = 32
        INNER = HEADS * DIM_HEAD
        DIM_INNER = int(DIM * 4 * 2 / 3)
        QK_SCALE = 8.0

        def shift_tokens(t):
            a, s = jnp.split(t, 2, -1)
            s = jnp.pad(s, ((0, 0), (1, 0), (0, 0)))[:, :-1]
            return jnp.concatenate([a, s], -1)

        def l2norm(t):
            return t / jnp.maximum(jnp.linalg.norm(t, axis=-1, keepdims=True), 1e-12)

        def rotate_half(x):
            x1, x2 = jnp.split(x, 2, -1)
            return jnp.concatenate([-x2, x1], -1)

        def rotary_tables(n):
            half = jnp.arange(0, DIM_HEAD, 2, dtype=jnp.float32)
            inv_freq = 1.0 / 10000.0 ** (half / DIM_HEAD)
            t = jnp.arange(n, dtype=jnp.float32)
            freqs = t[:, None] * inv_freq[None, :]
            freqs = jnp.concatenate([freqs, freqs], -1)
            base_scale = (half + 0.4 * DIM_HEAD) / (1.4 * DIM_HEAD)
            power = (t - n // 2) / (WINDOW // 2)
            scale = base_scale[None, :] ** power[:, None]
            scale = jnp.concatenate([scale, scale], -1)
            return (freqs, scale)

        def local_attention(q, k, v):
            b, h, n, d = q.shape
            w = WINDOW
            nw = n // w
            bq = q.reshape(b, h, nw, w, d)
            bk = k.reshape(b, h, nw, w, d)
            bv = v.reshape(b, h, nw, w, d)

            def look(t):
                p = jnp.pad(t, ((0, 0), (0, 0), (1, 0), (0, 0), (0, 0)))
                return jnp.concatenate([p[:, :, :nw], p[:, :, 1:]], axis=3)
            bk2, bv2 = (look(bk), look(bv))
            seq = jnp.arange(n).reshape(nw, w)
            seq_p = jnp.pad(seq, ((1, 0), (0, 0)), constant_values=-1)
            jt = jnp.concatenate([seq_p[:nw], seq_p[1:]], axis=1)
            it = seq[:, :, None]
            jb = jt[:, None, :]
            mask = (it < jb) | (it > jb + w) | (jb == -1)
            sim = jnp.einsum('bhwie,bhwje->bhwij', bq, bk2) * QK_SCALE
            sim = jnp.where(mask, -jnp.finfo(sim.dtype).max, sim)
            attn = jax.nn.softmax(sim, -1)
            out = jnp.einsum('bhwij,bhwje->bhwie', attn, bv2)
            return out.reshape(b, h, n, d)

        def attn_layer(x, Wqkv, qs, ksc, Wo):
            b, n, _ = x.shape
            qkv = x @ Wqkv
            q, k, v = jnp.split(qkv, 3, -1)
            sh = lambda t: t.reshape(b, n, HEADS, DIM_HEAD).transpose(0, 2, 1, 3)
            q, k, v = (sh(q), sh(k), sh(v))
            q = l2norm(q) * qs
            k = l2norm(k) * ksc
            freqs, scale = rotary_tables(n)
            cos, sin = (jnp.cos(freqs), jnp.sin(freqs))
            q = q * cos * scale + rotate_half(q) * sin * scale
            inv = 1.0 / scale
            k = k * cos * inv + rotate_half(k) * sin * inv
            out = local_attention(q, k, v)
            out = out.transpose(0, 2, 1, 3).reshape(b, n, INNER)
            return out @ Wo

        def ffn_layer(x, g, bln, W1, b1, W2, b2):
            mu = x.mean(-1, keepdims=True)
            var = ((x - mu) ** 2).mean(-1, keepdims=True)
            xn = (x - mu) / jnp.sqrt(var + 1e-05) * g + bln
            hg = xn @ W1 + b1
            a, gate = jnp.split(hg, 2, -1)
            return a * jax.nn.gelu(gate, approximate=False) @ W2 + b2
        for i in range(DEPTH):
            x = attn_layer(shift_tokens(x), Wqkv[i], q_scale[i], k_scale[i], Wo[i]) + x
            x = ffn_layer(shift_tokens(x), ln_g[i], ln_b[i], W1[i], b1[i], W2[i], b2[i]) + x
        return x
    x = L0_attn_hidden_states
    x = x + _layernorm(_L0_attn_ref(_layernorm(x, axis=-1), L0_attn_ln1_g, L0_attn_ln1_b, L0_attn_ln2_g, L0_attn_ln2_b, L0_attn_q_U, L0_attn_q_V, L0_attn_q_b, L0_attn_k_U, L0_attn_k_V, L0_attn_k_b, L0_attn_v_U, L0_attn_v_V, L0_attn_v_b, L0_attn_out_U, L0_attn_out_V, L0_attn_out_b, L0_attn_fc1_U, L0_attn_fc1_V, L0_attn_fc1_b, L0_attn_fc2_U, L0_attn_fc2_V, L0_attn_fc2_b), axis=-1)
    x = x + _layernorm(_L0_ffn_ref(_layernorm(x, axis=-1), L0_ffn_W_up, L0_ffn_W_down, L0_ffn_W_q, L0_ffn_keys, L0_ffn_down_embed, L0_ffn_up_embed), axis=-1)
    x = x + _layernorm(_L1_attn_ref(_layernorm(x, axis=-1), L1_attn_Wq, L1_attn_Wk, L1_attn_Wv, L1_attn_Wo, L1_attn_bo), axis=-1)
    x = x + _layernorm(_L1_ffn_ref(_layernorm(x, axis=-1), L1_ffn_Wqkv, L1_ffn_q_scale, L1_ffn_k_scale, L1_ffn_Wo, L1_ffn_ln_g, L1_ffn_ln_b, L1_ffn_W1, L1_ffn_b1, L1_ffn_W2, L1_ffn_b2), axis=-1)
    return x

_drawn_inputs = setup_inputs


def setup_inputs(seed=0):
    import zlib

    import numpy as np

    out = dict(_drawn_inputs(seed))
    spreads = {'L0_attn_ln1_g': (1.0, 0.6),
     'L0_attn_ln1_b': (0.0, 0.8),
     'L0_attn_ln2_g': (1.0, 0.6),
     'L0_attn_ln2_b': (0.0, 0.8),
     'L0_attn_out_b': (0.0, 0.8),
     'L0_attn_fc1_b': (0.0, 0.8),
     'L0_attn_fc2_b': (0.0, 0.8),
     'L1_ffn_q_scale': (1.0, 0.6),
     'L1_ffn_k_scale': (1.0, 0.6),
     'L1_ffn_ln_g': (1.0, 0.6),
     'L1_ffn_ln_b': (0.0, 0.8),
     'L1_ffn_b1': (0.0, 0.8),
     'L1_ffn_b2': (0.0, 0.8)}
    factors = {'L0_attn_q_U': 8.0,
     'L0_attn_q_V': 8.0,
     'L0_attn_q_b': 8.0,
     'L0_attn_k_U': 8.0,
     'L0_attn_k_V': 8.0,
     'L0_attn_k_b': 200.0,
     'L0_attn_v_U': 8.0,
     'L0_attn_v_V': 8.0,
     'L0_attn_v_b': 8.0,
     'L0_attn_out_U': 8.0,
     'L0_attn_out_V': 8.0,
     'L0_attn_fc1_U': 8.0,
     'L0_attn_fc1_V': 8.0,
     'L0_attn_fc2_U': 8.0,
     'L0_attn_fc2_V': 8.0,
     'L0_ffn_W_q': 85.758,
     'L0_ffn_keys': 29.831,
     'L1_ffn_W1': 6.382,
     'L1_ffn_W2': 6.275,
     'L1_attn_bo': 4.834}
    for name, (base, spread) in spreads.items():
        noise = np.random.default_rng([zlib.crc32(name.encode()), seed]).standard_normal(out[name].shape)
        drawn = base * np.exp(spread * noise) if base else spread * noise
        out[name] = jnp.asarray(drawn.astype(out[name].dtype))
    for name, factor in factors.items():
        out[name] = (out[name] * factor).astype(out[name].dtype)
    return out
```

```python
from contextlib import ExitStack

import numpy as np

import concourse.bass as bass
from concourse import mybir

F32 = mybir.dt.float32
BF16 = mybir.dt.bfloat16
U32 = mybir.dt.uint32
ACT = mybir.ActivationFunctionType
ALU = mybir.AluOpType
AX = mybir.AxisListType

NB = 16
DEPTH = 6
EPS = 1e-5
DI = 341
CH = [(0, 128), (128, 128), (256, 85)]

SPEC = {
    "x": ((NB, 256, 128), F32),
    "aUT": ((48, 48, 128), F32),
    "aV": ((48, 48, 8), F32),
    "ab": ((1, 384), F32),
    "aoUT": ((96, 128), F32),
    "aoV": ((96, 128), F32),
    "aob": ((1, 128), F32),
    "af1UT": ((64, 128), F32),
    "af1V": ((64, 512), F32),
    "af1b": ((128, 4), F32),
    "af2UT": ((64, 512), F32),
    "af2V": ((64, 128), F32),
    "af2b": ((1, 128), F32),
    "aln": ((128, 4), F32),
    "bWq": ((64, 8, 128), F32),
    "bkT": ((64, 8, 64), F32),
    "bdT": ((128, 512), F32),
    "bue": ((128, 4, 128), F32),
    "bup": ((128, 512), F32),
    "bdn": ((128, 4, 128), F32),
    "cW": ((128, 384), F32),
    "cWo": ((128, 128), F32),
    "cbo": ((1, 128), F32),
    "dWqkv": ((DEPTH, 128, 3072), F32),
    "dsc": ((DEPTH, 4, 64), F32),
    "dWo": ((DEPTH, 128, 8, 128), F32),
    "dln": ((DEPTH, 128, 2), F32),
    "dW1": ((DEPTH, 128, 682), F32),
    "db1": ((DEPTH, 128, 6), F32),
    "dW2": ((DEPTH, 128, 3, 128), F32),
    "kident": ((128, 128), F32),
    "kmask": ((128, 2, 128), F32),
    "kmaskd": ((128, 2, 384), F32),
    "ksel": ((128, 16, 128), F32),
    "krope": ((128, 2, 4, 64), F32),
    "kiota": ((128, 64, 8), F32),
    "kx8": ((128, 8, 8), F32),
    "kw8": ((128, 8), F32),
}


class Queue:

    def __init__(self, name, engine):
        self.name, self.e, self.sem, self.n = name, engine, None, 0

    def wait(self, *tokens):
        for t in tokens:
            if t is not None:
                self.e.wait_ge(t[0], t[1])

    def op(self, f, *tokens):
        self.wait(*tokens)
        self.n += 1
        f(self.e).then_inc(self.sem, 1)
        return (self.sem, self.n)

    def quiet(self, f, *tokens):
        self.wait(*tokens)
        f(self.e)

    def last(self):
        return (self.sem, self.n) if self.n else None


class Ring:

    def __init__(self, bufs):
        self.bufs, self.k, self.freed = bufs, 0, [()] * len(bufs)

    def take(self):
        i = self.k % len(self.bufs)
        self.k += 1
        freed = self.freed[i]
        assert freed is not None, "a buffer is taken before its last reader is known"
        self.freed[i] = None
        return i, self.bufs[i], freed

    def free(self, i, *tokens):
        self.freed[i] = tokens


def network(nc, d, out, run):
    ctx = ExitStack()
    with ctx:
        pe, act, dve, pool, sp = [Queue(n, e) for n, e in (
            ("pe", nc.tensor), ("act", nc.scalar), ("dve", nc.vector), ("pool", nc.gpsimd), ("sp", nc.sync))]
        queues = (pe, act, dve, pool)
        phases = [0]
        held = []

        def new_phase():
            for q in queues:
                if q.n or q.sem is None:
                    q.sem = ctx.enter_context(nc.semaphore(f"s_{q.name}{phases[0]}"))
                    q.n = 0
            phases[0] += 1

        def fence():
            ends = [q.last() for q in queues]
            for q in (*queues, sp):
                q.wait(*ends)

        nsem = [0]

        def dma(dst, src, *tokens, q=None):
            s = ctx.enter_context(nc.semaphore(f"s_d{nsem[0]}"))
            nsem[0] += 1
            q = q or sp
            q.wait(*tokens)
            q.e.dma_start(dst, src).then_inc(s, 16)
            return (s, 16)

        TOTAL = 50700
        arena = ctx.enter_context(nc.sbuf_tensor("arena", [128, TOTAL], F32))
        top = [0]

        def sb(shape, dt=F32):
            n = 1
            for s in shape[1:]:
                n *= s
            words = n if dt in (F32, U32) else (n + 1) // 2
            a = arena[0:shape[0], top[0]:top[0] + words]
            top[0] += words + (-words) % 8
            assert top[0] <= TOTAL, top[0]
            if dt != F32:
                a = a.bitcast(dt)
            if len(shape) == 3:
                a = a.rearrange("p (a b) -> p a b", a=shape[1])
            if len(shape) == 4:
                a = a.rearrange("p (a b c) -> p a b c", a=shape[1], b=shape[2])
            return a

        def bc(a, dim, n):
            v = a.unsqueeze(dim)
            sh = list(v.shape)
            sh[dim] = n
            return v.broadcast_to(sh)

        slots = [ctx.enter_context(nc.psum_tensor(f"ps{i}", [128, 1024], F32))[:, :] for i in range(4)]
        PS = Ring(slots)
        PO = Ring([slots[3][:, 0:512], slots[3][:, 512:1024]])

        def split_psum(n):
            PS.bufs, PS.k, PS.freed = slots[:n], 0, [()] * n
            PO.k, PO.freed = 0, [()] * 2

        new_phase()

        XR = sb([128, 2 * NB, 128])
        XX = sb([128, 2 * NB, 128])
        ident = sb([128, 128])
        identb = sb([128, 128], BF16)
        mask = sb([128, 2, 128], BF16)
        maskd = sb([128, 2, 384], BF16)
        mhalf = sb([128, 2])
        mhalf32 = sb([128, 32])
        ones1 = sb([1, 128])
        t_mh = pool.op(lambda e: e.memset(mhalf, -0.5))
        t_mh = pool.op(lambda e: e.memset(mhalf32, -0.5))
        base = top[0]

        t_x = []
        for b0 in range(0, NB, 4):
            t_x.append(dma(XR[:, 2 * b0:2 * b0 + 8, :],
                           d["x"][b0:b0 + 4].rearrange("b (t p) f -> p (b t) f", p=128)))
        t_id = dma(ident, d["kident"])
        stage_m = sb([128, 2, 128])
        stage_d = sb([128, 2, 384])
        t1 = dma(stage_m, d["kmask"])
        t2 = dma(stage_d, d["kmaskd"])
        t_idb = pool.op(lambda e: e.tensor_copy(identb, ident), t_id)
        t_mask = pool.op(lambda e: e.tensor_copy(mask, stage_m), t1)
        t_mask = pool.op(lambda e: e.tensor_copy(maskd, stage_d), t2)

        def layer_norm(src, dst, st, *tokens, dst_free=()):
            n = len(src)
            for t in range(n):
                tk = dve.op(lambda e, t=t: e.bn_stats(st["bn"][:, t, :], src[t]), *(tokens if t == 0 else ()))
            for t in range(n):
                tk = dve.op(lambda e, t=t: e.bn_aggr(st["mv"][:, t, :], st["bn"][:, t, :]), *((tk,) if t == 0 else ()))
            tk = pool.op(lambda e: e.tensor_scalar(st["rs"][:, 0:n], st["mv"][:, 0:n, 1], EPS, None, ALU.add), tk)
            tk = pool.op(lambda e: e.tensor_tensor(st["rs"][:, 0:n], st["rs"][:, 0:n], mhalf[:, 0:n], ALU.pow), tk, t_mh)
            for t in range(n):
                w = (tk, *dst_free) if t == 0 else ()
                last = dve.op(lambda e, t=t: e.tensor_scalar(dst[t], src[t], st["mv"][:, t, 0:1], st["rs"][:, t:t + 1],
                                                             ALU.subtract, ALU.mult), *w)
            return last

        def stats():
            return {"bn": sb([128, 2, 6]), "mv": sb([128, 2, 2]), "rs": sb([128, 2])}

        def turn(src, *tokens):
            i, p, freed = PS.take()
            for t, s in enumerate(src):
                f = lambda e, t=t, s=s: e.transpose(p[:, 128 * t:128 * t + 128], s, ident)
                w = (*tokens, *freed, t_id) if t == 0 else ()
                if t == len(src) - 1:
                    tk = pe.op(f, *w)
                else:
                    pe.quiet(f, *w)
            return i, p, tk

        def drive(units, width):
            live, todo = [], list(units)
            while live or todo:
                if len(live) < width and todo:
                    live.append(todo.pop(0))
                for g in list(live):
                    try:
                        next(g)
                    except StopIteration:
                        live.remove(g)

        def add_ln_residual(y, b, st, free, *tokens):
            tk = layer_norm([y[:, 0, :], y[:, 1, :]], [y[:, 0, :], y[:, 1, :]], st, *tokens)
            tk = dve.op(lambda e: e.tensor_tensor(XR[:, 2 * b:2 * b + 2, :], XR[:, 2 * b:2 * b + 2, :], y, ALU.add), tk)
            return tk

        def attention_buffers():
            bufs = []
            for _ in range(2):
                B = {"st": stats(), "h": sb([128, 2, 128]), "hT": sb([128, 256]), "qkv": sb([128, 2, 256]),
                     "va": sb([128, 2, 16, 9]), "r": sb([128, 2, 256]),
                     "b1": sb([128, 2, 256], BF16), "b2": sb([128, 2, 256], BF16),
                     "QS": sb([128, 2, 1024], BF16), "KS": sb([128, 2, 1024], BF16),
                     "QT": sb([128, 8, 256], BF16), "KT": sb([128, 8, 256], BF16),
                     "m": sb([128, 2, 16]), "mr": sb([128, 2, 16]), "ms": sb([128, 2, 128], BF16),
                     "mT": sb([128, 256], BF16), "PT": Ring([sb([128, 2, 384]) for _ in range(2)]), "rc": sb([128, 2, 16]), "ctx": sb([128, 2, 128]),
                     "cT": sb([128, 256]), "y": sb([128, 2, 128])}
                bufs.append(B)
            return bufs

        def prepare_attention(bufs):
            for B in bufs:
                pool.op(lambda e, B=B: e.memset(B["va"][:, :, :, 8:9], 1.0))
                pool.op(lambda e, B=B: e.memset(B["QS"], 0.0))
                pool.op(lambda e, B=B: e.memset(B["ms"], 0.0))
                B["ready"] = pool.op(lambda e, B=B: e.memset(B["KS"], 0.0))

        def attention(B, W, bias, sel, t_w, *t_h):
            PT = B["PT"]
            """B["hT"] -> B["ctx"] (token-major, normalised), stage by stage; yields between stages."""
            for t in range(2):
                i, p, freed = PS.take()
                tq = pe.op(lambda e, t=t: e.matmul(p[:, 0:384], B["hT"][:, 128 * t:128 * t + 128], W, start=True, stop=True),
                           *freed, *(t_h if t == 0 else ()), *t_w)
                if bias is not None:
                    tv = dve.op(lambda e, t=t: e.tensor_tensor(B["qkv"][:, t, :], p[:, 0:256], bias[:, 0:256], ALU.add), tq)
                    tv2 = dve.op(lambda e, t=t: e.tensor_tensor(B["va"][:, t, :, 0:8], p[:, 256:384].rearrange("p (h d) -> p h d", d=8),
                                                               bias[:, 256:384].rearrange("p (h d) -> p h d", d=8), ALU.add))
                else:
                    tv = dve.op(lambda e, t=t: e.tensor_copy(B["qkv"][:, t, :], p[:, 0:256]), tq)
                    tv2 = dve.op(lambda e, t=t: e.tensor_copy(B["va"][:, t, :, 0:8],
                                                              p[:, 256:384].rearrange("p (h d) -> p h d", d=8)))
                PS.free(i, tv2)
            t = act.op(lambda e: e.activation(B["b1"], B["qkv"], ACT.Copy), tv)
            t = dve.op(lambda e: e.tensor_tensor(B["r"], B["qkv"], B["b1"], ALU.subtract), t)
            t = act.op(lambda e: e.activation(B["b2"], B["r"], ACT.Copy), t)
            t = dve.op(lambda e: e.tensor_tensor(B["r"], B["r"], B["b2"], ALU.subtract), t)
            yield
            q = [B[n][:, :, 0:128].rearrange("p t (h e) -> p t h e", e=8) for n in ("b1", "b2", "r")]
            k = [B[n][:, :, 128:256].rearrange("p t (h e) -> p t h e", e=8) for n in ("b1", "b2", "r")]
            tb = []
            for S, parts, order in (("QS", q, (0, 0, 1, 1, 0, 2)), ("KS", k, (0, 1, 0, 1, 2, 0))):
                for tile in range(2):
                    s = B[S][:, tile, :].rearrange("p (h g e) -> p h g e", h=16, g=8)
                    for g, o in enumerate(order):
                        eng = pool if g % 2 else dve
                        tb.append(eng.op(lambda e, s=s, g=g, o=o, parts=parts, tile=tile:
                                         e.tensor_copy(s[:, :, g, :], parts[o][:, tile, :, :]), t, B["ready"]))
            tb = [dve.last(), pool.last()]
            yield
            for S, T in (("QS", "QT"), ("KS", "KT")):
                for tile in range(2):
                    i, p, freed = PS.take()
                    pb = p.bitcast(BF16)
                    for c in range(8):
                        f = lambda e, c=c, S=S, tile=tile, pb=pb: e.transpose(
                            pb[:, 128 * c:128 * c + 128], B[S][:, tile, 128 * c:128 * c + 128], identb)
                        w = (*freed, *tb, t_idb) if c == 0 else ()
                        if c == 7:
                            tk = pe.op(f, *w)
                        else:
                            pe.quiet(f, *w)
                    g = lambda e, T=T, tile=tile, pb=pb: e.tensor_copy(
                        B[T][:, :, 128 * tile:128 * tile + 128], pb[:, 0:1024].rearrange("p (c q) -> p c q", c=8))
                    if tile == 0:
                        te = act.op(lambda e, T=T, tile=tile, pb=pb: e.activation(
                            B[T][:, :, 128 * tile:128 * tile + 128], pb[:, 0:1024].rearrange("p (c q) -> p c q", c=8),
                            ACT.Copy), tk)
                    else:
                        te = dve.op(g, tk)
                    PS.free(i, te)
            t_qk = (act.last(), dve.last())
            yield

            def row(h):
                return slice(64 * (h % 2), 64 * (h % 2) + 48)

            for tile in range(2):
                nk = 128 * (tile + 1)
                per = 1024 // nk
                for g in range(16 // per):
                    i, p, freed = PS.take()
                    for j in range(per):
                        h = g * per + (2 * j if j < per // 2 else 2 * j - per + 1)
                        o = p[:, j * nk:(j + 1) * nk]
                        w = (*freed, *t_qk, t_mask) if j == 0 else ()
                        pe.quiet(lambda e, o=o, nk=nk, h=h, tile=tile: e.matmul(
                            o, B["QT"][row(h), h // 2, 128 * tile:128 * tile + 128],
                            B["KT"][row(h), h // 2, 0:nk], start=True, stop=False, skip_group_check=True), *w)
                        tk = pe.op(lambda e, o=o, nk=nk: e.matmul(
                            o[:, nk - 128:nk], identb, mask[:, 0, :], start=False, stop=True, skip_group_check=True))
                    td = dve.op(lambda e, p=p, g=g, per=per, nk=nk, tile=tile: e.tensor_reduce(
                        B["m"][:, tile, g * per:(g + 1) * per].rearrange("p (j u) -> p u j", u=2),
                        p.rearrange("p (u j k) -> p u j k", u=2, k=nk), AX.X, ALU.max), tk)
                    PS.free(i, td)
                    if g % 2:
                        yield
            ms = [B["ms"].rearrange("p t (u r) -> p t u r", u=2)[:, :, :, 16 * j:16 * j + 16] for j in range(3)]
            t = dve.op(lambda e: e.tensor_copy(ms[0], bc(B["m"], 2, 2)), td, B["ready"])
            t = dve.op(lambda e: e.tensor_tensor(B["mr"], B["m"], ms[0][:, :, 0, :], ALU.subtract), t)
            t = dve.op(lambda e: e.tensor_copy(ms[1], bc(B["mr"], 2, 2)), t)
            t = dve.op(lambda e: e.tensor_tensor(B["mr"], B["mr"], ms[1][:, :, 0, :], ALU.subtract), t)
            t = dve.op(lambda e: e.tensor_copy(ms[2], bc(B["mr"], 2, 2)), t)
            i, p, freed = PS.take()
            pb = p.bitcast(BF16)
            pe.quiet(lambda e, pb=pb: e.transpose(pb[:, 0:128], B["ms"][:, 0, :], identb), t, *freed)
            tk = pe.op(lambda e, pb=pb: e.transpose(pb[:, 128:256], B["ms"][:, 1, :], identb))
            t_m = act.op(lambda e, pb=pb: e.activation(B["mT"], pb[:, 0:256], ACT.Copy), tk)
            PS.free(i, t_m)
            yield
            io, po, ofreed = PO.take()
            O = po[:, 0:288].rearrange("p (t h e) -> p t h e", t=2, h=16)
            for g in range(8):
                i, p, freed = PS.take()
                for j in range(2):
                    h = 2 * g + j
                    a = p[:, 512 * j:512 * j + 256]
                    c = p[:, 512 * j + 256:512 * j + 384]
                    w = (*freed, t_m) if j == 0 else ()
                    pe.quiet(lambda e, a=a, h=h: e.matmul(a, B["KT"][row(h), h // 2, 0:128], B["QT"][row(h), h // 2, :],
                                                          start=True, stop=False, skip_group_check=True), *w)
                    pe.quiet(lambda e, a=a, h=h: e.matmul(a, sel[row(h), h, :], B["mT"][row(h), :], start=False, stop=False,
                                                          skip_group_check=True))
                    pe.quiet(lambda e, a=a: e.matmul(a[:, 0:128], identb, mask[:, 1, :], start=False, stop=False,
                                                     skip_group_check=True))
                    pe.quiet(lambda e, c=c, h=h: e.matmul(c, B["KT"][row(h), h // 2, 128:256],
                                                          B["QT"][row(h), h // 2, 128:256], start=False, stop=False,
                                                          skip_group_check=True))
                    pe.quiet(lambda e, c=c, h=h: e.matmul(c, sel[row(h), h, :], B["mT"][row(h), 128:256], start=False, stop=False,
                                                          skip_group_check=True))
                    tk = pe.op(lambda e, c=c: e.matmul(c, identb, mask[:, 1, :], start=False, stop=True,
                                                       skip_group_check=True))
                ip, P, pfreed = PT.take()
                te = act.op(lambda e, p=p, P=P: e.activation(
                    P, p.rearrange("p (j k) -> p j k", j=2)[:, :, 0:384], ACT.Exp), tk, *pfreed)
                PS.free(i, te)
                if g:
                    pv(g - 1, prev[0], prev[1], O, B, ofreed)
                    PT.free(prev[2], pe.last())
                prev = (P, te, ip)
                if g % 2:
                    yield
            pv(7, prev[0], prev[1], O, B, ofreed)
            PT.free(prev[2], pe.last())
            t = dve.op(lambda e: e.reciprocal(B["rc"], O[:, :, :, 8]), pe.last())
            for tile in range(2):
                t = dve.op(lambda e, tile=tile: e.tensor_tensor(
                    B["ctx"][:, tile, :].rearrange("p (h e) -> p h e", e=8), O[:, tile, :, 0:8],
                    bc(B["rc"][:, tile, :], 2, 8), ALU.mult), t if tile == 0 else None)
            PO.free(io, t)
            B["t_ctx"] = t

        def pv(g, P, te, O, B, ofreed):
            for j in range(2):
                h = 2 * g + j
                w = (te, *ofreed) if j == 0 else ()
                for tile, cols, kt, st, sp_ in ((0, 0, 0, True, True), (1, 128, 0, True, False), (1, 256, 1, False, True)):
                    f = lambda e, tile=tile, cols=cols, kt=kt, st=st, sp_=sp_, j=j, h=h: e.matmul(
                        O[:, tile, h, :], P[:, j, cols:cols + 128], B["va"][:, kt, h, :], start=st, stop=sp_,
                        skip_group_check=True)
                    if j == 1 and kt == 1:
                        pe.op(f, *w)
                    else:
                        pe.quiet(f, *w)
                    w = ()

        def phase_a():
            fence()
            split_psum(3)
            top[0] = base
            new_phase()
            raw_ut = sb([48, 48, 128])
            raw_v = sb([48, 48, 8])
            oU, oV = sb([96, 128]), sb([96, 128])
            f1U, f1V = sb([64, 128]), sb([64, 512])
            f2U, f2V = sb([64, 512]), sb([64, 128])
            ksel = sb([128, 16, 128])
            W, bias = sb([128, 384]), sb([128, 384])
            Wo, bo = sb([128, 128]), sb([128, 128])
            W1, b1 = sb([128, 512]), sb([128, 4])
            W2, b2 = sb([128, 4, 128]), sb([128, 128])
            sel = sb([128, 16, 128], BF16)
            ln = sb([128, 4])
            tw = [dma(x, d[n]) for x, n in ((raw_ut, "aUT"), (raw_v, "aV"), (oU, "aoUT"), (oV, "aoV"), (f1U, "af1UT"),
                                            (f1V, "af1V"), (f2U, "af2UT"), (f2V, "af2V"), (ksel, "ksel"), (b1, "af1b"),
                                            (ln, "aln"))]
            tb = dma(bias, d["ab"].partition_broadcast(128) if 0 else d["ab"].broadcast_to([128, 384]))
            tbo = dma(bo, d["aob"].broadcast_to([128, 128]))
            tb2 = dma(b2, d["af2b"].broadcast_to([128, 128]))
            s8 = float(np.float32(1.0) / np.sqrt(np.float32(8.0)))
            t_sel = pool.op(lambda e: e.tensor_copy(sel, ksel), tw[8])
            i, p, freed = PS.take()
            for j in range(48):
                f = lambda e, j=j: e.matmul(p[:, 8 * j:8 * j + 8], raw_ut[:, j, :], raw_v[:, j, :], start=True, stop=True,
                                            skip_group_check=True)
                if j == 47:
                    tk = pe.op(f)
                else:
                    pe.quiet(f, *((*freed, tw[0], tw[1]) if j == 0 else ()))
            act.op(lambda e: e.activation(W[:, 0:128], p[:, 0:128], ACT.Copy, scale=s8), tk)
            t_W = act.op(lambda e: e.activation(W[:, 128:384], p[:, 128:384], ACT.Copy))
            PS.free(i, t_W)
            t_b = act.op(lambda e: e.activation(bias[:, 0:128], bias[:, 0:128], ACT.Copy, scale=s8), tb)
            i, p, freed = PS.take()
            pe.quiet(lambda e: e.matmul(p[:, 0:128], oU, oV, start=True, stop=True), *freed, tw[2], tw[3])
            tk = pe.op(lambda e: e.matmul(p[:, 512:1024], f1U, f1V, start=True, stop=True), tw[4], tw[5])
            act.op(lambda e: e.activation(Wo, p[:, 0:128], ACT.Copy), tk)
            t_W1 = act.op(lambda e: e.activation(W1, p[:, 512:1024], ACT.Copy))
            PS.free(i, t_W1)
            i, p, freed = PS.take()
            for c in range(4):
                tk = pe.op(lambda e, c=c, p=p: e.matmul(p[:, 128 * c:128 * c + 128], f2U[:, 128 * c:128 * c + 128], f2V,
                                                        start=True, stop=True, skip_group_check=True),
                           *freed, tw[6], tw[7])
            t_W2 = act.op(lambda e: e.activation(W2, p[:, 0:512].rearrange("p (c n) -> p c n", c=4), ACT.Copy), tk)
            PS.free(i, t_W2)

            bufs = attention_buffers()
            prepare_attention(bufs)
            done = {}

            def unit(b):
                B = bufs[b % 2]
                prior = done.get(b - 2, ())
                X = [XR[:, 2 * b, :], XR[:, 2 * b + 1, :]]
                h, y = B["h"], B["y"]
                t = layer_norm(X, [h[:, 0, :], h[:, 1, :]], B["st"], t_x[b // 4], *prior)
                yield
                t = layer_norm([h[:, 0, :], h[:, 1, :]], [y[:, 0, :], y[:, 1, :]], B["st"], t)
                yield
                i, p, tk = turn([y[:, 0, :], y[:, 1, :]], t)
                t_h = act.op(lambda e: e.activation(B["hT"], p[:, 0:256], ACT.Identity, bias=ln[:, 1:2], scale=ln[:, 0:1]),
                             tk, tw[10])
                PS.free(i, t_h)
                yield
                yield from attention(B, W, bias, sel, (t_W, t_b, t_sel), t_h)
                yield
                i, p, tk = turn([B["ctx"][:, 0, :], B["ctx"][:, 1, :]], B["t_ctx"])
                t = act.op(lambda e: e.activation(B["cT"], p[:, 0:256], ACT.Copy), tk)
                PS.free(i, t)
                i, p, freed = PS.take()
                pe.quiet(lambda e: e.matmul(p[:, 0:128], B["cT"][:, 0:128], Wo, start=True, stop=True,
                                            skip_group_check=True), t, *freed)
                tk = pe.op(lambda e: e.matmul(p[:, 128:256], B["cT"][:, 128:256], Wo, start=True, stop=True,
                                              skip_group_check=True))
                th = pool.op(lambda e: e.tensor_tensor(h, h, bc(bo, 1, 2), ALU.add), tbo, B["t_ctx"])
                t = dve.op(lambda e: e.tensor_tensor(XX[:, 2 * b:2 * b + 2, :], h,
                                                     p[:, 0:256].rearrange("p (t f) -> p t f", t=2), ALU.add), tk, th)
                PS.free(i, t)
                done[b] = (t,)

            drive([unit(b) for b in range(NB)], 2)
            done_h = dict(done)
            fence()
            new_phase()
            mb = [{"st": stats(), "z": sb([128, 2, 128]), "zT": sb([128, 256]), "g": sb([128, 4, 256])} for _ in range(2)]
            mdone = {}

            def mlp(b):
                M = mb[b % 2]
                H = XX[:, 2 * b:2 * b + 2, :]
                z = M["z"]
                t = layer_norm([H[:, 0, :], H[:, 1, :]], [z[:, 0, :], z[:, 1, :]], M["st"], *mdone.get(b - 2, ()))
                yield
                i, p, tk = turn([z[:, 0, :], z[:, 1, :]], t)
                t = act.op(lambda e: e.activation(M["zT"], p[:, 0:256], ACT.Identity, bias=ln[:, 3:4], scale=ln[:, 2:3]), tk)
                PS.free(i, t)
                i, p, freed = PS.take()
                for c in range(4):
                    tk = pe.op(lambda e, c=c, p=p: e.matmul(p[:, 256 * c:256 * c + 256], W1[:, 128 * c:128 * c + 128],
                                                            M["zT"], start=True, stop=True, skip_group_check=True),
                               t, *freed, t_W1)
                for c in range(4):
                    t = act.op(lambda e, c=c, p=p: e.activation(M["g"][:, c, :], p[:, 256 * c:256 * c + 256],
                                                                ACT.Gelu_apprx_tanh, bias=b1[:, c:c + 1]), tk, tw[9])
                PS.free(i, t)
                yield
                i, p, freed = PS.take()
                for tile in range(2):
                    for c in range(4):
                        tk = pe.op(lambda e, c=c, tile=tile, p=p: e.matmul(
                            p[:, 128 * tile:128 * tile + 128], M["g"][:, c, 128 * tile:128 * tile + 128], W2[:, c, :],
                            start=(c == 0), stop=(c == 3), skip_group_check=True), t, *freed, t_W2)
                t = dve.op(lambda e: e.tensor_tensor(z, H, p[:, 0:256].rearrange("p (t f) -> p t f", t=2), ALU.add), tk)
                PS.free(i, t)
                t = dve.op(lambda e: e.tensor_tensor(z, z, bc(b2, 1, 2), ALU.add), t, tb2)
                yield
                mdone[b] = (add_ln_residual(z, b, M["st"], None, t),)

            drive([mlp(b) for b in range(NB)], 2)

        def phase_c():
            fence()
            split_psum(3)
            top[0] = base
            new_phase()
            W, Wo, bo = sb([128, 384]), sb([128, 128]), sb([128, 128])
            ksel, sel = sb([128, 16, 128]), sb([128, 16, 128], BF16)
            t_W, t_Wo, t_s = dma(W, d["cW"]), dma(Wo, d["cWo"]), dma(ksel, d["ksel"])
            tbo = dma(bo, d["cbo"].broadcast_to([128, 128]))
            t_sel = pool.op(lambda e: e.tensor_copy(sel, ksel), t_s)
            s8 = float(np.float32(1.0) / np.sqrt(np.float32(8.0)))
            t_Ws = act.op(lambda e: e.activation(W[:, 0:128], W[:, 0:128], ACT.Copy, scale=s8), t_W)
            bufs = attention_buffers()
            prepare_attention(bufs)
            done = {}

            def unit(b):
                B = bufs[b % 2]
                X = [XR[:, 2 * b, :], XR[:, 2 * b + 1, :]]
                h, y = B["h"], B["y"]
                t = layer_norm(X, [h[:, 0, :], h[:, 1, :]], B["st"], t_x[b // 4], *done.get(b - 2, ()))
                yield
                i, p, tk = turn([h[:, 0, :], h[:, 1, :]], t)
                t_h = act.op(lambda e: e.activation(B["hT"], p[:, 0:256], ACT.Copy), tk)
                PS.free(i, t_h)
                yield
                yield from attention(B, W, None, sel, (t_Ws, t_sel), t_h)
                yield
                i, p, tk = turn([B["ctx"][:, 0, :], B["ctx"][:, 1, :]], B["t_ctx"])
                t = act.op(lambda e: e.activation(B["cT"], p[:, 0:256], ACT.Copy), tk)
                PS.free(i, t)
                i, p, freed = PS.take()
                pe.quiet(lambda e: e.matmul(p[:, 0:128], B["cT"][:, 0:128], Wo, start=True, stop=True,
                                            skip_group_check=True), t, t_Wo, *freed)
                tk = pe.op(lambda e: e.matmul(p[:, 128:256], B["cT"][:, 128:256], Wo, start=True, stop=True,
                                              skip_group_check=True))
                t = dve.op(lambda e: e.tensor_tensor(y, p[:, 0:256].rearrange("p (t f) -> p t f", t=2), bc(bo, 1, 2),
                                                     ALU.add), tk, tbo)
                PS.free(i, t)
                yield
                done[b] = (add_ln_residual(y, b, B["st"], None, t),)

            drive([unit(b) for b in range(NB)], 2)

        def phase_b():
            fence()
            split_psum(4)
            top[0] = base
            new_phase()
            wq, kT = sb([64, 8, 128]), sb([64, 8, 64])
            Wsim, Wdn, Wue, Wup = sb([128, 512]), sb([128, 4, 128]), sb([128, 4, 128]), sb([128, 512])
            Wd = sb([128, 512])
            io, iob = sb([128, 64, 8]), sb([128, 64, 8], BF16)
            x8, w8, w8b = sb([128, 8, 8]), sb([128, 8]), sb([128, 8], BF16)
            tw = {n: dma(a, d[n]) for a, n in ((wq, "bWq"), (kT, "bkT"), (Wdn, "bdn"), (Wue, "bue"), (Wup, "bup"),
                                               (Wd, "bdT"), (io, "kiota"), (x8, "kx8"), (w8, "kw8"))}
            pool.op(lambda e: e.tensor_copy(iob, io), tw["kiota"])
            t_io = pool.op(lambda e: e.tensor_copy(w8b, w8), tw["kw8"])
            i, p, freed = PS.take()
            for g in range(8):
                tk = pe.op(lambda e, g=g: e.matmul(p[:, 64 * g:64 * g + 64], wq[:, g, :], kT[:, g, :], start=True,
                                                   stop=True, skip_group_check=True), *freed, tw["bWq"], tw["bkT"])
            t_sim = act.op(lambda e: e.activation(Wsim, p[:, 0:512], ACT.Copy), tk)
            PS.free(i, t_sim)
            ub = [{"st": stats(), "h": sb([128, 2, 128]), "hT": sb([128, 256]), "up": sb([128, 4, 256]),
                   "AT": sb([128, 4, 128]), "y": sb([128, 2, 128])} for _ in range(2)]
            tb_ = [{"SP": sb([128, 1024]), "v8": sb([128, 8, 8]), "ix": sb([128, 8, 8], U32), "ixf": sb([128, 8, 8]),
                    "iyb": sb([128, 4, 8], BF16), "C": sb([128, 4, 64]), "C2": sb([128, 4, 64]), "c8": sb([128, 4, 8]),
                    "M": sb([128, 4, 64]), "n": sb([128, 4, 8]), "E": sb([128, 576]), "Z": sb([128, 4]),
                    "rz": sb([128, 4]), "big": sb([128, 4, 8]), "oh": sb([128, 4, 64]), "thr": sb([128, 4, 8]),
                    "eq": sb([128, 256, 8], BF16), "R": sb([128, 4, 64]), "cs": sb([128, 1]),
                    "G": sb([128, 4, 8, 64]), "G2": sb([128, 4, 8, 64])} for _ in range(2)]
            done = {}
            tdone = [(), ()]

            def unit(b):
                U = ub[b % 2]
                h, hT = U["h"], U["hT"]
                t = layer_norm([XR[:, 2 * b, :], XR[:, 2 * b + 1, :]], [h[:, 0, :], h[:, 1, :]], U["st"], t_x[b // 4],
                               *done.get(b - 2, ()))
                i, p, tk = turn([h[:, 0, :], h[:, 1, :]], t)
                t_h = act.op(lambda e: e.activation(hT, p[:, 0:256], ACT.Copy), tk)
                PS.free(i, t_h)
                yield
                for tile in range(2):
                    T = tb_[tile]
                    SP, v8, ix, ixf, C, C2, c8, M, E = (T[n] for n in ("SP", "v8", "ix", "ixf", "C", "C2", "c8", "M", "E"))
                    SIM = SP[:, 0:512].rearrange("p (g k) -> p g k", g=8)
                    PRJ = SP[:, 512:1024].rearrange("p (x y) -> p x y", x=8)
                    i, p, freed = PS.take()
                    pe.quiet(lambda e, p=p, tile=tile: e.matmul(p[:, 0:512], hT[:, 128 * tile:128 * tile + 128], Wsim,
                                                                start=True, stop=True), t_h, t_sim, *freed)
                    tk = pe.op(lambda e, p=p, tile=tile: e.matmul(p[:, 512:1024], hT[:, 128 * tile:128 * tile + 128], Wd,
                                                                  start=True, stop=True), tw["bdT"])
                    ts = act.op(lambda e, p=p, SP=SP: e.activation(SP, p, ACT.Copy), tk, *tdone[tile])
                    PS.free(i, ts)
                    for g in range(8):
                        t = dve.op(lambda e, g=g, v8=v8, SIM=SIM: e.max(v8[:, g, :], SIM[:, g, :]), ts, *tdone[tile])
                    for g in range(8):
                        t = dve.op(lambda e, g=g, v8=v8, SIM=SIM, ix=ix: e.max_index(ix[:, g, :], v8[:, g, :], SIM[:, g, :]), t)
                    ti = dve.op(lambda e, ix=ix, ixf=ixf: e.tensor_copy(ixf, ix), t)
                    C4 = C.rearrange("p h (i j) -> p h i j", i=8)
                    tc = dve.op(lambda e, C4=C4, v8=v8: e.tensor_tensor(
                        C4, bc(v8[:, 0:4, :], 3, 8), bc(v8[:, 4:8, :], 2, 8), ALU.add))
                    for hh in range(4):
                        t = dve.op(lambda e, hh=hh, c8=c8, C=C: e.max(c8[:, hh, :], C[:, hh, :]), tc)
                    for hh in range(4):
                        t = dve.op(lambda e, hh=hh, c8=c8, C=C, C2=C2: e.match_replace(
                            C2[:, hh, :], c8[:, hh, :], C[:, hh, :], -3.0e38), t)
                    ey = E[:, 0:256].rearrange("p (h y) -> p h y", h=4)
                    ex = E[:, 256:288].rearrange("p (h x) -> p h x", h=4)
                    e8 = E[:, 288:320].rearrange("p (h x) -> p h x", h=4)
                    eC = E[:, 320:576].rearrange("p (h x) -> p h x", h=4)
                    dve.op(lambda e, ey=ey, SIM=SIM, v8=v8: e.tensor_tensor(ey, SIM[:, 4:8, :],
                           v8[:, 4:8, 0:1].broadcast_to([128, 4, 64]), ALU.subtract))
                    dve.op(lambda e, ex=ex, SIM=SIM, v8=v8: e.tensor_tensor(ex, SIM[:, 0:4, 0:8],
                           v8[:, 0:4, 0:1].broadcast_to([128, 4, 8]), ALU.subtract))
                    dve.op(lambda e, e8=e8, c8=c8: e.tensor_tensor(e8, c8, c8[:, :, 0:1].broadcast_to([128, 4, 8]),
                                                                  ALU.subtract))
                    t = dve.op(lambda e, eC=eC, C=C, c8=c8: e.tensor_tensor(
                        eC, C, c8[:, :, 0:1].broadcast_to([128, 4, 64]), ALU.subtract))
                    te = act.op(lambda e, E=E: e.activation(E, E, ACT.Exp), t)
                    yield
                    M_, n_, oh, thr, big, Z, rz = (T[n] for n in ("M", "n", "oh", "thr", "big", "Z", "rz"))
                    eq, R, iyb = T["eq"], T["R"], T["iyb"]
                    t = dve.op(lambda e, iyb=iyb, ixf=ixf: e.tensor_copy(iyb, ixf[:, 4:8, :]), ti)
                    for hh in range(4):
                        t_eq = dve.op(lambda e, hh=hh, eq=eq, iyb=iyb: e.tensor_tensor(
                            eq[:, 64 * hh:64 * hh + 64, :], iob, bc(iyb[:, hh, :], 1, 64), ALU.is_equal), t, t_io)
                    t_w8 = pool.op(lambda e, eq=eq: e.tensor_tensor(eq, eq, bc(w8b, 1, 256), ALU.mult), t_eq)
                    G, G2 = T["G"], T["G2"]
                    t = dve.op(lambda e, M_=M_, C=C, C2=C2: e.tensor_tensor(M_, C, C2, ALU.not_equal))
                    t = dve.op(lambda e, M_=M_, n_=n_: e.tensor_reduce(
                        n_, M_.rearrange("p h (i j) -> p h i j", i=8), AX.X, ALU.add), t)
                    oh4 = oh.rearrange("p h (x i) -> p h x i", x=8)
                    t = dve.op(lambda e, oh4=oh4, ixf=ixf: e.tensor_tensor(
                        oh4, bc(x8, 1, 4), bc(ixf[:, 0:4, :], 2, 8), ALU.is_equal), tw["kx8"])
                    t = dve.op(lambda e, oh4=oh4, n_=n_: e.tensor_tensor(oh4, oh4, bc(n_, 2, 8), ALU.mult), t)
                    t = dve.op(lambda e, thr=thr, oh4=oh4: e.tensor_reduce(thr, oh4, AX.X, ALU.add), t)
                    t_thr = dve.op(lambda e, thr=thr: e.tensor_scalar(thr, thr, -1.0, 8.0, ALU.mult, ALU.add), t)
                    t = dve.op(lambda e, Z=Z, e8=e8: e.tensor_reduce(Z, e8, AX.X, ALU.add), te)
                    t = dve.op(lambda e, Z=Z, rz=rz: e.reciprocal(rz, Z), t)
                    t_ex = dve.op(lambda e, ex=ex, rz=rz: e.tensor_tensor(ex, ex, bc(rz, 2, 8), ALU.mult), t)
                    dve.op(lambda e, big=big, ixf=ixf: e.tensor_scalar(big, ixf[:, 0:4, :], 7.5, None, ALU.is_gt))
                    t = dve.op(lambda e, M_=M_, eC=eC: e.tensor_tensor(M_, M_, eC, ALU.mult))
                    t = dve.op(lambda e, big=big, rz=rz: e.tensor_tensor(big, big, bc(rz, 2, 8), ALU.mult), t)
                    t = dve.op(lambda e, big=big, SP=SP: e.tensor_scalar(big, big, SP[:, 1023:1024], None, ALU.mult), t)
                    t_c = dve.op(lambda e, M_=M_, big=big: e.tensor_tensor(
                        M_.rearrange("p h (i j) -> p h i j", i=8), M_.rearrange("p h (i j) -> p h i j", i=8),
                        bc(big, 3, 8), ALU.mult), t)
                    for hh in range(4):
                        t_g2 = pool.op(lambda e, hh=hh, G2=G2, PRJ=PRJ, ex=ex: e.tensor_tensor(
                            G2[:, hh, :, :], PRJ, bc(ex[:, hh, :], 2, 64), ALU.mult), t_ex)
                    t = t_w8
                    t = dve.op(lambda e, eq=eq, R=R: e.tensor_reduce(R.rearrange("p h y -> p (h y)"), eq, AX.X, ALU.add), t)
                    for hh in range(4):
                        t = dve.op(lambda e, hh=hh, G=G, R=R, thr=thr: e.tensor_tensor(
                            G[:, hh, :, :], bc(R[:, hh, :], 1, 8), bc(thr[:, hh, :], 2, 64), ALU.is_gt), t)
                    for hh in range(4):
                        t = dve.op(lambda e, hh=hh, G=G, ey=ey: e.tensor_tensor(
                            G[:, hh, :, :], G[:, hh, :, :], bc(ey[:, hh, :], 1, 8), ALU.mult), t)
                    T["t_g"] = dve.op(lambda e, G=G, G2=G2: e.tensor_tensor(G, G, G2, ALU.mult), t, t_g2)
                    T["t_c"] = t_c
                    yield
                i, p, freed = PS.take()
                for c in range(4):
                    tk = pe.op(lambda e, c=c, p=p: e.matmul(p[:, 256 * c:256 * c + 256], Wup[:, 128 * c:128 * c + 128], hT,
                                                            start=True, stop=True, skip_group_check=True),
                               *freed, tw["bup"])
                t_up = act.op(lambda e, p=p: e.activation(U["up"], p.rearrange("p (c q) -> p c q", c=4), ACT.Silu), tk)
                PS.free(i, t_up)
                for tile in range(2):
                    T = tb_[tile]
                    act.op(lambda e, T=T: e.activation(T["M"], T["M"], ACT.Silu, accum_out=T["cs"]), T["t_c"])
                    t = act.op(lambda e, T=T: e.activation(T["G"], T["G"], ACT.Silu), T["t_g"])
                    g511 = T["G"].rearrange("p h x y -> p (h x y)")[:, 511:512]
                    T["t_s"] = dve.op(lambda e, T=T, g511=g511: e.tensor_tensor(g511, g511, T["cs"], ALU.add), t)
                yield
                io_, po, ofreed = PS.take()
                for tile in range(2):
                    T = tb_[tile]
                    Gf = T["G"].rearrange("p h x y -> p h (x y)")
                    i, p, freed = PS.take()
                    for c in range(4):
                        for hh in range(4):
                            tk = pe.op(lambda e, c=c, hh=hh, p=p, Gf=Gf: e.matmul(
                                p[:, 128 * c:128 * c + 128], Gf[:, hh, 128 * c:128 * c + 128], ident,
                                start=(hh == 0), stop=(hh == 3), skip_group_check=True),
                                *((*freed, T["t_s"]) if c == hh == 0 else ()))
                    tdone[tile] = (tk,)
                    ta = act.op(lambda e, p=p: e.activation(U["AT"], p[:, 0:512].rearrange("p (c q) -> p c q", c=4),
                                                            ACT.Copy), tk, *((tprev,) if tile else ()))
                    PS.free(i, ta)
                    for c in range(8):
                        lhs = U["up"][:, c, 128 * tile:128 * tile + 128] if c < 4 else U["AT"][:, c - 4, :]
                        rhs = Wdn[:, c, :] if c < 4 else Wue[:, c - 4, :]
                        tprev = pe.op(lambda e, c=c, lhs=lhs, rhs=rhs, tile=tile: e.matmul(
                            po[:, 128 * tile:128 * tile + 128], lhs, rhs, start=(c == 0), stop=(c == 7),
                            skip_group_check=True), *((ta, t_up, tw["bdn"], tw["bue"], *ofreed) if c == 0 else ()))
                t = dve.op(lambda e: e.tensor_copy(U["y"], po[:, 0:256].rearrange("p (t f) -> p t f", t=2)), tprev)
                PS.free(io_, t)
                yield
                done[b] = (add_ln_residual(U["y"], b, U["st"], None, t),)

            drive([unit(b) for b in range(NB)], 1)

        def phase_d():
            fence()
            split_psum(4)
            top[0] = base
            new_phase()
            wb = [{"qkv": sb([128, 3072]), "wo": sb([128, 8, 128]), "w1": sb([128, 682]), "w2": sb([128, 3, 128]),
                   "b1": sb([128, 6]), "ln": sb([128, 2]), "tab": sb([128, 2, 4, 64])} for _ in range(2)]
            rope = sb([128, 2, 4, 64])
            scb = sb([128, 4, 64])
            t_rope = dma(rope, d["krope"])
            st2 = [stats() for _ in range(2)]
            XS = [sb([128, 32 + 256]) for _ in range(2)]
            T1 = Ring([sb([128, 2048]) for _ in range(2)])
            T2 = Ring([sb([128, 2048])])
            SQ = Ring([sb([128, 2048])])
            SS = Ring([sb([128, 64]) for _ in range(2)])
            QT = Ring([sb([128, 8, 128]) for _ in range(1)])
            KT = [sb([128, 8, 160]) for _ in range(2)]
            V = Ring([sb([96, 2, 1024]) for _ in range(1)])
            PP = Ring([sb([128, 16, 96]) for _ in range(1)])
            PTr = Ring([sb([96, 16, 128]) for _ in range(1)])
            OT = Ring([sb([128, 8, 128]) for _ in range(1)])
            sm = Ring([sb([128, 3, 16]) for _ in range(2)])
            ffn_base = top[0]
            for s in XS:
                pool.op(lambda e, s=s: e.memset(s[:, 0:33], 0.0))
            t_z = pool.last()

            for b in range(NB):
                t_xx = layer_norm([XR[:, 2 * b, :], XR[:, 2 * b + 1, :]], [XX[:, 2 * b, :], XX[:, 2 * b + 1, :]],
                                  st2[b % 2], t_x[b // 4])

            wfree = [(), ()]
            ready = {}
            scfree = [()]

            def load(l):
                w = wb[l % 2]
                fr = wfree[l % 2]
                r = [dma(w["qkv"], d["dWqkv"][l], *fr), dma(w["wo"], d["dWo"][l]), dma(w["w1"], d["dW1"][l]),
                     dma(w["w2"], d["dW2"][l]), dma(w["b1"], d["db1"][l]), dma(w["ln"], d["dln"][l])]
                ts = dma(scb, d["dsc"][l:l + 1].broadcast_to([128, 4, 64]), *scfree[0])
                for t in range(2):
                    tt = pool.op(lambda e, w=w, t=t: e.tensor_tensor(w["tab"][:, t, :, :], rope[:, t, :, :], scb, ALU.mult),
                                 t_rope, ts, *fr)
                scfree[0] = (tt,)
                ready[l] = (*r, tt)

            xx_tok = {k: t_xx for k in range(2 * NB)}
            xsfree = [(), ()]
            ktfree = [(), ()]
            ktoks = {}
            xstok = {}

            def shifted(l, b, *extra):
                s = XS[b % 2]
                i, p, tk = turn([XX[:, 2 * b, :], XX[:, 2 * b + 1, :]], xx_tok[2 * b], xx_tok[2 * b + 1], *extra)
                act.op(lambda e: e.activation(s[0:64, 32:288], p[0:64, 0:256], ACT.Copy), tk, t_z, *xsfree[b % 2])
                t = act.op(lambda e: e.activation(s[64:128, 33:288], p[64:128, 0:255], ACT.Copy))
                PS.free(i, t)
                return t

            def attn(l, k):
                b, tile = k // 2, k % 2
                w = wb[l % 2]
                if tile == 0:
                    xstok[b] = shifted(l, b)
                t_s = xstok[b]
                s = XS[b % 2]
                xs = s[:, 32 + 128 * tile:160 + 128 * tile]
                i1, a1, f1 = T1.take()
                i2, a2, f2 = T2.take()
                iq, sq, fq = SQ.take()
                iss, ss, fss = SS.take()
                for half in range(2):
                    i, p, freed = PS.take()
                    for c in range(2):
                        col = 1024 * half + 512 * c
                        tk = pe.op(lambda e, p=p, c=c, col=col: e.matmul(p[:, 512 * c:512 * c + 512], xs,
                                   w["qkv"][:, col:col + 512], start=True, stop=True), *freed, t_s, ready[l][0])
                    tsq = act.op(lambda e, p=p, half=half: e.activation(sq[:, 1024 * half:1024 * half + 1024], p, ACT.Square),
                                 tk, *fq)
                    pv4 = p.rearrange("p (h u e) -> p h u e", h=16, u=2)
                    ph = p.rearrange("p (h e) -> p h e", h=16)
                    cs = w["tab"][:, tile, 2 * half, :]
                    sn = w["tab"][:, tile, 2 * half + 1, :]
                    o1 = a1[:, 1024 * half:1024 * half + 1024].rearrange("p (h e) -> p h e", h=16)
                    o2 = a2[:, 1024 * half:1024 * half + 1024].rearrange("p (h u e) -> p h u e", h=16, u=2)
                    dve.op(lambda e, ph=ph, cs=cs, o1=o1: e.tensor_tensor(o1, ph, bc(cs, 1, 16), ALU.mult),
                           tk, tsq, ready[l][6], *f1, *f2)
                    for u in range(2):
                        t2 = dve.op(lambda e, u=u, pv4=pv4, sn=sn, o2=o2: e.tensor_tensor(
                            o2[:, :, u, :], pv4[:, :, 1 - u, :], bc(sn[:, 32 * u:32 * u + 32], 1, 16), ALU.mult))
                    PS.free(i, t2)
                t = dve.op(lambda e: e.tensor_reduce(ss[:, 0:32], sq.rearrange("p (h e) -> p h e", h=32), AX.X, ALU.add),
                           tsq, *fss)
                SQ.free(iq, t)
                t = pool.op(lambda e: e.tensor_scalar(ss[:, 32:64], ss[:, 0:32], 1e-24, None, ALU.max), t)
                t_r = pool.op(lambda e: e.tensor_tensor(ss[:, 0:32], ss[:, 32:64], mhalf32, ALU.pow), t)
                ta = dve.op(lambda e: e.tensor_tensor(a1, a1, a2, ALU.add), t2)
                T2.free(i2, ta)
                yield
                iv, v, fv = V.take()
                for blk in range(2):
                    i, p, freed = PS.take()
                    c0 = 128 * tile + 64 * blk
                    for c in range(2):
                        tk = pe.op(lambda e, p=p, c=c, c0=c0: e.matmul(
                            p[0:96, 512 * c:512 * c + 512], s[:, c0:c0 + 96], w["qkv"][:, 2048 + 512 * c:2560 + 512 * c],
                            start=True, stop=True), *freed, t_s)
                    tv = act.op(lambda e, p=p, blk=blk: e.activation(v[:, blk, :], p[0:96, :], ACT.Copy), tk, *fv)
                    PS.free(i, tv)
                xsfree[b % 2] = (tk,)
                tn = dve.op(lambda e: e.tensor_tensor(a1.rearrange("p (h e) -> p h e", h=32),
                                                      a1.rearrange("p (h e) -> p h e", h=32), bc(ss[:, 0:32], 2, 64),
                                                      ALU.mult), ta, t_r)
                SS.free(iss, tn)
                yield
                iqt, qT, fqt = QT.take()
                kT = KT[tile]
                for half in range(2):
                    i, p, freed = PS.take()
                    for c in range(8):
                        f = lambda e, p=p, c=c, half=half: e.transpose(
                            p[:, 128 * c:128 * c + 128], a1[:, 1024 * half + 128 * c:1024 * half + 128 * c + 128], ident)
                        if c < 7:
                            pe.quiet(f, *((tn, *freed) if c == 0 else ()))
                        else:
                            tk = pe.op(f)
                    pv_ = p.rearrange("p (c q) -> p c q", c=8)
                    if half == 0:
                        tq = act.op(lambda e, pv_=pv_: e.activation(qT, pv_, ACT.Copy), tk, *fqt)
                        PS.free(i, tq)
                    else:
                        tkt = act.op(lambda e, pv_=pv_: e.activation(kT[:, :, 32:160], pv_, ACT.Copy), tk, *ktfree[tile])
                        PS.free(i, tkt)
                T1.free(i1, tk)
                if tile == 0:
                    tp = pool.op(lambda e: e.memset(kT[:, :, 0:32], 0.0), *ktfree[tile])
                else:
                    tp = pool.op(lambda e: e.tensor_copy(kT[:, :, 0:32], KT[0][:, :, 128:160]), ktoks[k - 1], *ktfree[tile])
                    kprev_read = tp
                ktoks[k] = tkt
                yield
                ip_, P, fp = PP.take()
                ism, m3, fm = sm.take()
                mx, sums, rc = m3[:, 0, :], m3[:, 1, :], m3[:, 2, :]
                for g in range(2):
                    i, p, freed = PS.take()
                    for bank in range(2):
                        pe.quiet(lambda e, p=p, bank=bank: e.matmul(
                            p[:, 512 * bank:512 * bank + 384], identb, maskd[:, 1 if tile else 0, :], start=True, stop=False,
                            skip_group_check=True), *((*freed, tq, tkt, tp, t_mask) if bank == 0 else ()))
                        for j in range(4):
                            h = 8 * g + 2 * j + bank
                            r = slice(64 * (h % 2), 64 * (h % 2) + 64)
                            for blk in range(2):
                                o = p[64 * blk:64 * blk + 64, 512 * bank + 96 * j:512 * bank + 96 * j + 96]
                                f = lambda e, o=o, r=r, h=h, blk=blk: e.matmul(
                                    o, qT[r, h // 2, 64 * blk:64 * blk + 64], kT[r, h // 2, 64 * blk:64 * blk + 96],
                                    start=False, stop=False, skip_group_check=True)
                                if bank == 1 and j == 3 and blk == 1:
                                    tk = pe.op(f)
                                else:
                                    pe.quiet(f)
                    pv_ = p.rearrange("p (a c) -> p a c", a=2)[:, :, 0:384].rearrange("p a (h k) -> p a h k", h=4)
                    Pg = P[:, 8 * g:8 * g + 8, :].rearrange("p (a h) k -> p a h k", a=2)
                    mg = mx[:, 8 * g:8 * g + 8].rearrange("p (a h) -> p a h", a=2)
                    t = dve.op(lambda e, pv_=pv_, mg=mg: e.tensor_reduce(mg, pv_, AX.X, ALU.max), tk, *fm)
                    for a in range(2):
                        t_ = dve.op(lambda e, pv_=pv_, mg=mg, Pg=Pg, a=a: e.tensor_tensor(
                            Pg[:, a, :, :], pv_[:, a, :, :], bc(mg[:, a, :], 2, 96), ALU.subtract), t, *fp)
                    t = t_
                    PS.free(i, t)
                    te = act.op(lambda e, g=g: e.activation(P[:, 8 * g:8 * g + 8, :], P[:, 8 * g:8 * g + 8, :], ACT.Exp), t)
                QT.free(iqt, tk)
                if tile == 1:
                    ktfree[0] = (tk, kprev_read)
                    ktfree[1] = (tk,)
                yield
                t = dve.op(lambda e: e.tensor_reduce(sums, P, AX.X, ALU.add), te)
                t = dve.op(lambda e: e.reciprocal(rc, sums), t)
                t = dve.op(lambda e: e.tensor_tensor(P, P, bc(rc, 2, 96), ALU.mult), t)
                sm.free(ism, t)
                ipt, PT, fpt = PTr.take()
                for g in range(2):
                    i, p, freed = PS.take()
                    for j in range(8):
                        f = lambda e, p=p, j=j, g=g: e.transpose(p[0:96, 128 * j:128 * j + 128], P[:, 8 * g + j, :], ident)
                        if j < 7:
                            pe.quiet(f, *((t, *freed) if j == 0 else ()))
                        else:
                            tk = pe.op(f)
                    tpt = act.op(lambda e, p=p, g=g: e.activation(
                        PT[:, 8 * g:8 * g + 8, :], p[0:96, :].rearrange("p (h q) -> p h q", h=8), ACT.Copy), tk, *fpt)
                    PS.free(i, tpt)
                PP.free(ip_, tk)
                yield
                io_, o, fo = OT.take()
                i, p, freed = PS.take()
                for h in range(16):
                    for blk in range(2):
                        f = lambda e, p=p, h=h, blk=blk: e.matmul(
                            p[64 * (h % 2):64 * (h % 2) + 64, 128 * (h // 2) + 64 * blk:128 * (h // 2) + 64 * blk + 64],
                            v[:, blk, 64 * h:64 * h + 64], PT[:, 8 * (h // 8) + 4 * (h % 2) + (h % 8) // 2, 64 * blk:64 * blk + 64], start=True, stop=True,
                            skip_group_check=True)
                        if h == 15 and blk == 1:
                            tk = pe.op(f)
                        else:
                            pe.quiet(f, *((tpt, tv, *freed) if h == blk == 0 else ()))
                V.free(iv, tk)
                PTr.free(ipt, tk)
                t = act.op(lambda e, p=p: e.activation(o, p.rearrange("p (c q) -> p c q", c=8), ACT.Copy), tk, *fo)
                PS.free(i, t)
                i, p, freed = PS.take()
                for c in range(8):
                    tk = pe.op(lambda e, p=p, c=c: e.matmul(p[:, 0:128], o[:, c, :], w["wo"][:, c, :], start=(c == 0),
                                                            stop=(c == 7)), *((t, ready[l][1], *freed) if c == 0 else ()))
                OT.free(io_, tk)
                t = dve.op(lambda e, p=p: e.tensor_tensor(XX[:, k, :], XX[:, k, :], p[:, 0:128], ALU.add), tk)
                PS.free(i, t)
                xx_tok[k] = t

            fb = [{"st": stats(), "z": sb([128, 2, 128]), "zT": sb([128, 256]), "ge": sb([128, 3, 256]),
                   "g": sb([128, 3, 256])} for _ in range(1)]
            for F in fb:
                F["t1"] = dve.op(lambda e, F=F: e.memset(F["g"][64:128, 2, :], 1.0))
            ffree = [() for _ in fb]

            def ffn(l, b):
                F = fb[b % len(fb)]
                fr = ffree[b % len(fb)]
                w = wb[l % 2]
                s = XS[b % 2]
                t = shifted(l, b, *fr)
                i, p, tk = turn([s[:, 32:160], s[:, 160:288]], t)
                xsfree[b % 2] = (tk,)
                z = F["z"]
                t = layer_norm([p[:, 0:128], p[:, 128:256]], [z[:, 0, :], z[:, 1, :]], F["st"], tk, *fr)
                PS.free(i, t)
                yield
                i, p, tk = turn([z[:, 0, :], z[:, 1, :]], t)
                t = act.op(lambda e, p=p: e.activation(F["zT"], p[:, 0:256], ACT.Identity, bias=w["ln"][:, 1:2],
                                                       scale=w["ln"][:, 0:1]), tk, ready[l][5], *fr)
                PS.free(i, t)
                ig, pg, freed = PS.take()
                for c, (c0, n) in enumerate(CH):
                    tg = pe.op(lambda e, c=c, c0=c0, n=n: e.matmul(pg[0:n, 256 * c:256 * c + 256],
                               w["w1"][:, DI + c0:DI + c0 + n], F["zT"], start=True, stop=True, skip_group_check=True),
                               *((t, ready[l][2], *freed) if c == 0 else ()))
                ia, pa, freed = PS.take()
                for c, (c0, n) in enumerate(CH):
                    ta = pe.op(lambda e, c=c, c0=c0, n=n: e.matmul(pa[0:n, 256 * c:256 * c + 256],
                               w["w1"][:, c0:c0 + n], F["zT"], start=True, stop=True, skip_group_check=True),
                               *(freed if c == 0 else ()))
                for c, (c0, n) in enumerate(CH):
                    t = act.op(lambda e, c=c, n=n: e.activation(F["ge"][0:n, c, :], pg[0:n, 256 * c:256 * c + 256], ACT.Gelu,
                                                                bias=w["b1"][0:n, 3 + c:4 + c]), tg, ready[l][4], *fr)
                PS.free(ig, t)
                for c, (c0, n) in enumerate(CH):
                    td = dve.op(lambda e, c=c, n=n: e.scalar_tensor_tensor(
                        F["g"][0:n, c, :], pa[0:n, 256 * c:256 * c + 256], w["b1"][0:n, c:c + 1], F["ge"][0:n, c, :],
                        ALU.add, ALU.mult), t, ta, F["t1"])
                PS.free(ia, td)
                yield
                i, p, freed = PS.take()
                for tile in range(2):
                    for c in range(3):
                        n = 128 if c < 2 else 86
                        tk = pe.op(lambda e, p=p, c=c, n=n, tile=tile: e.matmul(
                            p[:, 128 * tile:128 * tile + 128], F["g"][0:n, c, 128 * tile:128 * tile + 128],
                            w["w2"][0:n, c, :], start=(c == 0), stop=(c == 2), skip_group_check=True),
                            *((td, ready[l][3], *freed) if tile == c == 0 else ()))
                t = dve.op(lambda e, p=p: e.tensor_tensor(XX[:, 2 * b:2 * b + 2, :], XX[:, 2 * b:2 * b + 2, :],
                                                          p[:, 0:256].rearrange("p (t f) -> p t f", t=2), ALU.add), tk)
                PS.free(i, t)
                xx_tok[2 * b] = xx_tok[2 * b + 1] = t
                ffree[b % len(fb)] = (t,)

            load(0)
            for l in range(run["depth"]):
                new_phase()
                if l + 1 < run["depth"]:
                    load(l + 1)
                drive([attn(l, k) for k in range(2 * NB)], 1)
                new_phase()
                drive([ffn(l, b) for b in range(NB)], 1)
                wfree[l % 2] = (pe.last(), act.last(), dve.last(), pool.last())
            for b in range(NB):
                t = layer_norm([XX[:, 2 * b, :], XX[:, 2 * b + 1, :]], [XX[:, 2 * b, :], XX[:, 2 * b + 1, :]], st2[b % 2],
                               xx_tok[2 * b], xx_tok[2 * b + 1])
                dve.op(lambda e, b=b: e.tensor_tensor(XR[:, 2 * b:2 * b + 2, :], XR[:, 2 * b:2 * b + 2, :],
                                                      XX[:, 2 * b:2 * b + 2, :], ALU.add), t)

        for ph, f in (("A", phase_a), ("B", phase_b), ("C", phase_c), ("D", phase_d)):
            if ph in run["phases"]:
                f()

        fence()
        s_out = ctx.enter_context(nc.semaphore("s_out"))
        n_out = 0
        for b0 in range(0, NB, 4):
            sp.e.dma_start(out[b0:b0 + 4].rearrange("b (t p) f -> p (b t) f", p=128),
                           XR[:, 2 * b0:2 * b0 + 8, :]).then_inc(s_out, 16)
            n_out += 16
        sp.wait((s_out, n_out), *t_x)


def constants():
    f = np.float32
    c = {"kident": np.eye(128, dtype=f)}
    q, k = np.arange(128)[:, None], np.arange(128)[None, :]
    m = np.where(k > q, f(-1e30), f(0)).astype(f)
    c["kmask"] = np.ascontiguousarray(np.stack([m, m.T], 1))
    r = (np.arange(128) % 64)[:, None]
    j = np.arange(96)[None, :]
    ok = (j >= r) & (j <= r + 32)
    first = ok & ((np.arange(128)[:, None] >= 64) | (j >= 32))
    md = np.stack([np.where(x, f(0), f(-1e30)).astype(f) for x in (first, ok)], 1)
    c["kmaskd"] = np.ascontiguousarray(np.tile(md, (1, 1, 4)))
    sel = np.zeros((128, 16, 128), f)
    for i in range(48):
        sel[i, i % 16, :] = sel[64 + i, i % 16, :] = -1.0
    c["ksel"] = sel
    half = np.arange(0, 64, 2, dtype=f)
    inv = (f(1.0) / np.power(f(10000.0), half / f(64))).astype(f)
    t = np.arange(256, dtype=f)
    fr = (t[:, None] * inv[None, :]).astype(f)
    fr = np.concatenate([fr, fr], -1)
    bs = (half + f(25.6)) / f(89.6)
    power = (t - 128) / 16
    sc = np.power(bs[None, :].astype(np.float64), power[:, None].astype(np.float64))
    sc = np.concatenate([sc, sc], -1)
    sign = np.where(np.arange(64) < 32, -1.0, 1.0)
    cs, sn = np.cos(fr.astype(np.float64)), np.sin(fr.astype(np.float64)) * sign
    tab = np.stack([8 * cs * sc, 8 * sn * sc, cs / sc, sn / sc], 1).astype(f)
    c["krope"] = np.ascontiguousarray(tab.reshape(2, 128, 4, 64).transpose(1, 0, 2, 3))
    c["kiota"] = np.ascontiguousarray(np.broadcast_to(np.arange(64, dtype=f)[None, :, None], (128, 64, 8)))
    c["kx8"] = np.ascontiguousarray(np.broadcast_to(np.arange(8, dtype=f)[None, :, None], (128, 8, 8)))
    c["kw8"] = np.ascontiguousarray(np.broadcast_to((8 - np.arange(8)).astype(f)[None, :], (128, 8)))
    return c


def layout(i):
    g = lambda n: np.asarray(i[n])
    C = np.ascontiguousarray
    a = {"x": g("L0_attn_hidden_states")}
    a["aUT"] = C(np.concatenate([g(f"L0_attn_{n}_U").transpose(2, 1, 0) for n in "qkv"], 1))
    a["aV"] = C(np.concatenate([g(f"L0_attn_{n}_V").transpose(1, 0, 2) for n in "qkv"], 1))
    a["ab"] = C(np.concatenate([g(f"L0_attn_{n}_b").reshape(1, 128) for n in "qkv"], 1))
    a["aoUT"] = C(g("L0_attn_out_U").T)
    a["aoV"] = g("L0_attn_out_V")
    a["aob"] = g("L0_attn_out_b").reshape(1, 128)
    a["af1UT"] = C(g("L0_attn_fc1_U").T)
    a["af1V"] = g("L0_attn_fc1_V")
    a["af1b"] = C(g("L0_attn_fc1_b").reshape(4, 128).T)
    a["af2UT"] = C(g("L0_attn_fc2_U").T)
    a["af2V"] = g("L0_attn_fc2_V")
    a["af2b"] = g("L0_attn_fc2_b").reshape(1, 128)
    a["aln"] = C(np.stack([g(f"L0_attn_{n}") for n in ("ln1_g", "ln1_b", "ln2_g", "ln2_b")], 1))
    a["bWq"] = C(g("L0_ffn_W_q").reshape(8, 64, 128).transpose(1, 0, 2))
    a["bkT"] = C(g("L0_ffn_keys").transpose(3, 2, 0, 1).reshape(64, 8, 64))
    a["bdT"] = C(g("L0_ffn_down_embed").T)
    a["bue"] = C(g("L0_ffn_up_embed").reshape(4, 128, 128).transpose(1, 0, 2))
    a["bup"] = C(g("L0_ffn_W_up").T)
    a["bdn"] = C(g("L0_ffn_W_down").T.reshape(4, 128, 128).transpose(1, 0, 2))
    a["cW"] = C(np.concatenate([g(f"L1_attn_W{n}") for n in "qkv"], 1))
    a["cWo"] = g("L1_attn_Wo")
    a["cbo"] = g("L1_attn_bo").reshape(1, 128)
    a["dWqkv"] = g("L1_ffn_Wqkv")
    qs, ks = g("L1_ffn_q_scale"), g("L1_ffn_k_scale")
    rot = lambda s: np.concatenate([s[:, 32:], s[:, :32]], 1)
    a["dsc"] = C(np.stack([qs, rot(qs), ks, rot(ks)], 1))
    a["dWo"] = C(g("L1_ffn_Wo").reshape(DEPTH, 8, 128, 128).transpose(0, 2, 1, 3))
    a["dln"] = C(np.stack([g("L1_ffn_ln_g"), g("L1_ffn_ln_b")], 2))
    a["dW1"] = g("L1_ffn_W1")
    b1, w2, b2 = g("L1_ffn_b1"), g("L1_ffn_W2"), g("L1_ffn_b2")
    pb = np.zeros((DEPTH, 128, 6), np.float32)
    pw = np.zeros((DEPTH, 128, 3, 128), np.float32)
    for c, (c0, n) in enumerate(CH):
        pb[:, 0:n, c] = b1[:, c0:c0 + n]
        pb[:, 0:n, 3 + c] = b1[:, DI + c0:DI + c0 + n]
        pw[:, 0:n, c, :] = w2[:, c0:c0 + n, :]
    pw[:, 85, 2, :] = b2
    a["db1"], a["dW2"] = pb, pw
    a.update(constants())
    return a


RUN = {"phases": "ABCD", "depth": DEPTH}


def kernel(**inputs):
    import concourse.bacc as _bacc
    from concourse.bass_utils import run_bass_kernel_spmd as _run

    nc = _bacc.Bacc("TRN2", target_bir_lowering=False, num_devices=1)
    arrays, d = {}, {}
    given = layout(inputs)
    for name, (shape, dt) in SPEC.items():
        a = np.ascontiguousarray(given[name])
        assert a.shape == shape, (name, a.shape)
        arrays[f"in_{name}"] = a
        d[name] = nc.dram_tensor(f"in_{name}", shape, dt, kind="ExternalInput").ap()
    out = nc.dram_tensor("out_0", (NB, 256, 128), F32, kind="ExternalOutput").ap()
    network(nc, d, out, RUN)
    r = _run(nc, [arrays], core_ids=[0])
    return r.results[0]["out_0"]
```

```python
from contextlib import ExitStack

import numpy as np

import concourse.bass as bass
from concourse import mybir

F32 = mybir.dt.float32
BF16 = mybir.dt.bfloat16
U32 = mybir.dt.uint32
ACT = mybir.ActivationFunctionType
ALU = mybir.AluOpType
AX = mybir.AxisListType

NB = 16
DEPTH = 6
EPS = 1e-5
DI = 341
CH = [(0, 128), (128, 128), (256, 85)]

SPEC = {
    "x": ((NB, 256, 128), F32),
    "aUT": ((48, 48, 128), F32),
    "aV": ((48, 48, 8), F32),
    "ab": ((1, 384), F32),
    "aoUT": ((96, 128), F32),
    "aoV": ((96, 128), F32),
    "aob": ((1, 128), F32),
    "af1UT": ((64, 128), F32),
    "af1V": ((64, 512), F32),
    "af1b": ((128, 4), F32),
    "af2UT": ((64, 512), F32),
    "af2V": ((64, 128), F32),
    "af2b": ((1, 128), F32),
    "aln": ((128, 4), F32),
    "bWq": ((64, 8, 128), F32),
    "bkT": ((64, 8, 64), F32),
    "bdT": ((128, 512), F32),
    "bue": ((128, 4, 128), F32),
    "bup": ((128, 512), F32),
    "bdn": ((128, 4, 128), F32),
    "cW": ((128, 384), F32),
    "cWo": ((128, 128), F32),
    "cbo": ((1, 128), F32),
    "dWqkv": ((DEPTH, 128, 3072), F32),
    "dsc": ((DEPTH, 4, 64), F32),
    "dWo": ((DEPTH, 128, 8, 128), F32),
    "dln": ((DEPTH, 128, 2), F32),
    "dW1": ((DEPTH, 128, 682), F32),
    "db1": ((DEPTH, 128, 6), F32),
    "dW2": ((DEPTH, 128, 3, 128), F32),
    "kident": ((128, 128), F32),
    "kmask": ((128, 2, 128), F32),
    "kmaskd": ((128, 2, 384), F32),
    "ksel": ((128, 1024), F32),
    "krope": ((128, 2, 4, 64), F32),
    "kiota": ((128, 64, 8), F32),
    "kx8": ((128, 8, 8), F32),
    "kw8": ((128, 8), F32),
}


class Queue:

    def __init__(self, name, engine):
        self.name, self.e, self.sem, self.n = name, engine, None, 0

    def wait(self, *tokens):
        for t in tokens:
            if t is not None:
                self.e.wait_ge(t[0], t[1])

    def op(self, f, *tokens):
        self.wait(*tokens)
        self.n += 1
        f(self.e).then_inc(self.sem, 1)
        return (self.sem, self.n)

    def quiet(self, f, *tokens):
        self.wait(*tokens)
        f(self.e)

    def last(self):
        return (self.sem, self.n) if self.n else None


class Ring:

    def __init__(self, bufs):
        self.bufs, self.k, self.freed = bufs, 0, [()] * len(bufs)

    def take(self):
        i = self.k % len(self.bufs)
        self.k += 1
        freed = self.freed[i]
        assert freed is not None, "a buffer is taken before its last reader is known"
        self.freed[i] = None
        return i, self.bufs[i], freed

    def free(self, i, *tokens):
        self.freed[i] = tokens


def network(nc, d, out, run):
    ctx = ExitStack()
    with ctx:
        pe, act, dve, pool, sp = [Queue(n, e) for n, e in (
            ("pe", nc.tensor), ("act", nc.scalar), ("dve", nc.vector), ("pool", nc.gpsimd), ("sp", nc.sync))]
        queues = (pe, act, dve, pool)
        phases = [0]
        held = []

        def new_phase():
            for q in queues:
                if q.n or q.sem is None:
                    q.sem = ctx.enter_context(nc.semaphore(f"s_{q.name}{phases[0]}"))
                    q.n = 0
            phases[0] += 1

        def fence():
            ends = [q.last() for q in queues]
            for q in (*queues, sp):
                q.wait(*ends)

        nsem = [0]

        def dma(dst, src, *tokens, q=None):
            s = ctx.enter_context(nc.semaphore(f"s_d{nsem[0]}"))
            nsem[0] += 1
            q = q or sp
            q.wait(*tokens)
            q.e.dma_start(dst, src).then_inc(s, 16)
            return (s, 16)

        TOTAL = 51800
        arena = ctx.enter_context(nc.sbuf_tensor("arena", [128, TOTAL], F32))
        top = [0]

        def sb(shape, dt=F32):
            n = 1
            for s in shape[1:]:
                n *= s
            words = n if dt in (F32, U32) else (n + 1) // 2
            a = arena[0:shape[0], top[0]:top[0] + words]
            top[0] += words + (-words) % 8
            assert top[0] <= TOTAL, top[0]
            if dt != F32:
                a = a.bitcast(dt)
            if len(shape) == 3:
                a = a.rearrange("p (a b) -> p a b", a=shape[1])
            if len(shape) == 4:
                a = a.rearrange("p (a b c) -> p a b c", a=shape[1], b=shape[2])
            return a

        def bc(a, dim, n):
            v = a.unsqueeze(dim)
            sh = list(v.shape)
            sh[dim] = n
            return v.broadcast_to(sh)

        slots = [ctx.enter_context(nc.psum_tensor(f"ps{i}", [128, 1024], F32))[:, :] for i in range(4)]
        PS = Ring(slots)
        PO = Ring([slots[3][:, 0:512], slots[3][:, 512:1024]])

        def split_psum(n):
            PS.bufs, PS.k, PS.freed = slots[:n], 0, [()] * n
            PO.k, PO.freed = 0, [()] * 2

        new_phase()

        XR = sb([128, 2 * NB, 128])
        XX = sb([128, 2 * NB, 128])
        ident = sb([128, 128])
        identb = sb([128, 128], BF16)
        mask = sb([128, 2, 128], BF16)
        maskd = sb([128, 2, 384], BF16)
        mhalf = sb([128, 2])
        mhalf32 = sb([128, 32])
        ones1 = sb([1, 128])
        t_mh = pool.op(lambda e: e.memset(mhalf, -0.5))
        t_mh = pool.op(lambda e: e.memset(mhalf32, -0.5))
        base = top[0]

        t_x = []
        for b0 in range(0, NB, 4):
            t_x.append(dma(XR[:, 2 * b0:2 * b0 + 8, :],
                           d["x"][b0:b0 + 4].rearrange("b (t p) f -> p (b t) f", p=128)))
        t_id = dma(ident, d["kident"])
        stage_m = sb([128, 2, 128])
        stage_d = sb([128, 2, 384])
        t1 = dma(stage_m, d["kmask"])
        t2 = dma(stage_d, d["kmaskd"])
        t_idb = pool.op(lambda e: e.tensor_copy(identb, ident), t_id)
        t_mask = pool.op(lambda e: e.tensor_copy(mask, stage_m), t1)
        t_mask = pool.op(lambda e: e.tensor_copy(maskd, stage_d), t2)

        def layer_norm(src, dst, st, *tokens):
            n = len(src)
            for t in range(n):
                tk = dve.op(lambda e: e.bn_stats(st["bn"][:, t, :], src[t]), *(tokens if t == 0 else ()))
            for t in range(n):
                tk = dve.op(lambda e: e.bn_aggr(st["mv"][:, t, :], st["bn"][:, t, :]), *((tk,) if t == 0 else ()))
            tk = pool.op(lambda e: e.tensor_scalar(st["rs"][:, 0:n], st["mv"][:, 0:n, 1], EPS, None, ALU.add), tk)
            tk = pool.op(lambda e: e.tensor_tensor(st["rs"][:, 0:n], st["rs"][:, 0:n], mhalf[:, 0:n], ALU.pow), tk, t_mh)
            yield
            for t in range(n):
                last = dve.op(lambda e: e.tensor_scalar(dst[t], src[t], st["mv"][:, t, 0:1], st["rs"][:, t:t + 1],
                                                        ALU.subtract, ALU.mult), *((tk,) if t == 0 else ()))
            return last

        def stats():
            return {"bn": sb([128, 2, 6]), "mv": sb([128, 2, 2]), "rs": sb([128, 2])}

        def turn(src, *tokens):
            i, p, freed = PS.take()
            for t, s in enumerate(src):
                f = lambda e, t=t, s=s: e.transpose(p[:, 128 * t:128 * t + 128], s, ident)
                w = (*tokens, *freed, t_id) if t == 0 else ()
                if t == len(src) - 1:
                    tk = pe.op(f, *w)
                else:
                    pe.quiet(f, *w)
            return i, p, tk

        def drive(units, width, every=1):
            live, todo, k = [], list(units), 0
            while live or todo:
                if todo and len(live) < width and k >= every:
                    live.append(todo.pop(0))
                    k = 0
                k += 1
                if not live:
                    continue
                for g in list(live):
                    try:
                        next(g)
                    except StopIteration:
                        live.remove(g)

        def add_ln_residual(y, b, st, *tokens):
            tk = yield from layer_norm([y[:, 0, :], y[:, 1, :]], [y[:, 0, :], y[:, 1, :]], st, *tokens)
            tk = dve.op(lambda e: e.tensor_tensor(XR[:, 2 * b:2 * b + 2, :], XR[:, 2 * b:2 * b + 2, :], y, ALU.add), tk)
            return tk

        NS = 3

        def attention_buffers():
            bufs = []
            for _ in range(NS):
                B = {"st": stats(), "h": sb([128, 2, 128]), "hT": sb([128, 256]), "qkv": sb([128, 2, 256]),
                     "va": sb([128, 2, 16, 32]), "OT": sb([128, 2, 512]),
                     "QS": sb([128, 2, 1024], BF16), "KS": sb([128, 2, 1024], BF16),
                     "QT": sb([128, 8, 256], BF16), "KT": sb([128, 8, 256], BF16),
                     "m": sb([128, 2, 16]), "mr": sb([128, 2, 16]), "ms": sb([128, 2, 128], BF16),
                     "mT": sb([128, 256], BF16), "PT": Ring([sb([128, 3, 2, 128]) for _ in range(3)]), "rc": sb([128, 2, 16]),
                     "y": sb([128, 2, 128])}
                B["ctx"], B["cT"] = B["y"], B["hT"]
                B["r"] = B["OT"][:, 0, :].rearrange("p (t f) -> p t f", t=2)
                b12 = B["OT"][:, 1, :].bitcast(BF16).rearrange("p (s t f) -> p s t f", s=2, t=2)
                B["b1"], B["b2"] = b12[:, 0, :, :], b12[:, 1, :, :]
                bufs.append(B)
            return bufs

        def prepare_attention(bufs):
            for B in bufs:
                t = dve.op(lambda e, B=B: e.memset(B["va"], 0.0))
                B["va_ready"] = dve.op(lambda e, B=B: e.memset(B["va"][:, :, :, 8:9], 1.0), t)
                pool.op(lambda e, B=B: e.memset(B["QS"], 0.0))
                pool.op(lambda e, B=B: e.memset(B["ms"], 0.0))
                B["ready"] = pool.op(lambda e, B=B: e.memset(B["KS"], 0.0))

        def attention(B, W, bias, sel, t_w, *t_h):
            PT = B["PT"]
            """B["hT"] -> B["ctx"] (token-major, normalised), stage by stage; yields between stages."""
            for t in range(2):
                i, p, freed = PS.take()
                tq = pe.op(lambda e, t=t: e.matmul(p[:, 0:384], B["hT"][:, 128 * t:128 * t + 128], W, start=True, stop=True),
                           *freed, *(t_h if t == 0 else ()), *t_w)
                if bias is not None:
                    tv = dve.op(lambda e, t=t: e.tensor_tensor(B["qkv"][:, t, :], p[:, 0:256], bias[:, 0:256], ALU.add), tq)
                    tv2 = dve.op(lambda e, t=t: e.tensor_tensor(B["va"][:, t, :, 0:8], p[:, 256:384].rearrange("p (h d) -> p h d", d=8),
                                                               bias[:, 256:384].rearrange("p (h d) -> p h d", d=8), ALU.add))
                else:
                    tv = dve.op(lambda e, t=t: e.tensor_copy(B["qkv"][:, t, :], p[:, 0:256]), tq)
                    tv2 = dve.op(lambda e, t=t: e.tensor_copy(B["va"][:, t, :, 0:8],
                                                              p[:, 256:384].rearrange("p (h d) -> p h d", d=8)))
                PS.free(i, tv2)
            t = act.op(lambda e: e.activation(B["b1"], B["qkv"], ACT.Copy), tv)
            t = dve.op(lambda e: e.tensor_tensor(B["r"], B["qkv"], B["b1"], ALU.subtract), t)
            t = act.op(lambda e: e.activation(B["b2"], B["r"], ACT.Copy), t)
            t = dve.op(lambda e: e.tensor_tensor(B["r"], B["r"], B["b2"], ALU.subtract), t)
            yield
            q = [B[n][:, :, 0:128].rearrange("p t (h e) -> p t h e", e=8) for n in ("b1", "b2", "r")]
            k = [B[n][:, :, 128:256].rearrange("p t (h e) -> p t h e", e=8) for n in ("b1", "b2", "r")]
            tb = []
            for S, parts, order in (("QS", q, (0, 0, 1, 1, 0, 2)), ("KS", k, (0, 1, 0, 1, 2, 0))):
                for tile in range(2):
                    s = B[S][:, tile, :].rearrange("p (h g e) -> p h g e", h=16, g=8)
                    for g, o in enumerate(order):
                        eng = pool if g % 2 else dve
                        tb.append(eng.op(lambda e, s=s, g=g, o=o, parts=parts, tile=tile:
                                         e.tensor_copy(s[:, :, g, :], parts[o][:, tile, :, :]), t, B["ready"]))
            tb = [dve.last(), pool.last()]
            yield
            for S, T in (("QS", "QT"), ("KS", "KT")):
                for tile in range(2):
                    i, p, freed = PS.take()
                    pb = p.bitcast(BF16)
                    for c in range(8):
                        f = lambda e, c=c, S=S, tile=tile, pb=pb: e.transpose(
                            pb[:, 128 * c:128 * c + 128], B[S][:, tile, 128 * c:128 * c + 128], identb)
                        w = (*freed, *tb, t_idb) if c == 0 else ()
                        if c == 7:
                            tk = pe.op(f, *w)
                        else:
                            pe.quiet(f, *w)
                    g = lambda e, T=T, tile=tile, pb=pb: e.tensor_copy(
                        B[T][:, :, 128 * tile:128 * tile + 128], pb[:, 0:1024].rearrange("p (c q) -> p c q", c=8))
                    if tile == 0:
                        te = act.op(lambda e, T=T, tile=tile, pb=pb: e.activation(
                            B[T][:, :, 128 * tile:128 * tile + 128], pb[:, 0:1024].rearrange("p (c q) -> p c q", c=8),
                            ACT.Copy), tk)
                    else:
                        te = dve.op(g, tk)
                    PS.free(i, te)
            t_qk = (act.last(), dve.last())
            yield

            def row(h):
                return slice(64 * (h % 2), 64 * (h % 2) + 48)

            for tile in range(2):
                nk = 128 * (tile + 1)
                per = 1024 // nk
                for g in range(16 // per):
                    i, p, freed = PS.take()
                    for j in range(per):
                        h = g * per + j
                        o = p[:, 512 * (j % 2) + (j // 2) * nk:512 * (j % 2) + (j // 2 + 1) * nk]
                        w = (*freed, *t_qk, t_mask) if j == 0 else ()
                        pe.quiet(lambda e, o=o, nk=nk, h=h, tile=tile: e.matmul(
                            o, B["QT"][row(h), h // 2, 128 * tile:128 * tile + 128],
                            B["KT"][row(h), h // 2, 0:nk], start=True, stop=False, skip_group_check=True), *w)
                        tk = pe.op(lambda e, o=o, nk=nk: e.matmul(
                            o[:, nk - 128:nk], identb, mask[:, 0, :], start=False, stop=True, skip_group_check=True))
                    td = dve.op(lambda e, p=p, g=g, per=per, nk=nk, tile=tile: e.tensor_reduce(
                        B["m"][:, tile, g * per:(g + 1) * per].rearrange("p (j u) -> p u j", u=2),
                        p.rearrange("p (u j k) -> p u j k", u=2, k=nk), AX.X, ALU.max), tk)
                    PS.free(i, td)
                    if g % 2:
                        yield
            ms = [B["ms"].rearrange("p t (u r) -> p t u r", u=2)[:, :, :, 16 * j:16 * j + 16] for j in range(3)]
            t = dve.op(lambda e: e.tensor_copy(ms[0], bc(B["m"], 2, 2)), td, B["ready"])
            t = dve.op(lambda e: e.tensor_tensor(B["mr"], B["m"], ms[0][:, :, 0, :], ALU.subtract), t)
            t = dve.op(lambda e: e.tensor_copy(ms[1], bc(B["mr"], 2, 2)), t)
            t = dve.op(lambda e: e.tensor_tensor(B["mr"], B["mr"], ms[1][:, :, 0, :], ALU.subtract), t)
            t = dve.op(lambda e: e.tensor_copy(ms[2], bc(B["mr"], 2, 2)), t)
            i, p, freed = PS.take()
            pb = p.bitcast(BF16)
            pe.quiet(lambda e, pb=pb: e.transpose(pb[:, 0:128], B["ms"][:, 0, :], identb), t, *freed)
            tk = pe.op(lambda e, pb=pb: e.transpose(pb[:, 128:256], B["ms"][:, 1, :], identb))
            t_m = act.op(lambda e, pb=pb: e.activation(B["mT"], pb[:, 0:256], ACT.Copy), tk)
            PS.free(i, t_m)
            yield
            lag, waiting = 2, []
            ot = {}

            def product():
                g, P, tp, ip = waiting.pop(0)
                half = g // 4
                if g % 4 == 0:
                    ot["i"], ot["p"], ot["freed"] = PO.take()
                o = ot["p"]
                for kt, st in ((0, True), (1, False)):
                    for j in range(2):
                        h = 2 * g + j
                        c = 256 * ((h // 4) % 2)
                        q0 = 128 * kt
                        rhs = P[:, 1, j, :] if kt else P[:, 0:3:2, j, :]
                        f = lambda e: e.matmul(o[32 * (h % 4):32 * (h % 4) + 32, c + q0:c + 256], B["va"][:, kt, h, :],
                                               rhs, start=st, stop=not st, skip_group_check=True)
                        w = (tp, *ot["freed"]) if kt == j == 0 else ()
                        if kt and j:
                            tk = pe.op(f, *w)
                        else:
                            pe.quiet(f, *w)
                PT.free(ip, tk)
                if g % 4 == 3:
                    t = act.op(lambda e: e.activation(B["OT"][:, half, :], o, ACT.Copy), tk)
                    PO.free(ot["i"], t)
                    ot["t"] = t

            for g in range(8):
                i, p, freed = PS.take()
                w = (*freed, t_m)
                for kt, q0 in ((0, 0), (1, 128)):
                    for what in range(2):
                        for j in range(2):
                            h = 2 * g + j
                            o = p[:, 512 * j:512 * j + 512].rearrange("p (c q) -> p c q", c=4)
                            o = o[:, 1, :] if kt else o[:, 0:3:2, :]
                            lhs = sel[row(h), h, :] if what else B["KT"][row(h), h // 2, 128 * kt:128 * kt + 128]
                            rhs = B["mT"][row(h), q0:256] if what else B["QT"][row(h), h // 2, q0:256]
                            pe.quiet(lambda e: e.matmul(o, lhs, rhs, start=(kt == what == 0), stop=False,
                                                        skip_group_check=True), *w)
                            w = ()
                for j in range(2):
                    tk = pe.op(lambda e: e.matmul(p[:, 512 * j:512 * j + 256], identb, bc(mask[:, 1, :], 1, 2),
                                                  start=False, stop=True, skip_group_check=True))
                ip, P, pfreed = PT.take()
                te = act.op(lambda e: e.activation(P, p.rearrange("p (j c q) -> p c j q", j=2, c=4)[:, 0:3, :, :],
                                                   ACT.Exp), tk, *pfreed)
                PS.free(i, te)
                waiting.append((g, P, te, ip))
                if len(waiting) > lag:
                    product()
                yield
            while waiting:
                product()
            yield
            i, p, freed = PS.take()
            for tile in range(2):
                for c in range(4):
                    tk = pe.op(lambda e: e.transpose(
                        p[:, 512 * tile + 128 * c:512 * tile + 128 * c + 128],
                        B["OT"][:, c // 2, 256 * (c % 2) + 128 * tile:256 * (c % 2) + 128 * tile + 128], ident),
                        *((*freed, ot["t"]) if tile == c == 0 else ()))
            O = p.rearrange("p (t h e) -> p t h e", t=2, h=16)
            t = dve.op(lambda e: e.reciprocal(B["rc"], O[:, :, :, 8]), tk)
            for tile in range(2):
                t = dve.op(lambda e: e.tensor_tensor(
                    B["ctx"][:, tile, :].rearrange("p (h e) -> p h e", e=8), O[:, tile, :, 0:8],
                    bc(B["rc"][:, tile, :], 2, 8), ALU.mult), t if tile == 0 else None)
            PS.free(i, t)
            B["t_ctx"] = t

        def phase_a():
            fence()
            split_psum(3)
            top[0] = base
            new_phase()
            raw_ut = sb([48, 48, 128])
            raw_v = sb([48, 48, 8])
            oU, oV = sb([96, 128]), sb([96, 128])
            f1U, f1V = sb([64, 128]), sb([64, 512])
            f2U, f2V = sb([64, 512]), sb([64, 128])
            W, bias = sb([128, 384]), sb([128, 384])
            Wo, bo = sb([128, 128]), sb([128, 128])
            W1, b1 = sb([128, 512]), sb([128, 4])
            W2, b2 = sb([128, 4, 128]), sb([128, 128])
            sel32 = sb([128, 1024])
            sel = sel32.bitcast(BF16).rearrange("p (h k) -> p h k", h=16)
            ln = sb([128, 4])
            tw = [dma(x, d[n]) for x, n in ((raw_ut, "aUT"), (raw_v, "aV"), (oU, "aoUT"), (oV, "aoV"), (f1U, "af1UT"),
                                            (f1V, "af1V"), (f2U, "af2UT"), (f2V, "af2V"), (sel32, "ksel"), (b1, "af1b"),
                                            (ln, "aln"))]
            tb = dma(bias, d["ab"].partition_broadcast(128) if 0 else d["ab"].broadcast_to([128, 384]))
            tbo = dma(bo, d["aob"].broadcast_to([128, 128]))
            tb2 = dma(b2, d["af2b"].broadcast_to([128, 128]))
            s8 = float(np.float32(1.0) / np.sqrt(np.float32(8.0)))
            t_sel = tw[8]
            i, p, freed = PS.take()
            for j in range(48):
                f = lambda e, j=j: e.matmul(p[:, 8 * j:8 * j + 8], raw_ut[:, j, :], raw_v[:, j, :], start=True, stop=True,
                                            skip_group_check=True)
                if j == 47:
                    tk = pe.op(f)
                else:
                    pe.quiet(f, *((*freed, tw[0], tw[1]) if j == 0 else ()))
            act.op(lambda e: e.activation(W[:, 0:128], p[:, 0:128], ACT.Copy, scale=s8), tk)
            t_W = act.op(lambda e: e.activation(W[:, 128:384], p[:, 128:384], ACT.Copy))
            PS.free(i, t_W)
            t_b = act.op(lambda e: e.activation(bias[:, 0:128], bias[:, 0:128], ACT.Copy, scale=s8), tb)
            i, p, freed = PS.take()
            pe.quiet(lambda e: e.matmul(p[:, 0:128], oU, oV, start=True, stop=True), *freed, tw[2], tw[3])
            tk = pe.op(lambda e: e.matmul(p[:, 512:1024], f1U, f1V, start=True, stop=True), tw[4], tw[5])
            act.op(lambda e: e.activation(Wo, p[:, 0:128], ACT.Copy), tk)
            t_W1 = act.op(lambda e: e.activation(W1, p[:, 512:1024], ACT.Copy))
            PS.free(i, t_W1)
            i, p, freed = PS.take()
            for c in range(4):
                tk = pe.op(lambda e, c=c, p=p: e.matmul(p[:, 128 * c:128 * c + 128], f2U[:, 128 * c:128 * c + 128], f2V,
                                                        start=True, stop=True, skip_group_check=True),
                           *freed, tw[6], tw[7])
            t_W2 = act.op(lambda e: e.activation(W2, p[:, 0:512].rearrange("p (c n) -> p c n", c=4), ACT.Copy), tk)
            PS.free(i, t_W2)

            mark = top[0]
            bufs = attention_buffers()
            prepare_attention(bufs)
            done = {}

            def unit(b):
                B = bufs[b % NS]
                prior = done.get(b - NS, ())
                X = [XR[:, 2 * b, :], XR[:, 2 * b + 1, :]]
                h, y = B["h"], B["y"]
                t = yield from layer_norm(X, [h[:, 0, :], h[:, 1, :]], B["st"], t_x[b // 4], *prior)
                yield
                t = yield from layer_norm([h[:, 0, :], h[:, 1, :]], [y[:, 0, :], y[:, 1, :]], B["st"], t)
                yield
                i, p, tk = turn([y[:, 0, :], y[:, 1, :]], t)
                t_h = act.op(lambda e: e.activation(B["hT"], p[:, 0:256], ACT.Identity, bias=ln[:, 1:2], scale=ln[:, 0:1]),
                             tk, tw[10])
                PS.free(i, t_h)
                yield
                yield from attention(B, W, bias, sel, (t_W, t_b, t_sel), t_h)
                yield
                i, p, tk = turn([B["ctx"][:, 0, :], B["ctx"][:, 1, :]], B["t_ctx"])
                t = act.op(lambda e: e.activation(B["cT"], p[:, 0:256], ACT.Copy), tk)
                PS.free(i, t)
                i, p, freed = PS.take()
                pe.quiet(lambda e: e.matmul(p[:, 0:128], B["cT"][:, 0:128], Wo, start=True, stop=True,
                                            skip_group_check=True), t, *freed)
                tk = pe.op(lambda e: e.matmul(p[:, 128:256], B["cT"][:, 128:256], Wo, start=True, stop=True,
                                              skip_group_check=True))
                th = pool.op(lambda e: e.tensor_tensor(h, h, bc(bo, 1, 2), ALU.add), tbo, B["t_ctx"])
                t = dve.op(lambda e: e.tensor_tensor(XX[:, 2 * b:2 * b + 2, :], h,
                                                     p[:, 0:256].rearrange("p (t f) -> p t f", t=2), ALU.add), tk, th)
                PS.free(i, t)
                done[b] = (t,)

            drive([unit(b) for b in range(NB)], NS, 6)
            fence()
            top[0] = mark
            new_phase()
            mb = [{"st": stats(), "z": sb([128, 2, 128]), "zT": sb([128, 256]), "g": sb([128, 4, 256])} for _ in range(5)]
            mdone = {}

            def mlp(b):
                M = mb[b % 5]
                H = XX[:, 2 * b:2 * b + 2, :]
                z = M["z"]
                t = yield from layer_norm([H[:, 0, :], H[:, 1, :]], [z[:, 0, :], z[:, 1, :]], M["st"], *mdone.get(b - 5, ()))
                yield
                i, p, tk = turn([z[:, 0, :], z[:, 1, :]], t)
                t = act.op(lambda e: e.activation(M["zT"], p[:, 0:256], ACT.Identity, bias=ln[:, 3:4], scale=ln[:, 2:3]), tk)
                PS.free(i, t)
                i, p, freed = PS.take()
                for c in range(4):
                    tk = pe.op(lambda e, c=c, p=p: e.matmul(p[:, 256 * c:256 * c + 256], W1[:, 128 * c:128 * c + 128],
                                                            M["zT"], start=True, stop=True, skip_group_check=True),
                               t, *freed, t_W1)
                for c in range(4):
                    t = act.op(lambda e, c=c, p=p: e.activation(M["g"][:, c, :], p[:, 256 * c:256 * c + 256],
                                                                ACT.Gelu_apprx_tanh, bias=b1[:, c:c + 1]), tk, tw[9])
                PS.free(i, t)
                yield
                i, p, freed = PS.take()
                for tile in range(2):
                    for c in range(4):
                        tk = pe.op(lambda e, c=c, tile=tile, p=p: e.matmul(
                            p[:, 128 * tile:128 * tile + 128], M["g"][:, c, 128 * tile:128 * tile + 128], W2[:, c, :],
                            start=(c == 0), stop=(c == 3), skip_group_check=True), t, *freed, t_W2)
                t = dve.op(lambda e: e.tensor_tensor(z, H, p[:, 0:256].rearrange("p (t f) -> p t f", t=2), ALU.add), tk)
                PS.free(i, t)
                t = dve.op(lambda e: e.tensor_tensor(z, z, bc(b2, 1, 2), ALU.add), t, tb2)
                yield
                t = yield from add_ln_residual(z, b, M["st"], t)
                mdone[b] = (t,)

            drive([mlp(b) for b in range(NB)], 5, 1)

        def phase_c():
            fence()
            split_psum(3)
            top[0] = base
            new_phase()
            W, Wo, bo = sb([128, 384]), sb([128, 128]), sb([128, 128])
            sel32 = sb([128, 1024])
            sel = sel32.bitcast(BF16).rearrange("p (h k) -> p h k", h=16)
            t_W, t_Wo, t_sel = dma(W, d["cW"]), dma(Wo, d["cWo"]), dma(sel32, d["ksel"])
            tbo = dma(bo, d["cbo"].broadcast_to([128, 128]))
            s8 = float(np.float32(1.0) / np.sqrt(np.float32(8.0)))
            t_Ws = act.op(lambda e: e.activation(W[:, 0:128], W[:, 0:128], ACT.Copy, scale=s8), t_W)
            bufs = attention_buffers()
            prepare_attention(bufs)
            done = {}

            def unit(b):
                B = bufs[b % NS]
                X = [XR[:, 2 * b, :], XR[:, 2 * b + 1, :]]
                h, y = B["h"], B["y"]
                t = yield from layer_norm(X, [h[:, 0, :], h[:, 1, :]], B["st"], t_x[b // 4], *done.get(b - NS, ()))
                yield
                i, p, tk = turn([h[:, 0, :], h[:, 1, :]], t)
                t_h = act.op(lambda e: e.activation(B["hT"], p[:, 0:256], ACT.Copy), tk)
                PS.free(i, t_h)
                yield
                yield from attention(B, W, None, sel, (t_Ws, t_sel), t_h)
                yield
                i, p, tk = turn([B["ctx"][:, 0, :], B["ctx"][:, 1, :]], B["t_ctx"])
                t = act.op(lambda e: e.activation(B["cT"], p[:, 0:256], ACT.Copy), tk)
                PS.free(i, t)
                i, p, freed = PS.take()
                pe.quiet(lambda e: e.matmul(p[:, 0:128], B["cT"][:, 0:128], Wo, start=True, stop=True,
                                            skip_group_check=True), t, t_Wo, *freed)
                tk = pe.op(lambda e: e.matmul(p[:, 128:256], B["cT"][:, 128:256], Wo, start=True, stop=True,
                                              skip_group_check=True))
                t = dve.op(lambda e: e.tensor_tensor(y, p[:, 0:256].rearrange("p (t f) -> p t f", t=2), bc(bo, 1, 2),
                                                     ALU.add), tk, tbo)
                PS.free(i, t)
                yield
                t = yield from add_ln_residual(y, b, B["st"], t)
                done[b] = (t,)

            drive([unit(b) for b in range(NB)], NS, 6)

        def phase_b():
            fence()
            split_psum(4)
            top[0] = base
            new_phase()
            wq, kT = sb([64, 8, 128]), sb([64, 8, 64])
            Wsim, Wdn, Wue, Wup = sb([128, 512]), sb([128, 4, 128]), sb([128, 4, 128]), sb([128, 512])
            Wd = sb([128, 512])
            io, iob = sb([128, 64, 8]), sb([128, 64, 8], BF16)
            x8, w8, w8b = sb([128, 8, 8]), sb([128, 8]), sb([128, 8], BF16)
            tw = {n: dma(a, d[n]) for a, n in ((wq, "bWq"), (kT, "bkT"), (Wdn, "bdn"), (Wue, "bue"), (Wup, "bup"),
                                               (Wd, "bdT"), (io, "kiota"), (x8, "kx8"), (w8, "kw8"))}
            pool.op(lambda e: e.tensor_copy(iob, io), tw["kiota"])
            t_io = pool.op(lambda e: e.tensor_copy(w8b, w8), tw["kw8"])
            i, p, freed = PS.take()
            for g in range(8):
                tk = pe.op(lambda e, g=g: e.matmul(p[:, 64 * g:64 * g + 64], wq[:, g, :], kT[:, g, :], start=True,
                                                   stop=True, skip_group_check=True), *freed, tw["bWq"], tw["bkT"])
            t_sim = act.op(lambda e: e.activation(Wsim, p[:, 0:512], ACT.Copy), tk)
            PS.free(i, t_sim)
            ub = [{"st": stats(), "h": sb([128, 2, 128]), "hT": sb([128, 256]), "up": sb([128, 4, 256]),
                   "AT": sb([128, 4, 128]), "y": sb([128, 2, 128])} for _ in range(2)]
            tb_ = [{"SP": sb([128, 1024]), "v8": sb([128, 8, 8]), "ix": sb([128, 8, 8], U32), "ixf": sb([128, 8, 8]),
                    "iyb": sb([128, 4, 8], BF16), "C": sb([128, 4, 64]), "C2": sb([128, 4, 64]), "c8": sb([128, 4, 8]),
                    "M": sb([128, 4, 64]), "n": sb([128, 4, 8]), "E": sb([128, 576]), "Z": sb([128, 4]),
                    "rz": sb([128, 4]), "big": sb([128, 4, 8]), "oh": sb([128, 4, 64]), "thr": sb([128, 4, 8]),
                    "eq": sb([128, 256, 8], BF16), "R": sb([128, 4, 64]), "cs": sb([128, 1]),
                    "G": sb([128, 4, 8, 64]), "G2": sb([128, 4, 8, 64])} for _ in range(2)]
            done = {}
            tdone = [(), ()]

            def unit(b):
                U = ub[b % 2]
                h, hT = U["h"], U["hT"]
                t = yield from layer_norm([XR[:, 2 * b, :], XR[:, 2 * b + 1, :]], [h[:, 0, :], h[:, 1, :]], U["st"], t_x[b // 4],
                               *done.get(b - 2, ()))
                i, p, tk = turn([h[:, 0, :], h[:, 1, :]], t)
                t_h = act.op(lambda e: e.activation(hT, p[:, 0:256], ACT.Copy), tk)
                PS.free(i, t_h)
                yield
                for tile in range(2):
                    T = tb_[tile]
                    SP, v8, ix, ixf, C, C2, c8, M, E = (T[n] for n in ("SP", "v8", "ix", "ixf", "C", "C2", "c8", "M", "E"))
                    SIM = SP[:, 0:512].rearrange("p (g k) -> p g k", g=8)
                    PRJ = SP[:, 512:1024].rearrange("p (x y) -> p x y", x=8)
                    i, p, freed = PS.take()
                    pe.quiet(lambda e, p=p, tile=tile: e.matmul(p[:, 0:512], hT[:, 128 * tile:128 * tile + 128], Wsim,
                                                                start=True, stop=True), t_h, t_sim, *freed)
                    tk = pe.op(lambda e, p=p, tile=tile: e.matmul(p[:, 512:1024], hT[:, 128 * tile:128 * tile + 128], Wd,
                                                                  start=True, stop=True), tw["bdT"])
                    ts = act.op(lambda e, p=p, SP=SP: e.activation(SP, p, ACT.Copy), tk, *tdone[tile])
                    PS.free(i, ts)
                    for g in range(8):
                        t = dve.op(lambda e, g=g, v8=v8, SIM=SIM: e.max(v8[:, g, :], SIM[:, g, :]), ts, *tdone[tile])
                    for g in range(8):
                        t = dve.op(lambda e, g=g, v8=v8, SIM=SIM, ix=ix: e.max_index(ix[:, g, :], v8[:, g, :], SIM[:, g, :]), t)
                    ti = dve.op(lambda e, ix=ix, ixf=ixf: e.tensor_copy(ixf, ix), t)
                    C4 = C.rearrange("p h (i j) -> p h i j", i=8)
                    tc = dve.op(lambda e, C4=C4, v8=v8: e.tensor_tensor(
                        C4, bc(v8[:, 0:4, :], 3, 8), bc(v8[:, 4:8, :], 2, 8), ALU.add))
                    for hh in range(4):
                        t = dve.op(lambda e, hh=hh, c8=c8, C=C: e.max(c8[:, hh, :], C[:, hh, :]), tc)
                    for hh in range(4):
                        t = dve.op(lambda e, hh=hh, c8=c8, C=C, C2=C2: e.match_replace(
                            C2[:, hh, :], c8[:, hh, :], C[:, hh, :], -3.0e38), t)
                    ey = E[:, 0:256].rearrange("p (h y) -> p h y", h=4)
                    ex = E[:, 256:288].rearrange("p (h x) -> p h x", h=4)
                    e8 = E[:, 288:320].rearrange("p (h x) -> p h x", h=4)
                    eC = E[:, 320:576].rearrange("p (h x) -> p h x", h=4)
                    dve.op(lambda e, ey=ey, SIM=SIM, v8=v8: e.tensor_tensor(ey, SIM[:, 4:8, :],
                           v8[:, 4:8, 0:1].broadcast_to([128, 4, 64]), ALU.subtract))
                    dve.op(lambda e, ex=ex, SIM=SIM, v8=v8: e.tensor_tensor(ex, SIM[:, 0:4, 0:8],
                           v8[:, 0:4, 0:1].broadcast_to([128, 4, 8]), ALU.subtract))
                    dve.op(lambda e, e8=e8, c8=c8: e.tensor_tensor(e8, c8, c8[:, :, 0:1].broadcast_to([128, 4, 8]),
                                                                  ALU.subtract))
                    t = dve.op(lambda e, eC=eC, C=C, c8=c8: e.tensor_tensor(
                        eC, C, c8[:, :, 0:1].broadcast_to([128, 4, 64]), ALU.subtract))
                    te = act.op(lambda e, E=E: e.activation(E, E, ACT.Exp), t)
                    yield
                    M_, n_, oh, thr, big, Z, rz = (T[n] for n in ("M", "n", "oh", "thr", "big", "Z", "rz"))
                    eq, R, iyb = T["eq"], T["R"], T["iyb"]
                    t = dve.op(lambda e, iyb=iyb, ixf=ixf: e.tensor_copy(iyb, ixf[:, 4:8, :]), ti)
                    for hh in range(4):
                        t_eq = dve.op(lambda e, hh=hh, eq=eq, iyb=iyb: e.tensor_tensor(
                            eq[:, 64 * hh:64 * hh + 64, :], iob, bc(iyb[:, hh, :], 1, 64), ALU.is_equal), t, t_io)
                    t_w8 = pool.op(lambda e, eq=eq: e.tensor_tensor(eq, eq, bc(w8b, 1, 256), ALU.mult), t_eq)
                    G, G2 = T["G"], T["G2"]
                    t = dve.op(lambda e, M_=M_, C=C, C2=C2: e.tensor_tensor(M_, C, C2, ALU.not_equal))
                    t = dve.op(lambda e, M_=M_, n_=n_: e.tensor_reduce(
                        n_, M_.rearrange("p h (i j) -> p h i j", i=8), AX.X, ALU.add), t)
                    oh4 = oh.rearrange("p h (x i) -> p h x i", x=8)
                    t = dve.op(lambda e, oh4=oh4, ixf=ixf: e.tensor_tensor(
                        oh4, bc(x8, 1, 4), bc(ixf[:, 0:4, :], 2, 8), ALU.is_equal), tw["kx8"])
                    t = dve.op(lambda e, oh4=oh4, n_=n_: e.tensor_tensor(oh4, oh4, bc(n_, 2, 8), ALU.mult), t)
                    t = dve.op(lambda e, thr=thr, oh4=oh4: e.tensor_reduce(thr, oh4, AX.X, ALU.add), t)
                    t_thr = dve.op(lambda e, thr=thr: e.tensor_scalar(thr, thr, -1.0, 8.0, ALU.mult, ALU.add), t)
                    t = dve.op(lambda e, Z=Z, e8=e8: e.tensor_reduce(Z, e8, AX.X, ALU.add), te)
                    t = dve.op(lambda e, Z=Z, rz=rz: e.reciprocal(rz, Z), t)
                    t_ex = dve.op(lambda e, ex=ex, rz=rz: e.tensor_tensor(ex, ex, bc(rz, 2, 8), ALU.mult), t)
                    dve.op(lambda e, big=big, ixf=ixf: e.tensor_scalar(big, ixf[:, 0:4, :], 7.5, None, ALU.is_gt))
                    t = dve.op(lambda e, M_=M_, eC=eC: e.tensor_tensor(M_, M_, eC, ALU.mult))
                    t = dve.op(lambda e, big=big, rz=rz: e.tensor_tensor(big, big, bc(rz, 2, 8), ALU.mult), t)
                    t = dve.op(lambda e, big=big, SP=SP: e.tensor_scalar(big, big, SP[:, 1023:1024], None, ALU.mult), t)
                    t_c = dve.op(lambda e, M_=M_, big=big: e.tensor_tensor(
                        M_.rearrange("p h (i j) -> p h i j", i=8), M_.rearrange("p h (i j) -> p h i j", i=8),
                        bc(big, 3, 8), ALU.mult), t)
                    for hh in range(4):
                        t_g2 = pool.op(lambda e, hh=hh, G2=G2, PRJ=PRJ, ex=ex: e.tensor_tensor(
                            G2[:, hh, :, :], PRJ, bc(ex[:, hh, :], 2, 64), ALU.mult), t_ex)
                    t = t_w8
                    t = dve.op(lambda e, eq=eq, R=R: e.tensor_reduce(R.rearrange("p h y -> p (h y)"), eq, AX.X, ALU.add), t)
                    for hh in range(4):
                        t = dve.op(lambda e, hh=hh, G=G, R=R, thr=thr: e.tensor_tensor(
                            G[:, hh, :, :], bc(R[:, hh, :], 1, 8), bc(thr[:, hh, :], 2, 64), ALU.is_gt), t)
                    for hh in range(4):
                        t = dve.op(lambda e, hh=hh, G=G, ey=ey: e.tensor_tensor(
                            G[:, hh, :, :], G[:, hh, :, :], bc(ey[:, hh, :], 1, 8), ALU.mult), t)
                    T["t_g"] = dve.op(lambda e, G=G, G2=G2: e.tensor_tensor(G, G, G2, ALU.mult), t, t_g2)
                    T["t_c"] = t_c
                    yield
                i, p, freed = PS.take()
                for c in range(4):
                    tk = pe.op(lambda e, c=c, p=p: e.matmul(p[:, 256 * c:256 * c + 256], Wup[:, 128 * c:128 * c + 128], hT,
                                                            start=True, stop=True, skip_group_check=True),
                               *freed, tw["bup"])
                t_up = act.op(lambda e, p=p: e.activation(U["up"], p.rearrange("p (c q) -> p c q", c=4), ACT.Silu), tk)
                PS.free(i, t_up)
                for tile in range(2):
                    T = tb_[tile]
                    act.op(lambda e, T=T: e.activation(T["M"], T["M"], ACT.Silu, accum_out=T["cs"]), T["t_c"])
                    t = act.op(lambda e, T=T: e.activation(T["G"], T["G"], ACT.Silu), T["t_g"])
                    g511 = T["G"].rearrange("p h x y -> p (h x y)")[:, 511:512]
                    T["t_s"] = dve.op(lambda e, T=T, g511=g511: e.tensor_tensor(g511, g511, T["cs"], ALU.add), t)
                yield
                io_, po, ofreed = PS.take()
                for tile in range(2):
                    T = tb_[tile]
                    Gf = T["G"].rearrange("p h x y -> p h (x y)")
                    i, p, freed = PS.take()
                    for c in range(4):
                        for hh in range(4):
                            tk = pe.op(lambda e, c=c, hh=hh, p=p, Gf=Gf: e.matmul(
                                p[:, 128 * c:128 * c + 128], Gf[:, hh, 128 * c:128 * c + 128], ident,
                                start=(hh == 0), stop=(hh == 3), skip_group_check=True),
                                *((*freed, T["t_s"]) if c == hh == 0 else ()))
                    tdone[tile] = (tk,)
                    ta = act.op(lambda e, p=p: e.activation(U["AT"], p[:, 0:512].rearrange("p (c q) -> p c q", c=4),
                                                            ACT.Copy), tk, *((tprev,) if tile else ()))
                    PS.free(i, ta)
                    for c in range(8):
                        lhs = U["up"][:, c, 128 * tile:128 * tile + 128] if c < 4 else U["AT"][:, c - 4, :]
                        rhs = Wdn[:, c, :] if c < 4 else Wue[:, c - 4, :]
                        tprev = pe.op(lambda e, c=c, lhs=lhs, rhs=rhs, tile=tile: e.matmul(
                            po[:, 128 * tile:128 * tile + 128], lhs, rhs, start=(c == 0), stop=(c == 7),
                            skip_group_check=True), *((ta, t_up, tw["bdn"], tw["bue"], *ofreed) if c == 0 else ()))
                t = dve.op(lambda e: e.tensor_copy(U["y"], po[:, 0:256].rearrange("p (t f) -> p t f", t=2)), tprev)
                PS.free(io_, t)
                yield
                t = yield from add_ln_residual(U["y"], b, U["st"], t)
                done[b] = (t,)

            drive([unit(b) for b in range(NB)], 1)

        def phase_d():
            fence()
            split_psum(4)
            top[0] = base
            new_phase()
            w = {"qkv": sb([128, 3072]), "wo": sb([128, 8, 128]), "w1": sb([128, 682]), "w2": sb([128, 3, 128]),
                 "b1": sb([128, 6]), "ln": sb([128, 2]), "tab": sb([128, 2, 4, 64])}
            rope = sb([128, 2, 4, 64])
            scb = sb([128, 4, 64])
            t_rope = dma(rope, d["krope"])
            st2 = [stats() for _ in range(4)]
            NXS = 4
            XS = [sb([128, 32 + 256]) for _ in range(NXS)]
            T1 = Ring([sb([128, 2048]) for _ in range(3)])
            T2 = Ring([sb([128, 2048])])
            SQ = Ring([sb([128, 2048])])
            SS = Ring([sb([128, 64]) for _ in range(3)])
            QT = Ring([sb([128, 8, 128]) for _ in range(2)])
            NKT = 3
            KT = [sb([128, 8, 160]) for _ in range(NKT)]
            V = Ring([sb([96, 2, 1024]) for _ in range(2)])
            PP = Ring([sb([128, 16, 96]) for _ in range(3)])
            PTr = Ring([sb([96, 16, 128]) for _ in range(1)])
            OT = Ring([sb([128, 8, 128]) for _ in range(2)])
            sm = Ring([sb([128, 3, 16]) for _ in range(3)])
            for s in XS:
                pool.op(lambda e: e.memset(s[:, 0:33], 0.0))
            t_z = pool.last()

            xx_tok = {}

            def start(b):
                t = yield from layer_norm([XR[:, 2 * b, :], XR[:, 2 * b + 1, :]], [XX[:, 2 * b, :], XX[:, 2 * b + 1, :]],
                                          st2[b % 4], t_x[b // 4])
                xx_tok[2 * b] = xx_tok[2 * b + 1] = t

            ready = {}
            read = {}

            def load_attn(l):
                ready["qkv"] = dma(w["qkv"], d["dWqkv"][l], *read.get("qkv", ()))
                ready["wo"] = dma(w["wo"], d["dWo"][l], *read.get("wo", ()))
                ts = dma(scb, d["dsc"][l:l + 1].broadcast_to([128, 4, 64]), *read.get("scb", ()))
                for t in range(2):
                    tt = pool.op(lambda e: e.tensor_tensor(w["tab"][:, t, :, :], rope[:, t, :, :], scb, ALU.mult),
                                 t_rope, ts, *read.get("tab", ()))
                read["scb"] = (tt,)
                ready["tab"] = tt

            def load_ffn(l):
                r = read.get("ffn", ())
                for n, src in (("w1", "dW1"), ("w2", "dW2"), ("b1", "db1"), ("ln", "dln")):
                    ready[n] = dma(w[n], d[src][l], *r)

            xsfree = [() for _ in range(NXS)]
            ktfree = [() for _ in range(NKT)]
            ktoks, kcopy, sread = {}, {}, {}
            xstok = {}

            def shifted(l, b):
                j = b % NXS
                s = XS[j]
                i, p, tk = turn([XX[:, 2 * b, :], XX[:, 2 * b + 1, :]], xx_tok[2 * b], xx_tok[2 * b + 1])
                assert xsfree[j] is not None
                act.op(lambda e: e.activation(s[0:64, 32:288], p[0:64, 0:256], ACT.Copy), tk, t_z, *xsfree[j])
                t = act.op(lambda e: e.activation(s[64:128, 33:288], p[64:128, 0:255], ACT.Copy))
                PS.free(i, t)
                xsfree[j] = None
                return t

            def attn(l, k):
                b, tile = k // 2, k % 2
                if k == 0:
                    new_phase()
                if tile == 0:
                    xstok[b] = shifted(l, b)
                yield
                t_s = xstok[b]
                s = XS[b % NXS]
                xs = s[:, 32 + 128 * tile:160 + 128 * tile]
                i1, a1, f1 = T1.take()
                i2, a2, f2 = T2.take()
                iq, sq, fq = SQ.take()
                iss, ss, fss = SS.take()
                for half in range(2):
                    i, p, freed = PS.take()
                    for c in range(2):
                        col = 1024 * half + 512 * c
                        tk = pe.op(lambda e, p=p, c=c, col=col: e.matmul(p[:, 512 * c:512 * c + 512], xs,
                                   w["qkv"][:, col:col + 512], start=True, stop=True), *freed, t_s, ready["qkv"])
                    tsq = act.op(lambda e, p=p, half=half: e.activation(sq[:, 1024 * half:1024 * half + 1024], p, ACT.Square),
                                 tk, *fq)
                    pv4 = p.rearrange("p (h u e) -> p h u e", h=16, u=2)
                    ph = p.rearrange("p (h e) -> p h e", h=16)
                    cs = w["tab"][:, tile, 2 * half, :]
                    sn = w["tab"][:, tile, 2 * half + 1, :]
                    o1 = a1[:, 1024 * half:1024 * half + 1024].rearrange("p (h e) -> p h e", h=16)
                    o2 = a2[:, 1024 * half:1024 * half + 1024].rearrange("p (h u e) -> p h u e", h=16, u=2)
                    dve.op(lambda e, ph=ph, cs=cs, o1=o1: e.tensor_tensor(o1, ph, bc(cs, 1, 16), ALU.mult),
                           tk, tsq, ready["tab"], *f1, *f2)
                    for u in range(2):
                        t2 = dve.op(lambda e, u=u, pv4=pv4, sn=sn, o2=o2: e.tensor_tensor(
                            o2[:, :, u, :], pv4[:, :, 1 - u, :], bc(sn[:, 32 * u:32 * u + 32], 1, 16), ALU.mult))
                    PS.free(i, t2)
                if k == 2 * NB - 1:
                    read["tab"] = (t2,)
                t = dve.op(lambda e: e.tensor_reduce(ss[:, 0:32], sq.rearrange("p (h e) -> p h e", h=32), AX.X, ALU.add),
                           tsq, *fss)
                SQ.free(iq, t)
                t = pool.op(lambda e: e.tensor_scalar(ss[:, 32:64], ss[:, 0:32], 1e-24, None, ALU.max), t)
                t_r = pool.op(lambda e: e.tensor_tensor(ss[:, 0:32], ss[:, 32:64], mhalf32, ALU.pow), t)
                ta = pool.op(lambda e: e.tensor_tensor(a1, a1, a2, ALU.add), t2)
                T2.free(i2, ta)
                yield
                tn = dve.op(lambda e: e.tensor_tensor(a1.rearrange("p (h e) -> p h e", h=32),
                                                      a1.rearrange("p (h e) -> p h e", h=32), bc(ss[:, 0:32], 2, 64),
                                                      ALU.mult), ta, t_r)
                SS.free(iss, tn)
                yield
                iqt, qT, fqt = QT.take()
                kj = k % NKT
                kT = KT[kj]
                assert ktfree[kj] is not None
                for half in range(2):
                    i, p, freed = PS.take()
                    for c in range(8):
                        f = lambda e, p=p, c=c, half=half: e.transpose(
                            p[:, 128 * c:128 * c + 128], a1[:, 1024 * half + 128 * c:1024 * half + 128 * c + 128], ident)
                        if c < 7:
                            pe.quiet(f, *((tn, *freed) if c == 0 else ()))
                        else:
                            tk = pe.op(f)
                    pv_ = p.rearrange("p (c q) -> p c q", c=8)
                    if half == 0:
                        tq = act.op(lambda e, pv_=pv_: e.activation(qT, pv_, ACT.Copy), tk, *fqt)
                        PS.free(i, tq)
                    else:
                        tkt = act.op(lambda e, pv_=pv_: e.activation(kT[:, :, 32:160], pv_, ACT.Copy), tk, *ktfree[kj])
                        PS.free(i, tkt)
                T1.free(i1, tk)
                if tile == 0:
                    tp = pool.op(lambda e: e.memset(kT[:, :, 0:32], 0.0), *ktfree[kj])
                else:
                    tp = pool.op(lambda e: e.tensor_copy(kT[:, :, 0:32], KT[(k - 1) % NKT][:, :, 128:160]), ktoks[k - 1], *ktfree[kj])
                    if k - 1 in sread:
                        ktfree[(k - 1) % NKT] = (*sread.pop(k - 1), tp)
                    else:
                        kcopy[k - 1] = tp
                ktfree[kj] = None
                ktoks[k] = tkt
                yield
                ip_, P, fp = PP.take()
                ism, m3, fm = sm.take()
                mx, sums, rc = m3[:, 0, :], m3[:, 1, :], m3[:, 2, :]
                for g in range(2):
                    i, p, freed = PS.take()
                    for bank in range(2):
                        pe.quiet(lambda e, p=p, bank=bank: e.matmul(
                            p[:, 512 * bank:512 * bank + 384], identb, maskd[:, 1 if tile else 0, :], start=True, stop=False,
                            skip_group_check=True), *((*freed, tq, tkt, tp, t_mask) if bank == 0 else ()))
                        for j in range(4):
                            h = 8 * g + 2 * j + bank
                            r = slice(64 * (h % 2), 64 * (h % 2) + 64)
                            for blk in range(2):
                                o = p[64 * blk:64 * blk + 64, 512 * bank + 96 * j:512 * bank + 96 * j + 96]
                                f = lambda e, o=o, r=r, h=h, blk=blk: e.matmul(
                                    o, qT[r, h // 2, 64 * blk:64 * blk + 64], kT[r, h // 2, 64 * blk:64 * blk + 96],
                                    start=False, stop=False, skip_group_check=True)
                                if bank == 1 and j == 3 and blk == 1:
                                    tk = pe.op(f)
                                else:
                                    pe.quiet(f)
                    pv_ = p.rearrange("p (a c) -> p a c", a=2)[:, :, 0:384].rearrange("p a (h k) -> p a h k", h=4)
                    Pg = P[:, 8 * g:8 * g + 8, :].rearrange("p (a h) k -> p a h k", a=2)
                    mg = mx[:, 8 * g:8 * g + 8].rearrange("p (a h) -> p a h", a=2)
                    t = dve.op(lambda e, pv_=pv_, mg=mg: e.tensor_reduce(mg, pv_, AX.X, ALU.max), tk, *fm)
                    for a in range(2):
                        t_ = dve.op(lambda e, pv_=pv_, mg=mg, Pg=Pg, a=a: e.tensor_tensor(
                            Pg[:, a, :, :], pv_[:, a, :, :], bc(mg[:, a, :], 2, 96), ALU.subtract), t, *fp)
                    t = t_
                    PS.free(i, t)
                    te = act.op(lambda e, g=g: e.activation(P[:, 8 * g:8 * g + 8, :], P[:, 8 * g:8 * g + 8, :], ACT.Exp), t)
                QT.free(iqt, tk)
                if tile == 1:
                    ktfree[kj] = (tk,)
                elif k in kcopy:
                    ktfree[kj] = (tk, kcopy.pop(k))
                else:
                    sread[k] = (tk,)
                yield
                t = dve.op(lambda e: e.tensor_reduce(sums, P, AX.X, ALU.add), te)
                t = dve.op(lambda e: e.reciprocal(rc, sums), t)
                t = pool.op(lambda e: e.tensor_tensor(P, P, bc(rc, 2, 96), ALU.mult), t)
                sm.free(ism, t)
                yield
                ipt, PT, fpt = PTr.take()
                for g in range(2):
                    i, p, freed = PS.take()
                    for j in range(8):
                        f = lambda e, p=p, j=j, g=g: e.transpose(p[0:96, 128 * j:128 * j + 128], P[:, 8 * g + j, :], ident)
                        if j < 7:
                            pe.quiet(f, *((t, *freed) if j == 0 else ()))
                        else:
                            tk = pe.op(f)
                    tpt = act.op(lambda e, p=p, g=g: e.activation(
                        PT[:, 8 * g:8 * g + 8, :], p[0:96, :].rearrange("p (h q) -> p h q", h=8), ACT.Copy), tk, *fpt)
                    PS.free(i, tpt)
                PP.free(ip_, tk)
                iv, v, fv = V.take()
                for blk in range(2):
                    i, p, freed = PS.take()
                    c0 = 128 * tile + 64 * blk
                    for c in range(2):
                        tk = pe.op(lambda e, p=p, c=c, c0=c0: e.matmul(
                            p[0:96, 512 * c:512 * c + 512], s[:, c0:c0 + 96], w["qkv"][:, 2048 + 512 * c:2560 + 512 * c],
                            start=True, stop=True), *freed, t_s)
                    tv = act.op(lambda e, p=p, blk=blk: e.activation(v[:, blk, :], p[0:96, :], ACT.Copy), tk, *fv)
                    PS.free(i, tv)
                if tile == 1:
                    xsfree[b % NXS] = (tk,)
                if k == 2 * NB - 1:
                    read["qkv"] = (tk,)
                yield
                io_, o, fo = OT.take()
                i, p, freed = PS.take()
                for h in range(16):
                    for blk in range(2):
                        f = lambda e, p=p, h=h, blk=blk: e.matmul(
                            p[64 * (h % 2):64 * (h % 2) + 64, 128 * (h // 2) + 64 * blk:128 * (h // 2) + 64 * blk + 64],
                            v[:, blk, 64 * h:64 * h + 64], PT[:, 8 * (h // 8) + 4 * (h % 2) + (h % 8) // 2, 64 * blk:64 * blk + 64], start=True, stop=True,
                            skip_group_check=True)
                        if h == 15 and blk == 1:
                            tk = pe.op(f)
                        else:
                            pe.quiet(f, *((tpt, tv, *freed) if h == blk == 0 else ()))
                V.free(iv, tk)
                PTr.free(ipt, tk)
                t = act.op(lambda e, p=p: e.activation(o, p.rearrange("p (c q) -> p c q", c=8), ACT.Copy), tk, *fo)
                PS.free(i, t)
                yield
                i, p, freed = PS.take()
                for c in range(8):
                    tk = pe.op(lambda e, p=p, c=c: e.matmul(p[:, 0:128], o[:, c, :], w["wo"][:, c, :], start=(c == 0),
                                                            stop=(c == 7)), *((t, ready["wo"], *freed) if c == 0 else ()))
                OT.free(io_, tk)
                t = dve.op(lambda e, p=p: e.tensor_tensor(XX[:, k, :], XX[:, k, :], p[:, 0:128], ALU.add), tk)
                PS.free(i, t)
                xx_tok[k] = t
                if k == 2 * NB - 1:
                    read["wo"] = (tk,)
                    if l + 1 < run["depth"]:
                        load_attn(l + 1)

            fst = [stats() for _ in range(3)]

            def ffn(l, b):
                iF, buf, fr = T1.take()
                F = {"st": fst[b % 3], "z": buf[:, 0:256].rearrange("p (t f) -> p t f", t=2), "zT": buf[:, 256:512],
                     "ge": buf[:, 512:1280].rearrange("p (c q) -> p c q", c=3),
                     "g": buf[:, 1280:2048].rearrange("p (c q) -> p c q", c=3)}
                t_one = dve.op(lambda e: e.memset(F["g"][64:128, 2, :], 1.0), *fr)
                if b == 0:
                    new_phase()
                s = XS[b % NXS]
                t = shifted(l, b)
                i, p, tk = turn([s[:, 32:160], s[:, 160:288]], t)
                xsfree[b % NXS] = (tk,)
                z = F["z"]
                t = act.op(lambda e: e.activation(z, p[:, 0:256].rearrange("p (t f) -> p t f", t=2), ACT.Copy), tk, *fr)
                PS.free(i, t)
                yield
                t = yield from layer_norm([z[:, 0, :], z[:, 1, :]], [z[:, 0, :], z[:, 1, :]], F["st"], t, *fr)
                yield
                i, p, tk = turn([z[:, 0, :], z[:, 1, :]], t)
                t = act.op(lambda e, p=p: e.activation(F["zT"], p[:, 0:256], ACT.Identity, bias=w["ln"][:, 1:2],
                                                       scale=w["ln"][:, 0:1]), tk, ready["ln"], *fr)
                PS.free(i, t)
                ig, pg, freed = PS.take()
                for c, (c0, n) in enumerate(CH):
                    tg = pe.op(lambda e, c=c, c0=c0, n=n: e.matmul(pg[0:n, 256 * c:256 * c + 256],
                               w["w1"][:, DI + c0:DI + c0 + n], F["zT"], start=True, stop=True, skip_group_check=True),
                               *((t, ready["w1"], *freed) if c == 0 else ()))
                ia, pa, freed = PS.take()
                for c, (c0, n) in enumerate(CH):
                    ta = pe.op(lambda e, c=c, c0=c0, n=n: e.matmul(pa[0:n, 256 * c:256 * c + 256],
                               w["w1"][:, c0:c0 + n], F["zT"], start=True, stop=True, skip_group_check=True),
                               *(freed if c == 0 else ()))
                for c, (c0, n) in enumerate(CH):
                    t = act.op(lambda e, c=c, n=n: e.activation(F["ge"][0:n, c, :], pg[0:n, 256 * c:256 * c + 256], ACT.Gelu,
                                                                bias=w["b1"][0:n, 3 + c:4 + c]), tg, ready["b1"], *fr)
                PS.free(ig, t)
                for c, (c0, n) in enumerate(CH):
                    td = dve.op(lambda e, c=c, n=n: e.scalar_tensor_tensor(
                        F["g"][0:n, c, :], pa[0:n, 256 * c:256 * c + 256], w["b1"][0:n, c:c + 1], F["ge"][0:n, c, :],
                        ALU.add, ALU.mult), t, ta, t_one)
                PS.free(ia, td)
                yield
                i, p, freed = PS.take()
                for tile in range(2):
                    for c in range(3):
                        n = 128 if c < 2 else 86
                        tk = pe.op(lambda e, p=p, c=c, n=n, tile=tile: e.matmul(
                            p[:, 128 * tile:128 * tile + 128], F["g"][0:n, c, 128 * tile:128 * tile + 128],
                            w["w2"][0:n, c, :], start=(c == 0), stop=(c == 2), skip_group_check=True),
                            *((td, ready["w2"], *freed) if tile == c == 0 else ()))
                t = dve.op(lambda e, p=p: e.tensor_tensor(XX[:, 2 * b:2 * b + 2, :], XX[:, 2 * b:2 * b + 2, :],
                                                          p[:, 0:256].rearrange("p (t f) -> p t f", t=2), ALU.add), tk)
                PS.free(i, t)
                xx_tok[2 * b] = xx_tok[2 * b + 1] = t
                T1.free(iF, tk)
                if b == NB - 1:
                    read["ffn"] = (tk, t, act.last())
                    if l + 1 < run["depth"]:
                        load_ffn(l + 1)

            def end(b):
                t = yield from layer_norm([XX[:, 2 * b, :], XX[:, 2 * b + 1, :]], [XX[:, 2 * b, :], XX[:, 2 * b + 1, :]],
                                          st2[b % 4], xx_tok[2 * b], xx_tok[2 * b + 1])
                dve.op(lambda e: e.tensor_tensor(XR[:, 2 * b:2 * b + 2, :], XR[:, 2 * b:2 * b + 2, :],
                                                 XX[:, 2 * b:2 * b + 2, :], ALU.add), t)

            load_attn(0)
            load_ffn(0)
            drive([start(b) for b in range(NB)], 4)
            for l in range(run["depth"]):
                drive([attn(l, k) for k in range(2 * NB)], 9)
                drive([ffn(l, b) for b in range(NB)], 3, 2)
            drive([end(b) for b in range(NB)], 4)
        for ph, f in (("A", phase_a), ("B", phase_b), ("C", phase_c), ("D", phase_d)):
            if ph in run["phases"]:
                f()

        fence()
        s_out = ctx.enter_context(nc.semaphore("s_out"))
        n_out = 0
        for b0 in range(0, NB, 4):
            sp.e.dma_start(out[b0:b0 + 4].rearrange("b (t p) f -> p (b t) f", p=128),
                           XR[:, 2 * b0:2 * b0 + 8, :]).then_inc(s_out, 16)
            n_out += 16
        sp.wait((s_out, n_out), *t_x)


def constants():
    f = np.float32
    c = {"kident": np.eye(128, dtype=f)}
    q, k = np.arange(128)[:, None], np.arange(128)[None, :]
    m = np.where(k > q, f(-1e30), f(0)).astype(f)
    c["kmask"] = np.ascontiguousarray(np.stack([m, m.T], 1))
    r = (np.arange(128) % 64)[:, None]
    j = np.arange(96)[None, :]
    ok = (j >= r) & (j <= r + 32)
    first = ok & ((np.arange(128)[:, None] >= 64) | (j >= 32))
    md = np.stack([np.where(x, f(0), f(-1e30)).astype(f) for x in (first, ok)], 1)
    c["kmaskd"] = np.ascontiguousarray(np.tile(md, (1, 1, 4)))
    sel = np.zeros((128, 16, 128), np.uint16)
    for i in range(48):
        sel[i, i % 16, :] = sel[64 + i, i % 16, :] = 0xBF80
    c["ksel"] = sel.reshape(128, 2048).view(f)
    half = np.arange(0, 64, 2, dtype=f)
    inv = (f(1.0) / np.power(f(10000.0), half / f(64))).astype(f)
    t = np.arange(256, dtype=f)
    fr = (t[:, None] * inv[None, :]).astype(f)
    fr = np.concatenate([fr, fr], -1)
    bs = (half + f(25.6)) / f(89.6)
    power = (t - 128) / 16
    sc = np.power(bs[None, :].astype(np.float64), power[:, None].astype(np.float64))
    sc = np.concatenate([sc, sc], -1)
    sign = np.where(np.arange(64) < 32, -1.0, 1.0)
    cs, sn = np.cos(fr.astype(np.float64)), np.sin(fr.astype(np.float64)) * sign
    tab = np.stack([8 * cs * sc, 8 * sn * sc, cs / sc, sn / sc], 1).astype(f)
    c["krope"] = np.ascontiguousarray(tab.reshape(2, 128, 4, 64).transpose(1, 0, 2, 3))
    c["kiota"] = np.ascontiguousarray(np.broadcast_to(np.arange(64, dtype=f)[None, :, None], (128, 64, 8)))
    c["kx8"] = np.ascontiguousarray(np.broadcast_to(np.arange(8, dtype=f)[None, :, None], (128, 8, 8)))
    c["kw8"] = np.ascontiguousarray(np.broadcast_to((8 - np.arange(8)).astype(f)[None, :], (128, 8)))
    return c


def layout(i):
    g = lambda n: np.asarray(i[n])
    C = np.ascontiguousarray
    a = {"x": g("L0_attn_hidden_states")}
    a["aUT"] = C(np.concatenate([g(f"L0_attn_{n}_U").transpose(2, 1, 0) for n in "qkv"], 1))
    a["aV"] = C(np.concatenate([g(f"L0_attn_{n}_V").transpose(1, 0, 2) for n in "qkv"], 1))
    a["ab"] = C(np.concatenate([g(f"L0_attn_{n}_b").reshape(1, 128) for n in "qkv"], 1))
    a["aoUT"] = C(g("L0_attn_out_U").T)
    a["aoV"] = g("L0_attn_out_V")
    a["aob"] = g("L0_attn_out_b").reshape(1, 128)
    a["af1UT"] = C(g("L0_attn_fc1_U").T)
    a["af1V"] = g("L0_attn_fc1_V")
    a["af1b"] = C(g("L0_attn_fc1_b").reshape(4, 128).T)
    a["af2UT"] = C(g("L0_attn_fc2_U").T)
    a["af2V"] = g("L0_attn_fc2_V")
    a["af2b"] = g("L0_attn_fc2_b").reshape(1, 128)
    a["aln"] = C(np.stack([g(f"L0_attn_{n}") for n in ("ln1_g", "ln1_b", "ln2_g", "ln2_b")], 1))
    a["bWq"] = C(g("L0_ffn_W_q").reshape(8, 64, 128).transpose(1, 0, 2))
    a["bkT"] = C(g("L0_ffn_keys").transpose(3, 2, 0, 1).reshape(64, 8, 64))
    a["bdT"] = C(g("L0_ffn_down_embed").T)
    a["bue"] = C(g("L0_ffn_up_embed").reshape(4, 128, 128).transpose(1, 0, 2))
    a["bup"] = C(g("L0_ffn_W_up").T)
    a["bdn"] = C(g("L0_ffn_W_down").T.reshape(4, 128, 128).transpose(1, 0, 2))
    a["cW"] = C(np.concatenate([g(f"L1_attn_W{n}") for n in "qkv"], 1))
    a["cWo"] = g("L1_attn_Wo")
    a["cbo"] = g("L1_attn_bo").reshape(1, 128)
    a["dWqkv"] = g("L1_ffn_Wqkv")
    qs, ks = g("L1_ffn_q_scale"), g("L1_ffn_k_scale")
    rot = lambda s: np.concatenate([s[:, 32:], s[:, :32]], 1)
    a["dsc"] = C(np.stack([qs, rot(qs), ks, rot(ks)], 1))
    a["dWo"] = C(g("L1_ffn_Wo").reshape(DEPTH, 8, 128, 128).transpose(0, 2, 1, 3))
    a["dln"] = C(np.stack([g("L1_ffn_ln_g"), g("L1_ffn_ln_b")], 2))
    a["dW1"] = g("L1_ffn_W1")
    b1, w2, b2 = g("L1_ffn_b1"), g("L1_ffn_W2"), g("L1_ffn_b2")
    pb = np.zeros((DEPTH, 128, 6), np.float32)
    pw = np.zeros((DEPTH, 128, 3, 128), np.float32)
    for c, (c0, n) in enumerate(CH):
        pb[:, 0:n, c] = b1[:, c0:c0 + n]
        pb[:, 0:n, 3 + c] = b1[:, DI + c0:DI + c0 + n]
        pw[:, 0:n, c, :] = w2[:, c0:c0 + n, :]
    pw[:, 85, 2, :] = b2
    a["db1"], a["dW2"] = pb, pw
    a.update(constants())
    return a


RUN = {"phases": "ABCD", "depth": DEPTH}


def kernel(**inputs):
    import concourse.bacc as _bacc
    from concourse.bass_utils import run_bass_kernel_spmd as _run

    nc = _bacc.Bacc("TRN2", target_bir_lowering=False, num_devices=1)
    arrays, d = {}, {}
    given = layout(inputs)
    for name, (shape, dt) in SPEC.items():
        a = np.ascontiguousarray(given[name])
        assert a.shape == shape, (name, a.shape)
        arrays[f"in_{name}"] = a
        d[name] = nc.dram_tensor(f"in_{name}", shape, dt, kind="ExternalInput").ap()
    out = nc.dram_tensor("out_0", (NB, 256, 128), F32, kind="ExternalOutput").ap()
    network(nc, d, out, RUN)
    r = _run(nc, [arrays], core_ids=[0])
    return r.results[0]["out_0"]
```

```python
from contextlib import ExitStack

import numpy as np

import concourse.bass as bass
from concourse import mybir

F32 = mybir.dt.float32
BF16 = mybir.dt.bfloat16
U32 = mybir.dt.uint32
ACT = mybir.ActivationFunctionType
ALU = mybir.AluOpType
AX = mybir.AxisListType

NB = 16
DEPTH = 6
EPS = 1e-5
DI = 341
CH = [(0, 128), (128, 128), (256, 85)]

SPEC = {
    "x": ((NB, 256, 128), F32),
    "aUT": ((48, 48, 128), F32),
    "aV": ((48, 48, 8), F32),
    "ab": ((1, 384), F32),
    "aoUT": ((96, 128), F32),
    "aoV": ((96, 128), F32),
    "aob": ((1, 128), F32),
    "af1UT": ((64, 128), F32),
    "af1V": ((64, 512), F32),
    "af1b": ((128, 4), F32),
    "af2UT": ((64, 512), F32),
    "af2V": ((64, 128), F32),
    "af2b": ((1, 128), F32),
    "aln": ((128, 4), F32),
    "bWq": ((64, 8, 128), F32),
    "bkT": ((64, 8, 64), F32),
    "bdT": ((128, 512), F32),
    "bue": ((128, 4, 128), F32),
    "bup": ((128, 512), F32),
    "bdn": ((128, 4, 128), F32),
    "cW": ((128, 384), F32),
    "cWo": ((128, 128), F32),
    "cbo": ((1, 128), F32),
    "dWqkv": ((DEPTH, 128, 3072), F32),
    "dsc": ((DEPTH, 4, 64), F32),
    "dWo": ((DEPTH, 128, 8, 128), F32),
    "dln": ((DEPTH, 128, 2), F32),
    "dW1": ((DEPTH, 128, 682), F32),
    "db1": ((DEPTH, 128, 6), F32),
    "dW2": ((DEPTH, 128, 3, 128), F32),
    "kident": ((128, 128), F32),
    "kmask": ((128, 2, 128), F32),
    "kmaskd": ((128, 2, 384), F32),
    "ksel": ((128, 1024), F32),
    "krope": ((128, 2, 4, 64), F32),
    "kiota": ((128, 64, 8), F32),
    "kx8": ((128, 8, 8), F32),
    "kw8": ((128, 8), F32),
}


class Queue:

    def __init__(self, name, engine):
        self.name, self.e, self.sem, self.n = name, engine, None, 0

    def wait(self, *tokens):
        for t in tokens:
            if t is not None:
                self.e.wait_ge(t[0], t[1])

    def op(self, f, *tokens):
        self.wait(*tokens)
        self.n += 1
        f(self.e).then_inc(self.sem, 1)
        return (self.sem, self.n)

    def quiet(self, f, *tokens):
        self.wait(*tokens)
        f(self.e)

    def last(self):
        return (self.sem, self.n) if self.n else None


class Ring:

    def __init__(self, bufs):
        self.bufs, self.k, self.freed = bufs, 0, [()] * len(bufs)

    def take(self):
        i = self.k % len(self.bufs)
        self.k += 1
        freed = self.freed[i]
        assert freed is not None, "a buffer is taken before its last reader is known"
        self.freed[i] = None
        return i, self.bufs[i], freed

    def free(self, i, *tokens):
        self.freed[i] = tokens


def network(nc, d, out, run):
    ctx = ExitStack()
    with ctx:
        pe, act, dve, pool, sp = [Queue(n, e) for n, e in (
            ("pe", nc.tensor), ("act", nc.scalar), ("dve", nc.vector), ("pool", nc.gpsimd), ("sp", nc.sync))]
        queues = (pe, act, dve, pool)
        phases = [0]
        held = []

        def new_phase():
            for q in queues:
                if q.n or q.sem is None:
                    q.sem = ctx.enter_context(nc.semaphore(f"s_{q.name}{phases[0]}"))
                    q.n = 0
            phases[0] += 1

        def fence():
            ends = [q.last() for q in queues]
            for q in (*queues, sp):
                q.wait(*ends)

        nsem = [0]

        def dma(dst, src, *tokens, q=None):
            s = ctx.enter_context(nc.semaphore(f"s_d{nsem[0]}"))
            nsem[0] += 1
            q = q or sp
            q.wait(*tokens)
            q.e.dma_start(dst, src).then_inc(s, 16)
            return (s, 16)

        TOTAL = 52600
        arena = ctx.enter_context(nc.sbuf_tensor("arena", [128, TOTAL], F32))
        top = [0]

        def sb(shape, dt=F32):
            n = 1
            for s in shape[1:]:
                n *= s
            words = n if dt in (F32, U32) else (n + 1) // 2
            a = arena[0:shape[0], top[0]:top[0] + words]
            top[0] += words + (-words) % 8
            assert top[0] <= TOTAL, top[0]
            if dt != F32:
                a = a.bitcast(dt)
            if len(shape) == 3:
                a = a.rearrange("p (a b) -> p a b", a=shape[1])
            if len(shape) == 4:
                a = a.rearrange("p (a b c) -> p a b c", a=shape[1], b=shape[2])
            return a

        def bc(a, dim, n):
            v = a.unsqueeze(dim)
            sh = list(v.shape)
            sh[dim] = n
            return v.broadcast_to(sh)

        slots = [ctx.enter_context(nc.psum_tensor(f"ps{i}", [128, 1024], F32))[:, :] for i in range(4)]
        PS = Ring(slots)
        PO = Ring([slots[3][:, 0:512], slots[3][:, 512:1024]])

        def split_psum(n):
            PS.bufs, PS.k, PS.freed = slots[:n], 0, [()] * n
            PO.k, PO.freed = 0, [()] * 2

        new_phase()

        XR = sb([128, 2 * NB, 128])
        XX = sb([128, 2 * NB, 128])
        ident = sb([128, 128])
        identb = sb([128, 128], BF16)
        mask = sb([128, 2, 128], BF16)
        maskd = sb([128, 2, 384], BF16)
        mhalf = sb([128, 2])
        mhalf32 = sb([128, 32])
        ones1 = sb([1, 128])
        t_mh = pool.op(lambda e: e.memset(mhalf, -0.5))
        t_mh = pool.op(lambda e: e.memset(mhalf32, -0.5))
        base = top[0]

        t_x = []
        for b0 in range(0, NB, 4):
            t_x.append(dma(XR[:, 2 * b0:2 * b0 + 8, :],
                           d["x"][b0:b0 + 4].rearrange("b (t p) f -> p (b t) f", p=128)))
        t_id = dma(ident, d["kident"])
        stage_m = sb([128, 2, 128])
        stage_d = sb([128, 2, 384])
        t1 = dma(stage_m, d["kmask"])
        t2 = dma(stage_d, d["kmaskd"])
        t_idb = pool.op(lambda e: e.tensor_copy(identb, ident), t_id)
        t_mask = pool.op(lambda e: e.tensor_copy(mask, stage_m), t1)
        t_mask = pool.op(lambda e: e.tensor_copy(maskd, stage_d), t2)

        def layer_norm(src, dst, st, *tokens):
            n = len(src)
            for t in range(n):
                tk = dve.op(lambda e: e.bn_stats(st["bn"][:, t, :], src[t]), *(tokens if t == 0 else ()))
            for t in range(n):
                tk = dve.op(lambda e: e.bn_aggr(st["mv"][:, t, :], st["bn"][:, t, :]), *((tk,) if t == 0 else ()))
            tk = pool.op(lambda e: e.tensor_scalar(st["rs"][:, 0:n], st["mv"][:, 0:n, 1], EPS, None, ALU.add), tk)
            tk = pool.op(lambda e: e.tensor_tensor(st["rs"][:, 0:n], st["rs"][:, 0:n], mhalf[:, 0:n], ALU.pow), tk, t_mh)
            yield
            for t in range(n):
                last = dve.op(lambda e: e.tensor_scalar(dst[t], src[t], st["mv"][:, t, 0:1], st["rs"][:, t:t + 1],
                                                        ALU.subtract, ALU.mult), *((tk,) if t == 0 else ()))
            return last

        def stats():
            return {"bn": sb([128, 2, 6]), "mv": sb([128, 2, 2]), "rs": sb([128, 2])}

        def turn(src, *tokens):
            i, p, freed = PS.take()
            for t, s in enumerate(src):
                f = lambda e, t=t, s=s: e.transpose(p[:, 128 * t:128 * t + 128], s, ident)
                w = (*tokens, *freed, t_id) if t == 0 else ()
                if t == len(src) - 1:
                    tk = pe.op(f, *w)
                else:
                    pe.quiet(f, *w)
            return i, p, tk

        def drive_at(units, order):
            live, todo, k = [], sorted(units, key=lambda u: u[0]), 0
            while live or todo:
                while todo and todo[0][0] <= k:
                    live.append(todo.pop(0))
                for u in sorted(live, key=lambda u: order[u[1]][k - u[0]]):
                    try:
                        next(u[2])
                    except StopIteration:
                        live.remove(u)
                k += 1

        def add_ln_residual(y, b, st, *tokens):
            tk = yield from layer_norm([y[:, 0, :], y[:, 1, :]], [y[:, 0, :], y[:, 1, :]], st, *tokens)
            tk = dve.op(lambda e: e.tensor_tensor(XR[:, 2 * b:2 * b + 2, :], XR[:, 2 * b:2 * b + 2, :], y, ALU.add), tk)
            return tk

        NS = 3

        def attention_buffers():
            bufs = []
            for _ in range(NS):
                B = {"st": stats(), "h": sb([128, 2, 128]), "hT": sb([128, 256]), "qkv": sb([128, 2, 256]),
                     "va": sb([128, 2, 16, 32]), "OT": sb([128, 2, 512]),
                     "QS": sb([128, 2, 1024], BF16), "KS": sb([128, 2, 1024], BF16),
                     "QT": sb([128, 8, 256], BF16), "KT": sb([128, 8, 256], BF16),
                     "m": sb([128, 2, 16]), "mr": sb([128, 2, 16]), "ms": sb([128, 2, 128], BF16),
                     "mT": sb([128, 256], BF16), "PT": Ring([sb([128, 3, 2, 128]) for _ in range(3)]), "rc": sb([128, 2, 16]),
                     "y": sb([128, 2, 128])}
                B["ctx"], B["cT"] = B["y"], B["hT"]
                B["r"] = B["OT"][:, 0, :].rearrange("p (t f) -> p t f", t=2)
                b12 = B["OT"][:, 1, :].bitcast(BF16).rearrange("p (s t f) -> p s t f", s=2, t=2)
                B["b1"], B["b2"] = b12[:, 0, :, :], b12[:, 1, :, :]
                bufs.append(B)
            return bufs

        def prepare_attention(bufs):
            for B in bufs:
                t = dve.op(lambda e, B=B: e.memset(B["va"], 0.0))
                B["va_ready"] = dve.op(lambda e, B=B: e.memset(B["va"][:, :, :, 8:9], 1.0), t)
                pool.op(lambda e, B=B: e.memset(B["QS"], 0.0))
                pool.op(lambda e, B=B: e.memset(B["ms"], 0.0))
                B["ready"] = pool.op(lambda e, B=B: e.memset(B["KS"], 0.0))

        def attention(B, W, bias, sel, t_w, *t_h):
            PT = B["PT"]
            for t in range(2):
                i, p, freed = PS.take()
                tq = pe.op(lambda e, t=t: e.matmul(p[:, 0:384], B["hT"][:, 128 * t:128 * t + 128], W, start=True, stop=True),
                           *freed, *(t_h if t == 0 else ()), *t_w)
                if bias is not None:
                    tv = dve.op(lambda e, t=t: e.tensor_tensor(B["qkv"][:, t, :], p[:, 0:256], bias[:, 0:256], ALU.add), tq)
                    tv2 = dve.op(lambda e, t=t: e.tensor_tensor(B["va"][:, t, :, 0:8], p[:, 256:384].rearrange("p (h d) -> p h d", d=8),
                                                               bias[:, 256:384].rearrange("p (h d) -> p h d", d=8), ALU.add))
                else:
                    tv = dve.op(lambda e, t=t: e.tensor_copy(B["qkv"][:, t, :], p[:, 0:256]), tq)
                    tv2 = dve.op(lambda e, t=t: e.tensor_copy(B["va"][:, t, :, 0:8],
                                                              p[:, 256:384].rearrange("p (h d) -> p h d", d=8)))
                PS.free(i, tv2)
            t = act.op(lambda e: e.activation(B["b1"], B["qkv"], ACT.Copy), tv)
            t = dve.op(lambda e: e.tensor_tensor(B["r"], B["qkv"], B["b1"], ALU.subtract), t)
            t = act.op(lambda e: e.activation(B["b2"], B["r"], ACT.Copy), t)
            t = dve.op(lambda e: e.tensor_tensor(B["r"], B["r"], B["b2"], ALU.subtract), t)
            yield
            q = [B[n][:, :, 0:128].rearrange("p t (h e) -> p t h e", e=8) for n in ("b1", "b2", "r")]
            k = [B[n][:, :, 128:256].rearrange("p t (h e) -> p t h e", e=8) for n in ("b1", "b2", "r")]
            tb = []
            for S, parts, order in (("QS", q, (0, 0, 1, 1, 0, 2)), ("KS", k, (0, 1, 0, 1, 2, 0))):
                for tile in range(2):
                    s = B[S][:, tile, :].rearrange("p (h g e) -> p h g e", h=16, g=8)
                    for g, o in enumerate(order):
                        eng = pool if g == 5 else dve
                        tb.append(eng.op(lambda e, s=s, g=g, o=o, parts=parts, tile=tile:
                                         e.tensor_copy(s[:, :, g, :], parts[o][:, tile, :, :]), t, B["ready"]))
            tb = [dve.last(), pool.last()]
            yield
            for S, T in (("QS", "QT"), ("KS", "KT")):
                for tile in range(2):
                    i, p, freed = PS.take()
                    pb = p.bitcast(BF16)
                    for c in range(8):
                        f = lambda e, c=c, S=S, tile=tile, pb=pb: e.transpose(
                            pb[:, 128 * c:128 * c + 128], B[S][:, tile, 128 * c:128 * c + 128], identb)
                        w = (*freed, *tb, t_idb) if c == 0 else ()
                        if c == 7:
                            tk = pe.op(f, *w)
                        else:
                            pe.quiet(f, *w)
                    g = lambda e, T=T, tile=tile, pb=pb: e.tensor_copy(
                        B[T][:, :, 128 * tile:128 * tile + 128], pb[:, 0:1024].rearrange("p (c q) -> p c q", c=8))
                    if tile == 0:
                        te = act.op(lambda e, T=T, tile=tile, pb=pb: e.activation(
                            B[T][:, :, 128 * tile:128 * tile + 128], pb[:, 0:1024].rearrange("p (c q) -> p c q", c=8),
                            ACT.Copy), tk)
                    else:
                        te = dve.op(g, tk)
                    PS.free(i, te)
            t_qk = (act.last(), dve.last())
            yield

            def row(h):
                return slice(64 * (h % 2), 64 * (h % 2) + 48)

            for tile in range(2):
                nk = 128 * (tile + 1)
                per = 1024 // nk
                for g in range(16 // per):
                    i, p, freed = PS.take()
                    for j in range(per):
                        h = g * per + j
                        o = p[:, 512 * (j % 2) + (j // 2) * nk:512 * (j % 2) + (j // 2 + 1) * nk]
                        w = (*freed, *t_qk, t_mask) if j == 0 else ()
                        pe.quiet(lambda e, o=o, nk=nk, h=h, tile=tile: e.matmul(
                            o, B["QT"][row(h), h // 2, 128 * tile:128 * tile + 128],
                            B["KT"][row(h), h // 2, 0:nk], start=True, stop=False, skip_group_check=True), *w)
                        tk = pe.op(lambda e, o=o, nk=nk: e.matmul(
                            o[:, nk - 128:nk], identb, mask[:, 0, :], start=False, stop=True, skip_group_check=True))
                    td = dve.op(lambda e, p=p, g=g, per=per, nk=nk, tile=tile: e.tensor_reduce(
                        B["m"][:, tile, g * per:(g + 1) * per].rearrange("p (j u) -> p u j", u=2),
                        p.rearrange("p (u j k) -> p u j k", u=2, k=nk), AX.X, ALU.max), tk)
                    PS.free(i, td)
                    if g % 2:
                        yield
            ms = [B["ms"].rearrange("p t (u r) -> p t u r", u=2)[:, :, :, 16 * j:16 * j + 16] for j in range(3)]
            t = dve.op(lambda e: e.tensor_copy(ms[0], bc(B["m"], 2, 2)), td, B["ready"])
            t = dve.op(lambda e: e.tensor_tensor(B["mr"], B["m"], ms[0][:, :, 0, :], ALU.subtract), t)
            t = dve.op(lambda e: e.tensor_copy(ms[1], bc(B["mr"], 2, 2)), t)
            t = dve.op(lambda e: e.tensor_tensor(B["mr"], B["mr"], ms[1][:, :, 0, :], ALU.subtract), t)
            t = dve.op(lambda e: e.tensor_copy(ms[2], bc(B["mr"], 2, 2)), t)
            i, p, freed = PS.take()
            pb = p.bitcast(BF16)
            pe.quiet(lambda e, pb=pb: e.transpose(pb[:, 0:128], B["ms"][:, 0, :], identb), t, *freed)
            tk = pe.op(lambda e, pb=pb: e.transpose(pb[:, 128:256], B["ms"][:, 1, :], identb))
            t_m = act.op(lambda e, pb=pb: e.activation(B["mT"], pb[:, 0:256], ACT.Copy), tk)
            PS.free(i, t_m)
            yield
            lag, waiting = 2, []
            ot = {}

            def product():
                g, P, tp, ip = waiting.pop(0)
                half = g // 4
                if g % 4 == 0:
                    ot["i"], ot["p"], ot["freed"] = PO.take()
                o = ot["p"]
                for kt, st in ((0, True), (1, False)):
                    for j in range(2):
                        h = 2 * g + j
                        c = 256 * ((h // 4) % 2)
                        q0 = 128 * kt
                        rhs = P[:, 1, j, :] if kt else P[:, 0:3:2, j, :]
                        f = lambda e: e.matmul(o[32 * (h % 4):32 * (h % 4) + 32, c + q0:c + 256], B["va"][:, kt, h, :],
                                               rhs, start=st, stop=not st, skip_group_check=True)
                        w = (tp, *ot["freed"]) if kt == j == 0 else ()
                        if kt and j:
                            tk = pe.op(f, *w)
                        else:
                            pe.quiet(f, *w)
                PT.free(ip, tk)
                if g % 4 == 3:
                    t = act.op(lambda e: e.activation(B["OT"][:, half, :], o, ACT.Copy), tk)
                    PO.free(ot["i"], t)
                    ot["t"] = t

            for g in range(8):
                i, p, freed = PS.take()
                w = (*freed, t_m)
                for kt, q0 in ((0, 0), (1, 128)):
                    for what in range(2):
                        for j in range(2):
                            h = 2 * g + j
                            o = p[:, 512 * j:512 * j + 512].rearrange("p (c q) -> p c q", c=4)
                            o = o[:, 1, :] if kt else o[:, 0:3:2, :]
                            lhs = sel[row(h), h, :] if what else B["KT"][row(h), h // 2, 128 * kt:128 * kt + 128]
                            rhs = B["mT"][row(h), q0:256] if what else B["QT"][row(h), h // 2, q0:256]
                            pe.quiet(lambda e: e.matmul(o, lhs, rhs, start=(kt == what == 0), stop=False,
                                                        skip_group_check=True), *w)
                            w = ()
                for j in range(2):
                    tk = pe.op(lambda e: e.matmul(p[:, 512 * j:512 * j + 256], identb, bc(mask[:, 1, :], 1, 2),
                                                  start=False, stop=True, skip_group_check=True))
                ip, P, pfreed = PT.take()
                te = act.op(lambda e: e.activation(P, p.rearrange("p (j c q) -> p c j q", j=2, c=4)[:, 0:3, :, :],
                                                   ACT.Exp), tk, *pfreed)
                PS.free(i, te)
                waiting.append((g, P, te, ip))
                if len(waiting) > lag:
                    product()
                yield
            while waiting:
                product()
            yield
            i, p, freed = PS.take()
            for tile in range(2):
                for c in range(4):
                    tk = pe.op(lambda e: e.transpose(
                        p[:, 512 * tile + 128 * c:512 * tile + 128 * c + 128],
                        B["OT"][:, c // 2, 256 * (c % 2) + 128 * tile:256 * (c % 2) + 128 * tile + 128], ident),
                        *((*freed, ot["t"]) if tile == c == 0 else ()))
            O = p.rearrange("p (t h e) -> p t h e", t=2, h=16)
            t = dve.op(lambda e: e.reciprocal(B["rc"], O[:, :, :, 8]), tk)
            for tile in range(2):
                t = dve.op(lambda e: e.tensor_tensor(
                    B["ctx"][:, tile, :].rearrange("p (h e) -> p h e", e=8), O[:, tile, :, 0:8],
                    bc(B["rc"][:, tile, :], 2, 8), ALU.mult), t if tile == 0 else None)
            PS.free(i, t)
            B["t_ctx"] = t

        def phase_a():
            fence()
            split_psum(3)
            top[0] = base
            new_phase()
            early = sb([128, 6144])
            raw_ut = early[0:48, :].rearrange("p (j k) -> p j k", j=48)
            raw_v = sb([48, 48, 8])
            oU, oV = sb([96, 128]), sb([96, 128])
            f1U, f1V = sb([64, 128]), sb([64, 512])
            f2U, f2V = sb([64, 512]), sb([64, 128])
            W, bias = sb([128, 384]), sb([128, 384])
            Wo, bo = sb([128, 128]), sb([128, 128])
            W1, b1 = sb([128, 512]), sb([128, 4])
            W2, b2 = sb([128, 4, 128]), sb([128, 128])
            sel32 = sb([128, 1024])
            sel = sel32.bitcast(BF16).rearrange("p (h k) -> p h k", h=16)
            ln = sb([128, 4])
            tw = [dma(x, d[n]) for x, n in ((raw_ut, "aUT"), (raw_v, "aV"), (oU, "aoUT"), (oV, "aoV"), (f1U, "af1UT"),
                                            (f1V, "af1V"), (f2U, "af2UT"), (f2V, "af2V"), (sel32, "ksel"), (b1, "af1b"),
                                            (ln, "aln"))]
            tb = dma(bias, d["ab"].broadcast_to([128, 384]))
            tbo = dma(bo, d["aob"].broadcast_to([128, 128]))
            tb2 = dma(b2, d["af2b"].broadcast_to([128, 128]))
            s8 = float(np.float32(1.0) / np.sqrt(np.float32(8.0)))
            t_sel = tw[8]
            i, p, freed = PS.take()
            for j in range(48):
                f = lambda e, j=j: e.matmul(p[:, 8 * j:8 * j + 8], raw_ut[:, j, :], raw_v[:, j, :], start=True, stop=True,
                                            skip_group_check=True)
                if j == 47:
                    tk = pe.op(f)
                else:
                    pe.quiet(f, *((*freed, tw[0], tw[1]) if j == 0 else ()))
            act.op(lambda e: e.activation(W[:, 0:128], p[:, 0:128], ACT.Copy, scale=s8), tk)
            t_W = act.op(lambda e: e.activation(W[:, 128:384], p[:, 128:384], ACT.Copy))
            PS.free(i, t_W)
            t_b = act.op(lambda e: e.activation(bias[:, 0:128], bias[:, 0:128], ACT.Copy, scale=s8), tb)
            i, p, freed = PS.take()
            pe.quiet(lambda e: e.matmul(p[:, 0:128], oU, oV, start=True, stop=True), *freed, tw[2], tw[3])
            tk = pe.op(lambda e: e.matmul(p[:, 512:1024], f1U, f1V, start=True, stop=True), tw[4], tw[5])
            act.op(lambda e: e.activation(Wo, p[:, 0:128], ACT.Copy), tk)
            t_W1 = act.op(lambda e: e.activation(W1, p[:, 512:1024], ACT.Copy))
            PS.free(i, t_W1)
            i, p, freed = PS.take()
            for c in range(4):
                tk = pe.op(lambda e, c=c, p=p: e.matmul(p[:, 128 * c:128 * c + 128], f2U[:, 128 * c:128 * c + 128], f2V,
                                                        start=True, stop=True, skip_group_check=True),
                           *freed, tw[6], tw[7])
            t_W2 = act.op(lambda e: e.activation(W2, p[:, 0:512].rearrange("p (c n) -> p c n", c=4), ACT.Copy), tk)
            PS.free(i, t_W2)

            mb = []
            for j in range(3):
                a = early[:, 2048 * j:2048 * j + 2048]
                mb.append({"st": stats(), "z": a[:, 0:256].rearrange("p (t f) -> p t f", t=2), "zT": a[:, 256:512],
                           "g": a[:, 512:1536].rearrange("p (c q) -> p c q", c=4)})
            bufs = attention_buffers()
            done = {}

            def unit(b):
                B = bufs[b % NS]
                prior = (done[b - NS] if b >= NS else ())
                X = [XR[:, 2 * b, :], XR[:, 2 * b + 1, :]]
                h, y = B["h"], B["y"]
                t = yield from layer_norm(X, [h[:, 0, :], h[:, 1, :]], B["st"], t_x[b // 4], *prior)
                yield
                t = yield from layer_norm([h[:, 0, :], h[:, 1, :]], [y[:, 0, :], y[:, 1, :]], B["st"], t)
                if b < NS:
                    prepare_attention([B])
                yield
                i, p, tk = turn([y[:, 0, :], y[:, 1, :]], t)
                t_h = act.op(lambda e: e.activation(B["hT"], p[:, 0:256], ACT.Identity, bias=ln[:, 1:2], scale=ln[:, 0:1]),
                             tk, tw[10])
                PS.free(i, t_h)
                yield
                yield from attention(B, W, bias, sel, (t_W, t_b, t_sel), t_h)
                yield
                i, p, tk = turn([B["ctx"][:, 0, :], B["ctx"][:, 1, :]], B["t_ctx"])
                t = act.op(lambda e: e.activation(B["cT"], p[:, 0:256], ACT.Copy), tk)
                PS.free(i, t)
                i, p, freed = PS.take()
                pe.quiet(lambda e: e.matmul(p[:, 0:128], B["cT"][:, 0:128], Wo, start=True, stop=True,
                                            skip_group_check=True), t, *freed)
                tk = pe.op(lambda e: e.matmul(p[:, 128:256], B["cT"][:, 128:256], Wo, start=True, stop=True,
                                              skip_group_check=True))
                th = pool.op(lambda e: e.tensor_tensor(h, h, bc(bo, 1, 2), ALU.add), tbo, B["t_ctx"])
                t = dve.op(lambda e: e.tensor_tensor(XX[:, 2 * b:2 * b + 2, :], h,
                                                     p[:, 0:256].rearrange("p (t f) -> p t f", t=2), ALU.add), tk, th)
                PS.free(i, t)
                done[b] = (t,)

            mdone = {}

            def mlp(b):
                M = mb[b % 3]
                H = XX[:, 2 * b:2 * b + 2, :]
                z = M["z"]
                t = yield from layer_norm([H[:, 0, :], H[:, 1, :]], [z[:, 0, :], z[:, 1, :]], M["st"], *done[b],
                                          *(mdone[b - 3] if b >= 3 else (t_W,)))
                yield
                i, p, tk = turn([z[:, 0, :], z[:, 1, :]], t)
                t = act.op(lambda e: e.activation(M["zT"], p[:, 0:256], ACT.Identity, bias=ln[:, 3:4], scale=ln[:, 2:3]), tk)
                PS.free(i, t)
                yield
                i, p, freed = PS.take()
                for c in range(4):
                    tk = pe.op(lambda e, c=c, p=p: e.matmul(p[:, 256 * c:256 * c + 256], W1[:, 128 * c:128 * c + 128],
                                                            M["zT"], start=True, stop=True, skip_group_check=True),
                               t, *freed, t_W1)
                for c in range(4):
                    t = act.op(lambda e, c=c, p=p: e.activation(M["g"][:, c, :], p[:, 256 * c:256 * c + 256],
                                                                ACT.Gelu_apprx_tanh, bias=b1[:, c:c + 1]), tk, tw[9])
                PS.free(i, t)
                yield
                i, p, freed = PS.take()
                for tile in range(2):
                    for c in range(4):
                        tk = pe.op(lambda e, c=c, tile=tile, p=p: e.matmul(
                            p[:, 128 * tile:128 * tile + 128], M["g"][:, c, 128 * tile:128 * tile + 128], W2[:, c, :],
                            start=(c == 0), stop=(c == 3), skip_group_check=True), t, *freed, t_W2)
                t = dve.op(lambda e: e.tensor_tensor(z, H, p[:, 0:256].rearrange("p (t f) -> p t f", t=2), ALU.add), tk)
                PS.free(i, t)
                t = dve.op(lambda e: e.tensor_tensor(z, z, bc(b2, 1, 2), ALU.add), t, tb2)
                yield
                t = yield from add_ln_residual(z, b, M["st"], t)
                mdone[b] = (t,)

            EVERY_A = 8
            ORDER_A = [23, 20, 0, 17, 2, 3, 4, 22, 5, 7, 8, 16, 11, 12, 13, 14, 9, 18, 19, 27, 8, 25, 28]
            ORDER_M = [6, 1, 10, 15, 21, 24, 26, 29]
            drive_at([(EVERY_A * b, 0, unit(b)) for b in range(NB)] +
                     [(EVERY_A * b + 23, 1, mlp(b)) for b in range(NB)], [ORDER_A, ORDER_M])

        def phase_c():
            fence()
            split_psum(3)
            top[0] = base
            new_phase()
            W, Wo, bo = sb([128, 384]), sb([128, 128]), sb([128, 128])
            sel32 = sb([128, 1024])
            sel = sel32.bitcast(BF16).rearrange("p (h k) -> p h k", h=16)
            t_W, t_Wo, t_sel = dma(W, d["cW"]), dma(Wo, d["cWo"]), dma(sel32, d["ksel"])
            tbo = dma(bo, d["cbo"].broadcast_to([128, 128]))
            s8 = float(np.float32(1.0) / np.sqrt(np.float32(8.0)))
            t_Ws = act.op(lambda e: e.activation(W[:, 0:128], W[:, 0:128], ACT.Copy, scale=s8), t_W)
            bufs = attention_buffers()
            done = {}

            def unit(b):
                B = bufs[b % NS]
                X = [XR[:, 2 * b, :], XR[:, 2 * b + 1, :]]
                h, y = B["h"], B["y"]
                t = yield from layer_norm(X, [h[:, 0, :], h[:, 1, :]], B["st"], t_x[b // 4], *(done[b - NS] if b >= NS else ()))
                if b < NS:
                    prepare_attention([B])
                yield
                i, p, tk = turn([h[:, 0, :], h[:, 1, :]], t)
                t_h = act.op(lambda e: e.activation(B["hT"], p[:, 0:256], ACT.Copy), tk)
                PS.free(i, t_h)
                yield
                yield from attention(B, W, None, sel, (t_Ws, t_sel), t_h)
                yield
                i, p, tk = turn([B["ctx"][:, 0, :], B["ctx"][:, 1, :]], B["t_ctx"])
                t = act.op(lambda e: e.activation(B["cT"], p[:, 0:256], ACT.Copy), tk)
                PS.free(i, t)
                i, p, freed = PS.take()
                pe.quiet(lambda e: e.matmul(p[:, 0:128], B["cT"][:, 0:128], Wo, start=True, stop=True,
                                            skip_group_check=True), t, t_Wo, *freed)
                tk = pe.op(lambda e: e.matmul(p[:, 128:256], B["cT"][:, 128:256], Wo, start=True, stop=True,
                                              skip_group_check=True))
                t = dve.op(lambda e: e.tensor_tensor(y, p[:, 0:256].rearrange("p (t f) -> p t f", t=2), bc(bo, 1, 2),
                                                     ALU.add), tk, tbo)
                PS.free(i, t)
                yield
                t = yield from add_ln_residual(y, b, B["st"], t)
                done[b] = (t,)

            EVERY_C = 8
            ORDER_C = [7, 9, 0, 2, 3, 22, 8, 14, 10, 6, 21, 12, 11, 20, 1, 15, 16, 4, 19, 17, 18, 13, 5]
            drive_at([(EVERY_C * b, 0, unit(b)) for b in range(NB)], [ORDER_C])

        def phase_b():
            fence()
            split_psum(3)
            top[0] = base
            new_phase()
            wq, kT = sb([64, 8, 128]), sb([64, 8, 64])
            Wsim, Wdn, Wue, Wup = sb([128, 512]), sb([128, 4, 128]), sb([128, 4, 128]), sb([128, 512])
            Wd = sb([128, 512])
            io, iob = sb([128, 64, 8]), sb([128, 64, 8], BF16)
            x8, w8, w8b = sb([128, 8, 8]), sb([128, 8]), sb([128, 8], BF16)
            tw = {n: dma(a, d[n]) for a, n in ((wq, "bWq"), (kT, "bkT"), (Wdn, "bdn"), (Wue, "bue"), (Wup, "bup"),
                                               (Wd, "bdT"), (io, "kiota"), (x8, "kx8"), (w8, "kw8"))}
            pool.op(lambda e: e.tensor_copy(iob, io), tw["kiota"])
            t_io = pool.op(lambda e: e.tensor_copy(w8b, w8), tw["kw8"])
            i, p, freed = PS.take()
            for g in range(8):
                tk = pe.op(lambda e, g=g: e.matmul(p[:, 64 * g:64 * g + 64], wq[:, g, :], kT[:, g, :], start=True,
                                                   stop=True, skip_group_check=True), *freed, tw["bWq"], tw["bkT"])
            t_sim = act.op(lambda e: e.activation(Wsim, p[:, 0:512], ACT.Copy), tk)
            PS.free(i, t_sim)
            NU = 3
            ub = [{"st": stats(), "h": sb([128, 2, 128]), "hT": sb([128, 256]), "up": sb([128, 4, 256]),
                   "AT": sb([128, 4, 128]), "y": sb([128, 2, 128])} for _ in range(NU)]
            tb_ = [{"SP": sb([128, 1024]), "v8": sb([128, 8, 8]), "ix": sb([128, 8, 8], U32), "ixf": sb([128, 8, 8]),
                    "iyb": sb([128, 4, 8], BF16), "C": sb([128, 4, 64]), "C2": sb([128, 4, 64]), "c8": sb([128, 4, 8]),
                    "M": sb([128, 4, 64]), "n": sb([128, 4, 8]), "E": sb([128, 576]), "Z": sb([128, 4]),
                    "rz": sb([128, 4]), "big": sb([128, 4, 8]), "oh": sb([128, 4, 64]), "thr": sb([128, 4, 8]),
                    "eq": sb([128, 256, 8], BF16), "R": sb([128, 4, 64]), "cs": sb([128, 1]),
                    "G": sb([128, 4, 8, 64])} for _ in range(4)]
            G2s = Ring([sb([128, 4, 8, 64]) for _ in range(2)])
            done = {}
            tdone = {(b, tile): () for b in (-2, -1) for tile in range(2)}

            def unit(b):
                U = ub[b % NU]
                h, hT = U["h"], U["hT"]
                t = yield from layer_norm([XR[:, 2 * b, :], XR[:, 2 * b + 1, :]], [h[:, 0, :], h[:, 1, :]], U["st"], t_x[b // 4],
                               *(done[b - NU] if b >= NU else ()))
                i, p, tk = turn([h[:, 0, :], h[:, 1, :]], t)
                t_h = act.op(lambda e: e.activation(hT, p[:, 0:256], ACT.Copy), tk)
                PS.free(i, t_h)
                yield
                tsp = []
                for tile in range(2):
                    n4 = 2 * (b % 2) + tile
                    SP = tb_[n4]["SP"]
                    i, p, freed = PS.take()
                    pe.quiet(lambda e, p=p, tile=tile: e.matmul(p[:, 0:512], hT[:, 128 * tile:128 * tile + 128], Wsim,
                                                                start=True, stop=True), t_h, t_sim, *freed)
                    tk = pe.op(lambda e, p=p, tile=tile: e.matmul(p[:, 512:1024], hT[:, 128 * tile:128 * tile + 128], Wd,
                                                                  start=True, stop=True), tw["bdT"])
                    tsp.append(act.op(lambda e, p=p, SP=SP: e.activation(SP, p, ACT.Copy), tk, *tdone[b - 2, tile]))
                    PS.free(i, tsp[tile])
                yield

                def choose(tile):
                    n4 = 2 * (b % 2) + tile
                    T = tb_[n4]
                    SP, v8, ix, ixf, C, C2, c8, M, E = (T[n] for n in ("SP", "v8", "ix", "ixf", "C", "C2", "c8", "M", "E"))
                    SIM = SP[:, 0:512].rearrange("p (g k) -> p g k", g=8)
                    PRJ = SP[:, 512:1024].rearrange("p (x y) -> p x y", x=8)
                    ts = tsp[tile]
                    for g in range(8):
                        t = dve.op(lambda e, g=g, v8=v8, SIM=SIM: e.max(v8[:, g, :], SIM[:, g, :]), ts, *tdone[b - 2, tile])
                    for g in range(8):
                        t = dve.op(lambda e, g=g, v8=v8, SIM=SIM, ix=ix: e.max_index(ix[:, g, :], v8[:, g, :], SIM[:, g, :]), t)
                    ti = dve.op(lambda e, ix=ix, ixf=ixf: e.tensor_copy(ixf, ix), t)
                    C4 = C.rearrange("p h (i j) -> p h i j", i=8)
                    tc = dve.op(lambda e, C4=C4, v8=v8: e.tensor_tensor(
                        C4, bc(v8[:, 0:4, :], 3, 8), bc(v8[:, 4:8, :], 2, 8), ALU.add))
                    for hh in range(4):
                        t = dve.op(lambda e, hh=hh, c8=c8, C=C: e.max(c8[:, hh, :], C[:, hh, :]), tc)
                    for hh in range(4):
                        t = dve.op(lambda e, hh=hh, c8=c8, C=C, C2=C2: e.match_replace(
                            C2[:, hh, :], c8[:, hh, :], C[:, hh, :], -3.0e38), t)
                    ey = E[:, 0:256].rearrange("p (h y) -> p h y", h=4)
                    ex = E[:, 256:288].rearrange("p (h x) -> p h x", h=4)
                    e8 = E[:, 288:320].rearrange("p (h x) -> p h x", h=4)
                    eC = E[:, 320:576].rearrange("p (h x) -> p h x", h=4)
                    dve.op(lambda e, ey=ey, SIM=SIM, v8=v8: e.tensor_tensor(ey, SIM[:, 4:8, :],
                           v8[:, 4:8, 0:1].broadcast_to([128, 4, 64]), ALU.subtract))
                    dve.op(lambda e, ex=ex, SIM=SIM, v8=v8: e.tensor_tensor(ex, SIM[:, 0:4, 0:8],
                           v8[:, 0:4, 0:1].broadcast_to([128, 4, 8]), ALU.subtract))
                    dve.op(lambda e, e8=e8, c8=c8: e.tensor_tensor(e8, c8, c8[:, :, 0:1].broadcast_to([128, 4, 8]),
                                                                  ALU.subtract))
                    t = dve.op(lambda e, eC=eC, C=C, c8=c8: e.tensor_tensor(
                        eC, C, c8[:, :, 0:1].broadcast_to([128, 4, 64]), ALU.subtract))
                    te = act.op(lambda e, E=E: e.activation(E, E, ACT.Exp), t)
                    loc[tile] = (SP, ixf, C, C2, M, E, PRJ, ey, ex, e8, eC, ti, te)

                def ranks(tile):
                    T = tb_[2 * (b % 2) + tile]
                    SP, ixf, C, C2, M, E, PRJ, ey, ex, e8, eC, ti, te = loc[tile]
                    M_, n_, oh, thr, big, Z, rz = (T[n] for n in ("M", "n", "oh", "thr", "big", "Z", "rz"))
                    eq, R, iyb = T["eq"], T["R"], T["iyb"]
                    t = dve.op(lambda e, iyb=iyb, ixf=ixf: e.tensor_copy(iyb, ixf[:, 4:8, :]), ti)
                    for hh in range(4):
                        t_eq = dve.op(lambda e, hh=hh, eq=eq, iyb=iyb: e.tensor_tensor(
                            eq[:, 64 * hh:64 * hh + 64, :], iob, bc(iyb[:, hh, :], 1, 64), ALU.is_equal), t, t_io)
                    t_w8 = pool.op(lambda e, eq=eq: e.tensor_tensor(eq, eq, bc(w8b, 1, 256), ALU.mult), t_eq)
                    G = T["G"]
                    ig2, G2, fg2 = G2s.take()
                    t = dve.op(lambda e, M_=M_, C=C, C2=C2: e.tensor_tensor(M_, C, C2, ALU.not_equal))
                    t = dve.op(lambda e, M_=M_, n_=n_: e.tensor_reduce(
                        n_, M_.rearrange("p h (i j) -> p h i j", i=8), AX.X, ALU.add), t)
                    oh4 = oh.rearrange("p h (x i) -> p h x i", x=8)
                    t = dve.op(lambda e, oh4=oh4, ixf=ixf: e.tensor_tensor(
                        oh4, bc(x8, 1, 4), bc(ixf[:, 0:4, :], 2, 8), ALU.is_equal), tw["kx8"])
                    t = dve.op(lambda e, oh4=oh4, n_=n_: e.tensor_tensor(oh4, oh4, bc(n_, 2, 8), ALU.mult), t)
                    t = dve.op(lambda e, thr=thr, oh4=oh4: e.tensor_reduce(thr, oh4, AX.X, ALU.add), t)
                    t_thr = dve.op(lambda e, thr=thr: e.tensor_scalar(thr, thr, -1.0, 8.0, ALU.mult, ALU.add), t)
                    t = dve.op(lambda e, Z=Z, e8=e8: e.tensor_reduce(Z, e8, AX.X, ALU.add), te)
                    t = dve.op(lambda e, Z=Z, rz=rz: e.reciprocal(rz, Z), t)
                    t_ex = dve.op(lambda e, ex=ex, rz=rz: e.tensor_tensor(ex, ex, bc(rz, 2, 8), ALU.mult), t)
                    dve.op(lambda e, big=big, ixf=ixf: e.tensor_scalar(big, ixf[:, 0:4, :], 7.5, None, ALU.is_gt))
                    t = dve.op(lambda e, M_=M_, eC=eC: e.tensor_tensor(M_, M_, eC, ALU.mult))
                    t = dve.op(lambda e, big=big, rz=rz: e.tensor_tensor(big, big, bc(rz, 2, 8), ALU.mult), t)
                    t = dve.op(lambda e, big=big, SP=SP: e.tensor_scalar(big, big, SP[:, 1023:1024], None, ALU.mult), t)
                    t_c = dve.op(lambda e, M_=M_, big=big: e.tensor_tensor(
                        M_.rearrange("p h (i j) -> p h i j", i=8), M_.rearrange("p h (i j) -> p h i j", i=8),
                        bc(big, 3, 8), ALU.mult), t)
                    T["t_c"] = t_c
                    for hh in range(4):
                        t_g2 = pool.op(lambda e, hh=hh, G2=G2, PRJ=PRJ, ex=ex: e.tensor_tensor(
                            G2[:, hh, :, :], PRJ, bc(ex[:, hh, :], 2, 64), ALU.mult), t_ex, *fg2)
                    loc[tile] = (ey, thr, eq, R, G, G2, ig2, t_w8, t_g2)

                def gather(tile):
                    T = tb_[2 * (b % 2) + tile]
                    ey, thr, eq, R, G, G2, ig2, t_w8, t_g2 = loc[tile]
                    t = t_w8
                    t = dve.op(lambda e, eq=eq, R=R: e.tensor_reduce(R.rearrange("p h y -> p (h y)"), eq, AX.X, ALU.add), t)
                    for hh in range(4):
                        t = dve.op(lambda e, hh=hh, G=G, R=R, thr=thr: e.tensor_tensor(
                            G[:, hh, :, :], bc(R[:, hh, :], 1, 8), bc(thr[:, hh, :], 2, 64), ALU.is_gt), t)
                    for hh in range(4):
                        t = pool.op(lambda e, hh=hh, G=G, ey=ey: e.tensor_tensor(
                            G[:, hh, :, :], G[:, hh, :, :], bc(ey[:, hh, :], 1, 8), ALU.mult), t)
                    loc[tile] = (t, t_g2, G, G2, ig2)

                def product(tile):
                    T = tb_[2 * (b % 2) + tile]
                    t, t_g2, G, G2, ig2 = loc[tile]
                    T["t_g"] = (pool if tile == 1 else dve).op(lambda e, G=G, G2=G2: e.tensor_tensor(G, G, G2, ALU.mult), t, t_g2)
                    G2s.free(ig2, T["t_g"])

                loc = {}
                for f in (choose, ranks, gather, product):
                    for tile in range(2):
                        f(tile)
                        yield
                i, p, freed = PS.take()
                for c in range(4):
                    tk = pe.op(lambda e, c=c, p=p: e.matmul(p[:, 256 * c:256 * c + 256], Wup[:, 128 * c:128 * c + 128], hT,
                                                            start=True, stop=True, skip_group_check=True),
                               *freed, tw["bup"])
                t_up = act.op(lambda e, p=p: e.activation(U["up"], p.rearrange("p (c q) -> p c q", c=4), ACT.Silu), tk)
                PS.free(i, t_up)
                for tile in range(2):
                    T = tb_[2 * (b % 2) + tile]
                    act.op(lambda e, T=T: e.activation(T["M"], T["M"], ACT.Silu, accum_out=T["cs"]), T["t_c"])
                    T["t_a"] = act.op(lambda e, T=T: e.activation(T["G"], T["G"], ACT.Silu), T["t_g"])
                yield
                for tile in range(2):
                    T = tb_[2 * (b % 2) + tile]
                    g511 = T["G"].rearrange("p h x y -> p (h x y)")[:, 511:512]
                    T["t_s"] = dve.op(lambda e, T=T, g511=g511: e.tensor_tensor(g511, g511, T["cs"], ALU.add), T["t_a"])
                io_, po, ofreed = PO.take()
                for tile in range(2):
                    T = tb_[2 * (b % 2) + tile]
                    Gf = T["G"].rearrange("p h x y -> p h (x y)")
                    i, p, freed = PS.take()
                    for c in range(4):
                        for hh in range(4):
                            tk = pe.op(lambda e, c=c, hh=hh, p=p, Gf=Gf: e.matmul(
                                p[:, 128 * c:128 * c + 128], Gf[:, hh, 128 * c:128 * c + 128], ident,
                                start=(hh == 0), stop=(hh == 3), skip_group_check=True),
                                *((*freed, T["t_s"]) if c == hh == 0 else ()))
                    tdone[b, tile] = (tk,)
                    ta = act.op(lambda e, p=p: e.activation(U["AT"], p[:, 0:512].rearrange("p (c q) -> p c q", c=4),
                                                            ACT.Copy), tk, *((tprev,) if tile else ()))
                    PS.free(i, ta)
                    for c in range(8):
                        lhs = U["up"][:, c, 128 * tile:128 * tile + 128] if c < 4 else U["AT"][:, c - 4, :]
                        rhs = Wdn[:, c, :] if c < 4 else Wue[:, c - 4, :]
                        tprev = pe.op(lambda e, c=c, lhs=lhs, rhs=rhs, tile=tile: e.matmul(
                            po[:, 128 * tile:128 * tile + 128], lhs, rhs, start=(c == 0), stop=(c == 7),
                            skip_group_check=True), *((ta, t_up, tw["bdn"], tw["bue"], *ofreed) if c == 0 else ()))
                    yield
                t = dve.op(lambda e: e.tensor_copy(U["y"], po[:, 0:256].rearrange("p (t f) -> p t f", t=2)), tprev)
                PO.free(io_, t)
                t = yield from add_ln_residual(U["y"], b, U["st"], t)
                done[b] = (t,)

            EVERY_B = 6
            ORDER_B = [15, 14, 13, 12, 11, 6, 10, 9, 8, 0, 7, 5, 4, 3, 2, 1]
            drive_at([(EVERY_B * b, 0, unit(b)) for b in range(NB)], [ORDER_B])

        def phase_d():
            fence()
            split_psum(4)
            top[0] = base
            new_phase()
            w = {"qkv": sb([128, 3072]), "wo": sb([128, 8, 128]), "w1": sb([128, 682]), "w2": sb([128, 3, 128]),
                 "b1": sb([128, 6]), "ln": sb([128, 2]), "tab": sb([128, 2, 4, 64])}
            rope = sb([128, 2, 4, 64])
            scb = sb([128, 4, 64])
            t_rope = dma(rope, d["krope"])
            st2 = [stats() for _ in range(4)]
            NXS = 4
            XS = [sb([128, 32 + 256]) for _ in range(NXS)]
            T1 = Ring([sb([128, 2048]) for _ in range(3)])
            T2 = Ring([sb([128, 2048])])
            SQ = Ring([sb([128, 2048])])
            SS = Ring([sb([128, 64]) for _ in range(3)])
            QT = Ring([sb([128, 8, 128]) for _ in range(2)])
            NKT = 3
            KT = [sb([128, 8, 160]) for _ in range(NKT)]
            V = Ring([sb([96, 2, 1024]) for _ in range(2)])
            PP = Ring([sb([128, 16, 96]) for _ in range(3)])
            VN = [sb([128, 1024]) for _ in range(2)]
            vnfree, tv_n = [(), ()], [0]
            s_v = [ctx.enter_context(nc.semaphore(f"s_v{i}")) for i in range(2)]
            v_n = [0, 0]
            PTr = Ring([sb([96, 16, 128]) for _ in range(1)])
            OT = Ring([sb([128, 8, 128]) for _ in range(2)])
            sm = Ring([sb([128, 3, 16]) for _ in range(3)])
            for s in XS:
                pool.op(lambda e: e.memset(s[:, 0:33], 0.0))
            t_z = pool.last()

            xx_tok = {}

            def start(b):
                t = yield from layer_norm([XR[:, 2 * b, :], XR[:, 2 * b + 1, :]], [XX[:, 2 * b, :], XX[:, 2 * b + 1, :]],
                                          st2[b % 4], t_x[b // 4])
                xx_tok[2 * b] = xx_tok[2 * b + 1] = t

            ready = {}

            def loaded(n, l):
                assert ready[n][0] == l, (n, l)
                return ready[n][1]

            read = {}

            def load_v(l):
                ready["v"] = (l, dma(w["qkv"][:, 2048:3072], d["dWqkv"][l][:, 2048:3072], *read.get("v", ())))

            def load_wo(l):
                ready["wo"] = (l, dma(w["wo"], d["dWo"][l], *read.get("wo", ())))

            def load_qk(l):
                ready["qk"] = (l, dma(w["qkv"][:, 0:2048], d["dWqkv"][l][:, 0:2048], *read.get("qk", ())))
                ts = dma(scb, d["dsc"][l:l + 1].broadcast_to([128, 4, 64]), *read.get("scb", ()))
                for t in range(2):
                    tt = pool.op(lambda e: e.tensor_tensor(w["tab"][:, t, :, :], rope[:, t, :, :], scb, ALU.mult),
                                 t_rope, ts, *read.get("tab", ()))
                read["scb"] = (tt,)
                ready["tab"] = (l, tt)

            def load_ffn(l):
                r = read.get("ffn", ())
                for n, src in (("w1", "dW1"), ("w2", "dW2"), ("b1", "db1"), ("ln", "dln")):
                    ready[n] = (l, dma(w[n], d[src][l], *r))

            xsfree = [() for _ in range(NXS)]
            ktfree = [() for _ in range(NKT)]
            ktoks, kcopy, sread = {}, {}, {}
            xstok = {}

            def shifted(l, b, s, *tokens):
                i, p, tk = turn([XX[:, 2 * b, :], XX[:, 2 * b + 1, :]], xx_tok[2 * b], xx_tok[2 * b + 1])
                act.op(lambda e: e.activation(s[0:64, 32:288], p[0:64, 0:256], ACT.Copy), tk, *tokens)
                t = act.op(lambda e: e.activation(s[64:128, 33:288], p[64:128, 0:255], ACT.Copy))
                PS.free(i, t)
                return t

            def attn(l, k):
                b, tile = k // 2, k % 2
                if k == 0:
                    new_phase()
                if tile == 0:
                    assert xsfree[b % NXS] is not None
                    xstok[b] = shifted(l, b, XS[b % NXS], t_z, *xsfree[b % NXS])
                    xsfree[b % NXS] = None
                yield
                t_s = xstok[b]
                s = XS[b % NXS]
                xs = s[:, 32 + 128 * tile:160 + 128 * tile]
                i1, a1, f1 = T1.take()
                i2, a2, f2 = T2.take()
                iq, sq, fq = SQ.take()
                iss, ss, fss = SS.take()
                for half in range(2):
                    i, p, freed = PS.take()
                    for c in range(2):
                        col = 1024 * half + 512 * c
                        tk = pe.op(lambda e, p=p, c=c, col=col: e.matmul(p[:, 512 * c:512 * c + 512], xs,
                                   w["qkv"][:, col:col + 512], start=True, stop=True), *freed, t_s, loaded("qk", l))
                    tsq = act.op(lambda e, p=p, half=half: e.activation(sq[:, 1024 * half:1024 * half + 1024], p, ACT.Square),
                                 tk, *fq)
                    pv4 = p.rearrange("p (h u e) -> p h u e", h=16, u=2)
                    ph = p.rearrange("p (h e) -> p h e", h=16)
                    cs = w["tab"][:, tile, 2 * half, :]
                    sn = w["tab"][:, tile, 2 * half + 1, :]
                    o1 = a1[:, 1024 * half:1024 * half + 1024].rearrange("p (h e) -> p h e", h=16)
                    o2 = a2[:, 1024 * half:1024 * half + 1024].rearrange("p (h u e) -> p h u e", h=16, u=2)
                    dve.op(lambda e, ph=ph, cs=cs, o1=o1: e.tensor_tensor(o1, ph, bc(cs, 1, 16), ALU.mult),
                           tk, tsq, loaded("tab", l), *f1, *f2)
                    for u in range(2):
                        t2 = dve.op(lambda e, u=u, pv4=pv4, sn=sn, o2=o2: e.tensor_tensor(
                            o2[:, :, u, :], pv4[:, :, 1 - u, :], bc(sn[:, 32 * u:32 * u + 32], 1, 16), ALU.mult))
                    PS.free(i, t2)
                if k == 2 * NB - 1:
                    read["qk"], read["tab"] = (tk,), (t2,)
                    if l + 1 < run["depth"]:
                        load_qk(l + 1)
                t = dve.op(lambda e: e.tensor_reduce(ss[:, 0:32], sq.rearrange("p (h e) -> p h e", h=32), AX.X, ALU.add),
                           tsq, *fss)
                SQ.free(iq, t)
                t = pool.op(lambda e: e.tensor_scalar(ss[:, 32:64], ss[:, 0:32], 1e-24, None, ALU.max), t)
                t_r = pool.op(lambda e: e.tensor_tensor(ss[:, 0:32], ss[:, 32:64], mhalf32, ALU.pow), t)
                ta = pool.op(lambda e: e.tensor_tensor(a1, a1, a2, ALU.add), t2)
                T2.free(i2, ta)
                yield
                tn = dve.op(lambda e: e.tensor_tensor(a1.rearrange("p (h e) -> p h e", h=32),
                                                      a1.rearrange("p (h e) -> p h e", h=32), bc(ss[:, 0:32], 2, 64),
                                                      ALU.mult), ta, t_r)
                SS.free(iss, tn)
                yield
                iqt, qT, fqt = QT.take()
                kj = k % NKT
                kT = KT[kj]
                assert ktfree[kj] is not None
                for half in range(2):
                    i, p, freed = PS.take()
                    for c in range(8):
                        f = lambda e, p=p, c=c, half=half: e.transpose(
                            p[:, 128 * c:128 * c + 128], a1[:, 1024 * half + 128 * c:1024 * half + 128 * c + 128], ident)
                        if c < 7:
                            pe.quiet(f, *((tn, *freed) if c == 0 else ()))
                        else:
                            tk = pe.op(f)
                    pv_ = p.rearrange("p (c q) -> p c q", c=8)
                    if half == 0:
                        tq = act.op(lambda e, pv_=pv_: e.activation(qT, pv_, ACT.Copy), tk, *fqt)
                        PS.free(i, tq)
                    else:
                        tkt = act.op(lambda e, pv_=pv_: e.activation(kT[:, :, 32:160], pv_, ACT.Copy), tk, *ktfree[kj])
                        PS.free(i, tkt)
                T1.free(i1, tk)
                if tile == 0:
                    tp = pool.op(lambda e: e.memset(kT[:, :, 0:32], 0.0), *ktfree[kj])
                else:
                    tp = pool.op(lambda e: e.tensor_copy(kT[:, :, 0:32], KT[(k - 1) % NKT][:, :, 128:160]), ktoks[k - 1], *ktfree[kj])
                    if k - 1 in sread:
                        ktfree[(k - 1) % NKT] = (*sread.pop(k - 1), tp)
                    else:
                        kcopy[k - 1] = tp
                ktfree[kj] = None
                ktoks[k] = tkt
                yield
                ip_, P, fp = PP.take()
                ism, m3, fm = sm.take()
                mx, sums, rc = m3[:, 0, :], m3[:, 1, :], m3[:, 2, :]
                for g in range(2):
                    i, p, freed = PS.take()
                    for bank in range(2):
                        pe.quiet(lambda e, p=p, bank=bank: e.matmul(
                            p[:, 512 * bank:512 * bank + 384], identb, maskd[:, 1 if tile else 0, :], start=True, stop=False,
                            skip_group_check=True), *((*freed, tq, tkt, tp, t_mask) if bank == 0 else ()))
                        for j in range(4):
                            h = 8 * g + 2 * j + bank
                            r = slice(64 * (h % 2), 64 * (h % 2) + 64)
                            for blk in range(2):
                                o = p[64 * blk:64 * blk + 64, 512 * bank + 96 * j:512 * bank + 96 * j + 96]
                                f = lambda e, o=o, r=r, h=h, blk=blk: e.matmul(
                                    o, qT[r, h // 2, 64 * blk:64 * blk + 64], kT[r, h // 2, 64 * blk:64 * blk + 96],
                                    start=False, stop=False, skip_group_check=True)
                                if bank == 1 and j == 3 and blk == 1:
                                    tk = pe.op(f)
                                else:
                                    pe.quiet(f)
                    pv_ = p.rearrange("p (a c) -> p a c", a=2)[:, :, 0:384].rearrange("p a (h k) -> p a h k", h=4)
                    Pg = P[:, 8 * g:8 * g + 8, :].rearrange("p (a h) k -> p a h k", a=2)
                    mg = mx[:, 8 * g:8 * g + 8].rearrange("p (a h) -> p a h", a=2)
                    t = dve.op(lambda e, pv_=pv_, mg=mg: e.tensor_reduce(mg, pv_, AX.X, ALU.max), tk, *fm)
                    for a in range(2):
                        t_ = dve.op(lambda e, pv_=pv_, mg=mg, Pg=Pg, a=a: e.tensor_tensor(
                            Pg[:, a, :, :], pv_[:, a, :, :], bc(mg[:, a, :], 2, 96), ALU.subtract), t, *fp)
                    t = t_
                    PS.free(i, t)
                    te = act.op(lambda e, g=g: e.activation(P[:, 8 * g:8 * g + 8, :], P[:, 8 * g:8 * g + 8, :], ACT.Exp), t)
                QT.free(iqt, tk)
                if tile == 1:
                    ktfree[kj] = (tk,)
                elif k in kcopy:
                    ktfree[kj] = (tk, kcopy.pop(k))
                else:
                    sread[k] = (tk,)
                yield
                t = dve.op(lambda e: e.tensor_reduce(sums, P, AX.X, ALU.add), te)
                t = dve.op(lambda e: e.reciprocal(rc, sums), t)
                t = pool.op(lambda e: e.tensor_tensor(P, P, bc(rc, 2, 96), ALU.mult), t)
                sm.free(ism, t)
                yield
                ipt, PT, fpt = PTr.take()
                for g in range(2):
                    i, p, freed = PS.take()
                    for j in range(8):
                        f = lambda e, p=p, j=j, g=g: e.transpose(p[0:96, 128 * j:128 * j + 128], P[:, 8 * g + j, :], ident)
                        if j < 7:
                            pe.quiet(f, *((t, *freed) if j == 0 else ()))
                        else:
                            tk = pe.op(f)
                    tpt = act.op(lambda e, p=p, g=g: e.activation(
                        PT[:, 8 * g:8 * g + 8, :], p[0:96, :].rearrange("p (h q) -> p h q", h=8), ACT.Copy), tk, *fpt)
                    PS.free(i, tpt)
                PP.free(ip_, tk)
                nv = tv_n[0]
                tv_n[0] += 1
                vn = VN[nv % 2]
                i, p, freed = PS.take()
                for c in range(2):
                    tk = pe.op(lambda e, p=p, c=c: e.matmul(
                        p[:, 512 * c:512 * c + 512], xs, w["qkv"][:, 2048 + 512 * c:2560 + 512 * c],
                        start=True, stop=True), *freed, t_s, loaded("v", l))
                tvn = act.op(lambda e, p=p: e.activation(vn, p, ACT.Copy), tk, *vnfree[nv % 2])
                PS.free(i, tvn)
                iv, v, fv = V.take()
                before = VN[(nv + 1) % 2] if tile else vn
                copies = ((v[0:32, 0, :], before[96:128, :]), (v[32:96, 0, :], vn[0:64, :]), (v[:, 1, :], vn[32:128, :]))
                for n, (dst, src) in enumerate(copies):
                    sp.wait(*((tvn, *fv) if n == 0 else ()))
                    sp.e.dma_start(dst, src).then_inc(s_v[iv], 16)
                    v_n[iv] += 16
                tv = (s_v[iv], v_n[iv])
                vnfree[nv % 2] = vnfree[(nv + 1) % 2] = (tv,)
                if tile == 1:
                    xsfree[b % NXS] = (tk,)
                if k == 2 * NB - 1:
                    read["v"] = (tk,)
                    if l + 1 < run["depth"]:
                        load_v(l + 1)
                yield
                io_, o, fo = OT.take()
                i, p, freed = PS.take()
                for h in range(16):
                    for blk in range(2):
                        f = lambda e, p=p, h=h, blk=blk: e.matmul(
                            p[64 * (h % 2):64 * (h % 2) + 64, 128 * (h // 2) + 64 * blk:128 * (h // 2) + 64 * blk + 64],
                            v[:, blk, 64 * h:64 * h + 64], PT[:, 8 * (h // 8) + 4 * (h % 2) + (h % 8) // 2, 64 * blk:64 * blk + 64], start=True, stop=True,
                            skip_group_check=True)
                        if h == 15 and blk == 1:
                            tk = pe.op(f)
                        else:
                            pe.quiet(f, *((tpt, tv, *freed) if h == blk == 0 else ()))
                V.free(iv, tk)
                PTr.free(ipt, tk)
                t = act.op(lambda e, p=p: e.activation(o, p.rearrange("p (c q) -> p c q", c=8), ACT.Copy), tk, *fo)
                PS.free(i, t)
                yield
                i, p, freed = PS.take()
                for c in range(8):
                    tk = pe.op(lambda e, p=p, c=c: e.matmul(p[:, 0:128], o[:, c, :], w["wo"][:, c, :], start=(c == 0),
                                                            stop=(c == 7)), *((t, loaded("wo", l), *freed) if c == 0 else ()))
                OT.free(io_, tk)
                t = dve.op(lambda e, p=p: e.tensor_tensor(XX[:, k, :], XX[:, k, :], p[:, 0:128], ALU.add), tk)
                PS.free(i, t)
                xx_tok[k] = t
                if k == 2 * NB - 1:
                    read["wo"] = (tk,)
                    if l + 1 < run["depth"]:
                        load_wo(l + 1)

            NF = 3
            FB = []
            for _ in range(NF):
                a, g = sb([128, 2, 128]), sb([128, 3, 256])
                FB.append({"st": stats(), "z": a, "zT": a.rearrange("p t f -> p (t f)"), "ge": g, "g": g})
            ffree = [(pool.op(lambda e: e.memset(F["g"][:, 0, 32:33], 0.0)),) for F in FB]

            def ffn(l, b):
                j = (l * NB + b) % NF
                F, fr = FB[j], ffree[j]
                assert fr is not None
                ffree[j] = None
                s = F["g"].rearrange("p c q -> p (c q)")[:, 0:288]
                t = shifted(l, b, s, *fr)
                yield
                i, p, tk = turn([s[:, 32:160], s[:, 160:288]], t)
                t_one = dve.op(lambda e: e.memset(F["g"][64:128, 2, :], 1.0), tk)
                z = F["z"]
                t = act.op(lambda e: e.activation(z, p[:, 0:256].rearrange("p (t f) -> p t f", t=2), ACT.Copy), tk, *fr)
                PS.free(i, t)
                yield
                t = yield from layer_norm([z[:, 0, :], z[:, 1, :]], [z[:, 0, :], z[:, 1, :]], F["st"], t, *fr)
                yield
                i, p, tk = turn([z[:, 0, :], z[:, 1, :]], t)
                t = act.op(lambda e, p=p: e.activation(F["zT"], p[:, 0:256], ACT.Identity, bias=w["ln"][:, 1:2],
                                                       scale=w["ln"][:, 0:1]), tk, loaded("ln", l), *fr)
                PS.free(i, t)
                yield
                ig, pg, freed = PS.take()
                for c, (c0, n) in enumerate(CH):
                    tg = pe.op(lambda e, c=c, c0=c0, n=n: e.matmul(pg[0:n, 256 * c:256 * c + 256],
                               w["w1"][:, DI + c0:DI + c0 + n], F["zT"], start=True, stop=True, skip_group_check=True),
                               *((t, loaded("w1", l), *freed) if c == 0 else ()))
                ia, pa, freed = PS.take()
                for c, (c0, n) in enumerate(CH):
                    ta = pe.op(lambda e, c=c, c0=c0, n=n: e.matmul(pa[0:n, 256 * c:256 * c + 256],
                               w["w1"][:, c0:c0 + n], F["zT"], start=True, stop=True, skip_group_check=True),
                               *(freed if c == 0 else ()))
                for c, (c0, n) in enumerate(CH):
                    t = act.op(lambda e, c=c, n=n: e.activation(F["ge"][0:n, c, :], pg[0:n, 256 * c:256 * c + 256], ACT.Gelu,
                                                                bias=w["b1"][0:n, 3 + c:4 + c]), tg, loaded("b1", l), t_one)
                PS.free(ig, t)
                for c, (c0, n) in enumerate(CH):
                    td = dve.op(lambda e, c=c, n=n: e.scalar_tensor_tensor(
                        F["g"][0:n, c, :], pa[0:n, 256 * c:256 * c + 256], w["b1"][0:n, c:c + 1], F["ge"][0:n, c, :],
                        ALU.add, ALU.mult), t, ta)
                PS.free(ia, td)
                yield
                i, p, freed = PS.take()
                for tile in range(2):
                    for c in range(3):
                        n = 128 if c < 2 else 86
                        tk = pe.op(lambda e, p=p, c=c, n=n, tile=tile: e.matmul(
                            p[:, 128 * tile:128 * tile + 128], F["g"][0:n, c, 128 * tile:128 * tile + 128],
                            w["w2"][0:n, c, :], start=(c == 0), stop=(c == 2), skip_group_check=True),
                            *((td, loaded("w2", l), *freed) if tile == c == 0 else ()))
                t = dve.op(lambda e, p=p: e.tensor_tensor(XX[:, 2 * b:2 * b + 2, :], XX[:, 2 * b:2 * b + 2, :],
                                                          p[:, 0:256].rearrange("p (t f) -> p t f", t=2), ALU.add), tk)
                PS.free(i, t)
                xx_tok[2 * b] = xx_tok[2 * b + 1] = t
                ffree[j] = (pool.op(lambda e: e.memset(F["g"][:, 0, 32:33], 0.0), tk),)
                if b == NB - 1:
                    read["ffn"] = (tk, t, act.last())
                    if l + 1 < run["depth"]:
                        load_ffn(l + 1)

            def end(b):
                t = yield from layer_norm([XX[:, 2 * b, :], XX[:, 2 * b + 1, :]], [XX[:, 2 * b, :], XX[:, 2 * b + 1, :]],
                                          st2[b % 4], xx_tok[2 * b], xx_tok[2 * b + 1])
                dve.op(lambda e: e.tensor_tensor(XR[:, 2 * b:2 * b + 2, :], XR[:, 2 * b:2 * b + 2, :],
                                                 XX[:, 2 * b:2 * b + 2, :], ALU.add), t)

            load_qk(0)
            load_v(0)
            load_wo(0)
            load_ffn(0)
            PERIOD, LAG, HEAD, TAIL = 33, 12, 3, 9
            ORDER = {"edge": [14, 15],
                     "attn": [0, 12, 16, 10, 4, 7, 13, 5, 3],
                     "ffn": [17, 11, 6, 9, 8, 2, 1]}
            last = run["depth"] - 1
            drive_at([(2 * b, "edge", start(b)) for b in range(NB)] +
                     [(HEAD + PERIOD * l + k, "attn", attn(l, k)) for l in range(run["depth"]) for k in range(2 * NB)] +
                     [(HEAD + PERIOD * l + 2 * b + 1 + LAG, "ffn", ffn(l, b)) for l in range(run["depth"]) for b in range(NB)] +
                     [(HEAD + PERIOD * last + 2 * b + 1 + LAG + TAIL, "edge", end(b)) for b in range(NB)], ORDER)
        for ph, f in (("A", phase_a), ("B", phase_b), ("C", phase_c), ("D", phase_d)):
            if ph in run["phases"]:
                f()

        fence()
        s_out = ctx.enter_context(nc.semaphore("s_out"))
        n_out = 0
        for b0 in range(0, NB, 4):
            sp.e.dma_start(out[b0:b0 + 4].rearrange("b (t p) f -> p (b t) f", p=128),
                           XR[:, 2 * b0:2 * b0 + 8, :]).then_inc(s_out, 16)
            n_out += 16
        sp.wait((s_out, n_out), *t_x)


def constants():
    f = np.float32
    c = {"kident": np.eye(128, dtype=f)}
    q, k = np.arange(128)[:, None], np.arange(128)[None, :]
    m = np.where(k > q, f(-1e30), f(0)).astype(f)
    c["kmask"] = np.ascontiguousarray(np.stack([m, m.T], 1))
    r = (np.arange(128) % 64)[:, None]
    j = np.arange(96)[None, :]
    ok = (j >= r) & (j <= r + 32)
    first = ok & ((np.arange(128)[:, None] >= 64) | (j >= 32))
    md = np.stack([np.where(x, f(0), f(-1e30)).astype(f) for x in (first, ok)], 1)
    c["kmaskd"] = np.ascontiguousarray(np.tile(md, (1, 1, 4)))
    sel = np.zeros((128, 16, 128), np.uint16)
    for i in range(48):
        sel[i, i % 16, :] = sel[64 + i, i % 16, :] = 0xBF80
    c["ksel"] = sel.reshape(128, 2048).view(f)
    half = np.arange(0, 64, 2, dtype=f)
    inv = (f(1.0) / np.power(f(10000.0), half / f(64))).astype(f)
    t = np.arange(256, dtype=f)
    fr = (t[:, None] * inv[None, :]).astype(f)
    fr = np.concatenate([fr, fr], -1)
    bs = (half + f(25.6)) / f(89.6)
    power = (t - 128) / 16
    sc = np.power(bs[None, :].astype(np.float64), power[:, None].astype(np.float64))
    sc = np.concatenate([sc, sc], -1)
    sign = np.where(np.arange(64) < 32, -1.0, 1.0)
    cs, sn = np.cos(fr.astype(np.float64)), np.sin(fr.astype(np.float64)) * sign
    tab = np.stack([8 * cs * sc, 8 * sn * sc, cs / sc, sn / sc], 1).astype(f)
    c["krope"] = np.ascontiguousarray(tab.reshape(2, 128, 4, 64).transpose(1, 0, 2, 3))
    c["kiota"] = np.ascontiguousarray(np.broadcast_to(np.arange(64, dtype=f)[None, :, None], (128, 64, 8)))
    c["kx8"] = np.ascontiguousarray(np.broadcast_to(np.arange(8, dtype=f)[None, :, None], (128, 8, 8)))
    c["kw8"] = np.ascontiguousarray(np.broadcast_to((8 - np.arange(8)).astype(f)[None, :], (128, 8)))
    return c


def layout(i):
    g = lambda n: np.asarray(i[n])
    C = np.ascontiguousarray
    a = {"x": g("L0_attn_hidden_states")}
    a["aUT"] = C(np.concatenate([g(f"L0_attn_{n}_U").transpose(2, 1, 0) for n in "qkv"], 1))
    a["aV"] = C(np.concatenate([g(f"L0_attn_{n}_V").transpose(1, 0, 2) for n in "qkv"], 1))
    a["ab"] = C(np.concatenate([g(f"L0_attn_{n}_b").reshape(1, 128) for n in "qkv"], 1))
    a["aoUT"] = C(g("L0_attn_out_U").T)
    a["aoV"] = g("L0_attn_out_V")
    a["aob"] = g("L0_attn_out_b").reshape(1, 128)
    a["af1UT"] = C(g("L0_attn_fc1_U").T)
    a["af1V"] = g("L0_attn_fc1_V")
    a["af1b"] = C(g("L0_attn_fc1_b").reshape(4, 128).T)
    a["af2UT"] = C(g("L0_attn_fc2_U").T)
    a["af2V"] = g("L0_attn_fc2_V")
    a["af2b"] = g("L0_attn_fc2_b").reshape(1, 128)
    a["aln"] = C(np.stack([g(f"L0_attn_{n}") for n in ("ln1_g", "ln1_b", "ln2_g", "ln2_b")], 1))
    a["bWq"] = C(g("L0_ffn_W_q").reshape(8, 64, 128).transpose(1, 0, 2))
    a["bkT"] = C(g("L0_ffn_keys").transpose(3, 2, 0, 1).reshape(64, 8, 64))
    a["bdT"] = C(g("L0_ffn_down_embed").T)
    a["bue"] = C(g("L0_ffn_up_embed").reshape(4, 128, 128).transpose(1, 0, 2))
    a["bup"] = C(g("L0_ffn_W_up").T)
    a["bdn"] = C(g("L0_ffn_W_down").T.reshape(4, 128, 128).transpose(1, 0, 2))
    a["cW"] = C(np.concatenate([g(f"L1_attn_W{n}") for n in "qkv"], 1))
    a["cWo"] = g("L1_attn_Wo")
    a["cbo"] = g("L1_attn_bo").reshape(1, 128)
    a["dWqkv"] = g("L1_ffn_Wqkv")
    qs, ks = g("L1_ffn_q_scale"), g("L1_ffn_k_scale")
    rot = lambda s: np.concatenate([s[:, 32:], s[:, :32]], 1)
    a["dsc"] = C(np.stack([qs, rot(qs), ks, rot(ks)], 1))
    a["dWo"] = C(g("L1_ffn_Wo").reshape(DEPTH, 8, 128, 128).transpose(0, 2, 1, 3))
    a["dln"] = C(np.stack([g("L1_ffn_ln_g"), g("L1_ffn_ln_b")], 2))
    a["dW1"] = g("L1_ffn_W1")
    b1, w2, b2 = g("L1_ffn_b1"), g("L1_ffn_W2"), g("L1_ffn_b2")
    pb = np.zeros((DEPTH, 128, 6), np.float32)
    pw = np.zeros((DEPTH, 128, 3, 128), np.float32)
    for c, (c0, n) in enumerate(CH):
        pb[:, 0:n, c] = b1[:, c0:c0 + n]
        pb[:, 0:n, 3 + c] = b1[:, DI + c0:DI + c0 + n]
        pw[:, 0:n, c, :] = w2[:, c0:c0 + n, :]
    pw[:, 85, 2, :] = b2
    a["db1"], a["dW2"] = pb, pw
    a.update(constants())
    return a


RUN = {"phases": "ABCD", "depth": DEPTH}


def kernel(**inputs):
    import concourse.bacc as _bacc
    from concourse.bass_utils import run_bass_kernel_spmd as _run

    nc = _bacc.Bacc("TRN2", target_bir_lowering=False, num_devices=1)
    arrays, d = {}, {}
    given = layout(inputs)
    for name, (shape, dt) in SPEC.items():
        a = np.ascontiguousarray(given[name])
        assert a.shape == shape, (name, a.shape)
        arrays[f"in_{name}"] = a
        d[name] = nc.dram_tensor(f"in_{name}", shape, dt, kind="ExternalInput").ap()
    out = nc.dram_tensor("out_0", (NB, 256, 128), F32, kind="ExternalOutput").ap()
    network(nc, d, out, RUN)
    r = _run(nc, [arrays], core_ids=[0])
    return r.results[0]["out_0"]
```
